# Optimizing a Trainium2 kernel written in Bass

```python
import numpy as np
import jax
import jax.numpy as jnp

def _softmax(x, axis=-1):
    return jax.nn.softmax(x, axis=axis)

def _gelu(x):
    return jax.nn.gelu(x, approximate=True)

def _silu(x):
    return jax.nn.silu(x)

def _sigmoid(x):
    return jax.nn.sigmoid(x)

def _layernorm(x, axis=-1, eps=1e-05):
    m = jnp.mean(x, axis=axis, keepdims=True)
    v = jnp.var(x, axis=axis, keepdims=True)
    return (x - m) / jnp.sqrt(v + eps)

def _scatter_add(tgt, idx, src, axis=0):
    return tgt.at[idx].add(src)

def _segment_sum(src, seg, n):
    return jax.ops.segment_sum(src, seg, n)
kernel_name = 'mk_decoder_postln_d1_seqx_r4_121104'

def setup_inputs(seed: int=0):
    np.random.seed(seed)
    _w = jnp.asarray

    def _rec_inputs():
        import jax
        import jax.numpy as jnp
        _rk = jax.random.key(seed)
        x = -0.0003929 + 0.9999 * jax.random.normal(jax.random.fold_in(_rk, 1), (32, 112, 256), jnp.float32)
        _lenS = 112 - jax.random.randint(jax.random.fold_in(_rk, 7), (32,), 0, max(1, 112 // 4) + 1, jnp.int32)
        _lenS2 = 375 - jax.random.randint(jax.random.fold_in(_rk, 8), (32,), 0, max(1, 375 // 4) + 1, jnp.int32)
        _ctx_512P = jax.random.normal(jax.random.fold_in(_rk, 11), (32, 16, 128), jnp.float32)
        _ctx_512c = jax.random.dirichlet(jax.random.fold_in(_rk, 511), 0.3 * jnp.ones((16,), jnp.float32), (32, 375))
        _ctx_512t = jnp.einsum('bsk,bkd->bsd', _ctx_512c, _ctx_512P)
        _ctx_512t = _ctx_512t * jax.lax.rsqrt(jnp.mean(jnp.square(_ctx_512t)) + 1e-12) * 0.953939
        ctx_512 = -1.39393e-06 + 0.999914 * (_ctx_512t + 0.3 * jax.random.normal(jax.random.fold_in(_rk, 611), (32, 375, 128), jnp.float32))
        return (x, ctx_512)
    x, ctx_512 = _rec_inputs()

    def _L0_attn_setup():
        import jax, jax.numpy as jnp
        import numpy as np
        B, N, E, D = (2, 1024, 256, 128)
        H = E // D
        LN_EPS = 1e-05

        def _gla_scan(q, k, v, g):

            def step(S, inp):
                qt, kt, vt, gt = inp
                S = jnp.exp(gt)[..., None] * S + kt[..., None] * vt[..., None, :]
                ot = jnp.einsum('bhd,bhde->bhe', qt, S)
                return (S, ot)
            xs = tuple((jnp.moveaxis(a, 2, 0) for a in (q, k, v, g)))
            S0 = jnp.zeros(q.shape[:2] + (q.shape[-1], v.shape[-1]), q.dtype)
            _, o = jax.lax.scan(step, S0, xs)
            return jnp.moveaxis(o, 0, 2)
        key = jax.random.key(seed)
        ks = jax.random.split(key, 6)
        s = 0.02
        return {'x': jax.random.normal(ks[0], (B, N, E), jnp.float32), 'W_in': jax.random.normal(ks[1], (3 * E, E), jnp.float32) * s, 'W_out': jax.random.normal(ks[2], (E, E), jnp.float32) * s, 'W_g1': jax.random.normal(ks[3], (D, E), jnp.float32) * s, 'W_g2': jax.random.normal(ks[4], (E, D), jnp.float32) * s, 'ln_w': jnp.ones((E,), jnp.float32)}
    _L0_attn_all = _L0_attn_setup()
    _L0_attn_in = {k: v for k, v in _L0_attn_all.items() if k in ('W_in', 'W_out', 'W_g1', 'W_g2', 'ln_w')}
    del _L0_attn_all

    def _L0_xattn_setup():
        import jax, jax.numpy as jnp
        import numpy as np
        HEADS = 16
        D_MODEL = 256
        IMG_MODEL = 128
        D_K = D_MODEL // HEADS
        key = jax.random.key(seed)
        ks = jax.random.split(key, 12)
        B, LQ, LKV = (8, 512, 256)
        s_dm = 1.0 / np.sqrt(D_MODEL)
        s_im = 1.0 / np.sqrt(IMG_MODEL)
        return {'q': jax.random.normal(ks[0], (B, LQ, D_MODEL), jnp.float32), 'k': jax.random.normal(ks[1], (B, LKV, IMG_MODEL), jnp.float32), 'v': jax.random.normal(ks[2], (B, LKV, IMG_MODEL), jnp.float32), 'Wq': jax.random.normal(ks[3], (D_MODEL, D_MODEL), jnp.float32) * s_dm, 'bq': jnp.zeros((D_MODEL,), jnp.float32), 'Wk': jax.random.normal(ks[4], (IMG_MODEL, D_MODEL), jnp.float32) * s_im, 'bk': jnp.zeros((D_MODEL,), jnp.float32), 'Wv': jax.random.normal(ks[5], (IMG_MODEL, D_MODEL), jnp.float32) * s_im, 'bv': jnp.zeros((D_MODEL,), jnp.float32), 'Wo': jax.random.normal(ks[6], (D_MODEL, D_MODEL), jnp.float32) * s_dm, 'bo': jnp.zeros((D_MODEL,), jnp.float32)}
    _L0_xattn_all = _L0_xattn_setup()
    _L0_xattn_in = {k: v for k, v in _L0_xattn_all.items() if k in ('Wq', 'bq', 'Wk', 'bk', 'Wv', 'bv', 'Wo', 'bo')}
    del _L0_xattn_all

    def _L0_ffn_setup():
        import jax, jax.numpy as jnp
        import numpy as np
        LORA_DIM = 16
        LORA_TOKEN_INDEX = 1
        B, S, D, H = (4, 512, 256, 1024)
        key = jax.random.key(seed)
        ks = jax.random.split(key, 6)
        x = jax.random.normal(ks[0], (B, S, D), dtype=jnp.float32)
        W1 = jax.random.normal(ks[1], (H, D), dtype=jnp.float32) * 0.02
        b1 = jnp.zeros((H,), dtype=jnp.float32)
        W2 = jax.random.normal(ks[2], (D, H), dtype=jnp.float32) * 0.02
        b2 = jnp.zeros((D,), dtype=jnp.float32)
        scale = jnp.asarray(0.001, dtype=jnp.float32)
        return {'x': x, 'W1': W1, 'b1': b1, 'W2': W2, 'b2': b2, 'scale': scale}
    _L0_ffn_all = _L0_ffn_setup()
    _L0_ffn_in = {k: v for k, v in _L0_ffn_all.items() if k in ('W1', 'b1', 'W2', 'b2', 'scale')}
    del _L0_ffn_all
    return {'x': x, 'ctx_512': ctx_512, 'L0_attn_W_in': _L0_attn_in['W_in'], 'L0_attn_W_out': _L0_attn_in['W_out'], 'L0_attn_W_g1': _L0_attn_in['W_g1'], 'L0_attn_W_g2': _L0_attn_in['W_g2'], 'L0_attn_ln_w': _L0_attn_in['ln_w'], 'L0_xattn_Wq': _L0_xattn_in['Wq'], 'L0_xattn_bq': _L0_xattn_in['bq'], 'L0_xattn_Wk': _L0_xattn_in['Wk'], 'L0_xattn_bk': _L0_xattn_in['bk'], 'L0_xattn_Wv': _L0_xattn_in['Wv'], 'L0_xattn_bv': _L0_xattn_in['bv'], 'L0_xattn_Wo': _L0_xattn_in['Wo'], 'L0_xattn_bo': _L0_xattn_in['bo'], 'L0_ffn_W1': _L0_ffn_in['W1'], 'L0_ffn_b1': _L0_ffn_in['b1'], 'L0_ffn_W2': _L0_ffn_in['W2'], 'L0_ffn_b2': _L0_ffn_in['b2'], 'L0_ffn_scale': _L0_ffn_in['scale']}

def reference(x, ctx_512, L0_attn_W_in, L0_attn_W_out, L0_attn_W_g1, L0_attn_W_g2, L0_attn_ln_w, L0_xattn_Wq, L0_xattn_bq, L0_xattn_Wk, L0_xattn_bk, L0_xattn_Wv, L0_xattn_bv, L0_xattn_Wo, L0_xattn_bo, L0_ffn_W1, L0_ffn_b1, L0_ffn_W2, L0_ffn_b2, L0_ffn_scale):
    import jax
    import jax.numpy as jnp

    def _L0_attn_ref(x, W_in, W_out, W_g1, W_g2, ln_w):
        import jax, jax.numpy as jnp
        import numpy as np
        B, N, E, D = (2, 1024, 256, 128)
        H = E // D
        LN_EPS = 1e-05

        def _gla_scan(q, k, v, g):

            def step(S, inp):
                qt, kt, vt, gt = inp
                S = jnp.exp(gt)[..., None] * S + kt[..., None] * vt[..., None, :]
                ot = jnp.einsum('bhd,bhde->bhe', qt, S)
                return (S, ot)
            xs = tuple((jnp.moveaxis(a, 2, 0) for a in (q, k, v, g)))
            S0 = jnp.zeros(q.shape[:2] + (q.shape[-1], v.shape[-1]), q.dtype)
            _, o = jax.lax.scan(step, S0, xs)
            return jnp.moveaxis(o, 0, 2)
        b, n, e = x.shape
        u = x @ W_in.T
        v, q, lg = jnp.split(u, 3, axis=-1)
        q = jax.nn.silu(q)
        f = jax.nn.sigmoid(lg)
        k = 1.0 - f
        g = jax.nn.log_sigmoid(lg)

        def tohead(a):
            return a.reshape(b, n, H, D).transpose(0, 2, 1, 3)
        o = _gla_scan(tohead(q), tohead(k), tohead(v), tohead(g))
        o = o.transpose(0, 2, 1, 3).reshape(b, n, e)
        gate = jax.nn.sigmoid(x @ W_g1.T @ W_g2.T)
        o = o * gate
        mu = jnp.mean(o, axis=-1, keepdims=True)
        var = jnp.var(o, axis=-1, keepdims=True)
        o = (o - mu) * jax.lax.rsqrt(var + LN_EPS) * ln_w
        return o @ W_out.T

    def _L0_xattn_ref(q, k, v, Wq, bq, Wk, bk, Wv, bv, Wo, bo):
        import jax, jax.numpy as jnp
        import numpy as np
        HEADS = 16
        D_MODEL = 256
        IMG_MODEL = 128
        D_K = D_MODEL // HEADS
        B, LQ, _ = q.shape
        LKV = k.shape[1]
        qh = (q @ Wq + bq).reshape(B, LQ, HEADS, D_K).transpose(0, 2, 1, 3)
        kh = (k @ Wk + bk).reshape(B, LKV, HEADS, D_K).transpose(0, 2, 1, 3)
        vh = (v @ Wv + bv).reshape(B, LKV, HEADS, D_K).transpose(0, 2, 1, 3)
        scale = 1.0 / np.sqrt(D_K)
        scores = jnp.einsum('bhqd,bhkd->bhqk', qh, kh) * scale
        attn = jax.nn.softmax(scores, axis=-1)
        out = jnp.einsum('bhqk,bhkd->bhqd', attn, vh)
        concat = out.transpose(0, 2, 1, 3).reshape(B, LQ, D_MODEL)
        return concat @ Wo + bo

    def _L0_ffn_ref(x, W1, b1, W2, b2, scale):
        import jax, jax.numpy as jnp
        import numpy as np
        LORA_DIM = 16
        LORA_TOKEN_INDEX = 1
        B, S, D, H = (4, 512, 256, 1024)
        Bx, Sx, Dx = x.shape
        Hx = W1.shape[0]
        lt = jax.lax.dynamic_slice_in_dim(x, LORA_TOKEN_INDEX, LORA_DIM, axis=1)
        even = lt[:, ::2, :]
        odd = lt[:, 1::2, :]
        m1 = (even[:, :4, :, None] * odd[:, :4, None, :]).reshape(Bx, Hx, Dx)
        m2 = (even[:, 4:, :, None] * odd[:, 4:, None, :]).reshape(Bx, Dx, Hx)
        h = jnp.einsum('bsd,hd->bsh', x, W1) + scale * jnp.einsum('bsd,bhd->bsh', x, m1) + b1
        h = jax.nn.gelu(h, approximate=False)
        out = jnp.einsum('bsh,oh->bso', h, W2) + scale * jnp.einsum('bsh,boh->bso', h, m2) + b2
        return out
    x = _layernorm(x + _L0_attn_ref(x, L0_attn_W_in, L0_attn_W_out, L0_attn_W_g1, L0_attn_W_g2, L0_attn_ln_w), axis=-1)
    x = _layernorm(x + _L0_xattn_ref(x, ctx_512, ctx_512, L0_xattn_Wq, L0_xattn_bq, L0_xattn_Wk, L0_xattn_bk, L0_xattn_Wv, L0_xattn_bv, L0_xattn_Wo, L0_xattn_bo), axis=-1)
    x = _layernorm(x + _L0_ffn_ref(x, L0_ffn_W1, L0_ffn_b1, L0_ffn_W2, L0_ffn_b2, L0_ffn_scale), axis=-1)
    return x

_drawn_inputs = setup_inputs


def setup_inputs(seed=0):
    import zlib

    import numpy as np

    out = dict(_drawn_inputs(seed))
    spreads = {'L0_attn_ln_w': (1.0, 0.2),
     'L0_xattn_bq': (0.0, 0.393),
     'L0_xattn_bk': (0.0, 0.8),
     'L0_xattn_bv': (0.0, 0.1),
     'L0_xattn_bo': (0.0, 0.1),
     'L0_ffn_b1': (0.0, 0.1),
     'L0_ffn_b2': (0.0, 0.1)}
    factors = {'L0_attn_W_g1': 5.584, 'L0_attn_W_g2': 5.585}
    for name, (base, spread) in spreads.items():
        noise = np.random.default_rng([zlib.crc32(name.encode()), seed]).standard_normal(out[name].shape)
        drawn = base * np.exp(spread * noise) if base else spread * noise
        out[name] = jnp.asarray(drawn.astype(out[name].dtype))
    for name, factor in factors.items():
        out[name] = (out[name] * factor).astype(out[name].dtype)
    return out
```

```python
import numpy as np
import concourse.bass as bass
from concourse import mybir
from contextlib import ExitStack

F32 = mybir.dt.float32
BF16 = mybir.dt.bfloat16
I32 = mybir.dt.int32
ALU = mybir.AluOpType
ACT = mybir.ActivationFunctionType
AX = mybir.AxisListType

B, S, E = 32, 112, 256
D = 128
H = E // D
KE = E // 128
SC, C = 375, 128
NH, DK = 16, 16
HID = 1024
EPS = 1e-5
GELU = "gelu_and_others"
LOG_EXP = "natural_log_exp_and_others"

LEFT = [[(0, 1, 112, 64, 63)], [(0, 2, 64, 32, 31)], [(0, 3, 32, 16, 15)], [(0, 7, 16, 8, 7)]]
RIGHT = [[(64, 1, 112, 48, 63)], [(32, 2, 64, 16, 31), (48, 1, 112, 16, 31)], [(16, 3, 32, 16, 15)], [(8, 7, 16, 8, 7)]]
BASE = 8
BASE_CUT = 3
LEVELS = len(LEFT) + 1
LOG_MAX = 20.0
GATE_MAX = 40.0
SEG = 4
GT = 2 * S
GROUPS = B // 2


def tokens_of(run):
    first, blocks, stride, length, _ = run
    return [first + n * stride + i for n in range(blocks) for i in range(length)]


def constants():
    f = np.float32
    ident = np.eye(128, dtype=f)
    mask = np.zeros((S, LEVELS, S), np.int32)
    for n in range(LEVELS - 1):
        for l in LEFT[n]:
            for r in RIGHT[n]:
                for lb in range(l[1]):
                    for rb in range(r[1]):
                        if lb == rb:
                            s0, t0 = l[0] + lb * l[2], r[0] + rb * r[2]
                            mask[s0:s0 + l[3], n, t0:t0 + r[3]] = 1
    s, t = np.arange(S)[:, None], np.arange(S)[None, :]
    mask[:, LEVELS - 1, :] = (s // BASE == t // BASE) & (s <= t)
    assert (mask.sum(1) == (s <= t)).all()
    masks = np.repeat(mask[:, :, None, :], SEG, axis=2).reshape(S, LEVELS * SEG * S)
    keep = np.ones((128, SEG, S), f)
    keep[:, :, 0] = 0
    sel = np.zeros((128, 128), f)
    for i in range(4):
        sel[32 * i + DK, 32 * i:32 * i + 32] = 1
    vmask = np.ones((128, CHUNKS), f)
    vmask[0:CHUNK[1] + 128 - CHUNK[2], 2] = 0
    row = np.arange(128)
    batch_of = np.where(row % 32 < FB * LR, row % 32 // LR, -1)
    own_batch = (batch_of[:, None] == np.arange(FT)[None, :] // S).astype(f)
    own_rows = np.repeat((row[:, None] % LR == np.arange(LR)[None, :]).astype(f)[:, :, None], E // LR, axis=2)
    return {"c_own_batch": own_batch, "c_own_rows": own_rows, "c_sel": sel, "c_vmask": vmask, "c_ident": ident, "c_masks": np.ascontiguousarray(masks), "c_keep": keep.reshape(128, SEG * S)}


def after(eng, sem, value):
    if not isinstance(value, int) or value > 0:
        eng.wait_ge(sem, value)


def apart(eng, m):
    eng.sem_inc(m.passed, 1)


def there(g, n):
    return not isinstance(g, int) or 0 <= g < n


def steps(eng, first, lo, hi, last, step):
    for g in range(first, lo):
        step(g, g // 2, g % 2)
    with eng.Fori(0, (hi - lo) // 2) as i:
        for k in range(2):
            step(i * 2 + (lo + k), i + lo // 2, k)
    for g in range(hi, last):
        step(g, g // 2, g % 2)


def blocks(seg, run):
    first, n, stride, length, _ = run
    a = seg[:, :, first:first + length]
    return bass.AP(tensor=a.tensor, offset=a.offset, ap=[list(a.ap[0]), list(a.ap[1]), [stride, n], list(a.ap[2])])


def cuts(seg, run):
    _, n, stride, length, cut = run
    a = seg[:, :, cut:cut + 1]
    return bass.AP(tensor=a.tensor, offset=a.offset, ap=[list(a.ap[0]), list(a.ap[1]), [stride, n], [0, length]])


class Memory:
    pass


def gla_phase(nc, m, ctx, io):
    def sb(name, shape, dt=F32):
        return ctx.enter_context(nc.sbuf_tensor(name, shape, dt))

    def sem(name):
        return ctx.enter_context(nc.semaphore(name))

    W = SEG * S
    w_in = sb("w_in", [128, KE, 3 * E])
    w_out = sb("w_out", [128, KE, E])
    w_g1 = sb("w_g1", [128, KE, D])
    w_g2 = sb("w_g2", [128, E])
    ln_w = sb("ln_w", [128, KE])
    masks = sb("masks", [S, LEVELS, W], I32)
    keep = sb("keep", [128, W])
    xT = [sb(f"xT{k}", [128, KE, GT]) for k in range(2)]
    xr = [sb(f"xr{k}", [S, 2, E]) for k in range(2)]
    pre = sb("pre", [128, 2, W])
    ex = sb("ex", [128, 2, W])
    lp = sb("lp", [128, 2, W])
    sg = sb("sg", [128, 2, W])
    kk = sb("kk", [128, SEG, S])
    qq = sb("qq", [128, SEG, S])
    cum = sb("cum", [128, SEG, S])
    dist = sb("dist", [128, LEVELS, SEG, S])
    dec = sb("dec", [128, LEVELS + 1, SEG, S])
    kh = [sb(f"kh{k}", [128, LEVELS, SEG, S]) for k in range(2)]
    qh = [sb(f"qh{k}", [128, LEVELS, SEG, S]) for k in range(2)]
    aT = [sb(f"aT{k}", [S, W]) for k in range(2)]
    vv = [sb(f"vv{k}", [S, 2 * E]) for k in range(2)]
    g1 = sb("g1", [128, GT])
    gpre = sb("gpre", [S, 2 * E])
    gex = sb("gex", [S, 2 * E])
    gate = [sb(f"gate{k}", [S, 2 * E]) for k in range(2)]
    og = sb("og", [S, 2, E])
    on = sb("on", [S, 2, E])
    onT = sb("onT", [128, KE, GT])
    r1 = sb("r1", [S, 2, E])
    x1 = [sb(f"x1{k}", [S, 2, E]) for k in range(2)]
    st = sb("st", [S, 2, 2, 6])
    mv = sb("mv", [S, 2, 2, 2])
    lnv = sb("lnv", [S, 2, 2])
    rstd = sb("rstd", [S, 2, 2])

    names = ("w_here zeroed lnw_folded q_ps lg_ps v_ps g1_ps gate_ps a_ps o_ps onT_ps att_ps x1T_ps "
             "pre_lg pre_q e_done l_done f_done k_done q_done cum_done dist_done dec_done hats_done a_masked "
             "gpre_done gex_done glog_done gate_done v_sb g1_sb og_done st_done mv_done lnv_done rstd_done on_done "
             "onT_sb r1_done st2_done mv2_done lnv2_done rstd2_done x1_done x1T_sb x1_kept").split()
    s = {n: sem("g_" + n) for n in names}
    xT_in = [sem(f"g_xT_in{k}") for k in range(2)]
    xr_in = [sem(f"g_xr_in{k}") for k in range(2)]
    q_bank, lg_bank, v_bank, g1_bank, gate_bank, a0, a1, o_bank = m.bank
    a_bank = [a0, a1]
    N = GROUPS

    def seg(ap):
        return ap.rearrange("p (g s) -> p g s", g=SEG)

    with nc.Block() as block:
        @block.sync
        def _(sp):
            sp.dma_start(w_in[:, :, :], io["W_inT"].rearrange("(k p) n -> p k n", p=128)).then_inc(s["w_here"], 16)
            sp.dma_start(w_g1[:, :, :], io["W_g1T"].rearrange("(k p) n -> p k n", p=128)).then_inc(s["w_here"], 16)
            sp.dma_start(w_g2[:, :], io["W_g2T"]).then_inc(s["w_here"], 16)
            sp.dma_start(w_out[:, :, :], io["W_outT"].rearrange("(k p) n -> p k n", p=128)).then_inc(s["w_here"], 16)
            sp.dma_start(ln_w[:, :], io["ln_w"]).then_inc(s["w_here"], 16)
            sp.dma_start(masks[:, :, :], io["c_masks"].rearrange("p (l n) -> p l n", l=LEVELS)).then_inc(s["w_here"], 16)
            sp.dma_start(keep[:, :], io["c_keep"]).then_inc(s["w_here"], 16)

            def step(g, half, k):
                if there(g, N):
                    after(sp, s["v_ps"], g - 1)
                    apart(sp, m)
                    sp.dma_start(xT[k][:, :, :], io["xT"][:, :, bass.ds(g * GT, GT)].rearrange("k p n -> p k n")).then_inc(xT_in[k], 16)
                    after(sp, s["r1_done"], g - 1)
                    apart(sp, m)
                    sp.dma_start(xr[k][:, :, :], io["x"][bass.ds(g * 2, 2), :, :].rearrange("b s e -> s b e")).then_inc(xr_in[k], 16)
            steps(sp, 0, 2, N, N, step)

        WTS = 7 * 16

        @block.tensor
        def _(pe):
            pe.wait_ge(s["w_here"], WTS)

            def step(g, half, k):
                n, nk, nhalf = g + 1, 1 - k, (half + k) if not isinstance(g, int) else (g + 1) // 2
                if there(n, N):
                    pe.wait_ge(xT_in[nk], nhalf * 16 + 16)
                    after(pe, s["pre_lg"], n)
                    for h in range(H):
                        for e in range(KE):
                            mm = pe.matmul(lg_bank[:, h * GT:(h + 1) * GT], w_in[:, e, 2 * E + h * D:2 * E + (h + 1) * D],
                                           xT[nk][:, e, :], start=(e == 0), stop=(e == KE - 1))
                    mm.then_inc(s["lg_ps"], 1)
                    after(pe, s["q_done"], n)
                    for h in range(H):
                        for e in range(KE):
                            mm = pe.matmul(q_bank[:, h * GT:(h + 1) * GT], w_in[:, e, E + h * D:E + (h + 1) * D],
                                           xT[nk][:, e, :], start=(e == 0), stop=(e == KE - 1))
                    mm.then_inc(s["q_ps"], 1)
                if there(g - 2, N):
                    pe.wait_ge(s["x1_done"], g - 1)
                    after(pe, s["v_sb"], g + 1 if there(g, N) else N)
                    for e in range(KE):
                        for b in range(2):
                            mm = pe.transpose(v_bank[:, (e * 2 + b) * S:(e * 2 + b + 1) * S], x1[k][:, b, e * 128:(e + 1) * 128],
                                              m.ident[0:S, 0:S])
                    mm.then_inc(s["x1T_ps"], 1)
                if there(g, N):
                    pe.wait_ge(s["hats_done"], g + 1)
                    for l in range(LEVELS):
                        turn = g * LEVELS + l
                        after(pe, s["a_masked"], turn - 1)
                        for j in range(SEG):
                            mm = pe.matmul(a_bank[(k * LEVELS + l) % 2][0:S, j * S:(j + 1) * S], kh[k][:, l, j, :], qh[k][:, l, j, :],
                                           start=True, stop=True)
                        mm.then_inc(s["a_ps"], 1)
                if there(n, N):
                    after(pe, s["onT_sb"], n - 2)
                    for e in range(KE):
                        mm = pe.matmul(g1_bank[:, 0:GT], w_g1[:, e, :], xT[nk][:, e, :], start=(e == 0), stop=(e == KE - 1))
                    mm.then_inc(s["g1_ps"], 1)
                    after(pe, s["x1T_sb"], n - 2)
                    for b in range(2):
                        for e in range(KE):
                            mm = pe.matmul(v_bank[0:S, b * E:(b + 1) * E], xT[nk][:, e, b * S:(b + 1) * S], w_in[:, e, 0:E],
                                           start=(e == 0), stop=(e == KE - 1))
                    mm.then_inc(s["v_ps"], 1)
                    pe.wait_ge(s["g1_sb"], n + 1)
                    after(pe, s["r1_done"], n - 2)
                    for b in range(2):
                        mm = pe.matmul(gate_bank[0:S, b * E:(b + 1) * E], g1[:, b * S:(b + 1) * S], w_g2[:, :], start=True, stop=True)
                    mm.then_inc(s["gate_ps"], 1)
                if there(g - 1, N):
                    pe.wait_ge(s["on_done"], g)
                    for e in range(KE):
                        for b in range(2):
                            mm = pe.transpose(g1_bank[:, (e * 2 + b) * S:(e * 2 + b + 1) * S], on[:, b, e * 128:(e + 1) * 128],
                                              m.ident[0:S, 0:S])
                    mm.then_inc(s["onT_ps"], 1)
                if there(g, N):
                    pe.wait_ge(s["a_masked"], g * LEVELS + LEVELS)
                    pe.wait_ge(s["v_sb"], g + 1)
                    after(pe, s["og_done"], g)
                    for b in range(2):
                        for h in range(H):
                            j = h * 2 + b
                            c = b * E + h * D
                            mm = pe.matmul(o_bank[0:S, c:c + D], aT[k][:, j * S:(j + 1) * S], vv[k][:, c:c + D], start=True, stop=True)
                    mm.then_inc(s["o_ps"], 1)
                if there(g - 1, N):
                    pe.wait_ge(s["onT_sb"], g)
                    pe.wait_ge(s["gpre_done"], g + 2 if there(g + 1, N) else N)
                    for b in range(2):
                        for e in range(KE):
                            mm = pe.matmul(gate_bank[0:S, b * E:(b + 1) * E], onT[:, e, b * S:(b + 1) * S], w_out[:, e, :],
                                           start=(e == 0), stop=(e == KE - 1))
                    mm.then_inc(s["att_ps"], 1)
            pe.wait_ge(s["lnw_folded"], 1)
            steps(pe, -1, 2, N - 2, N + 2, step)

        @block.vector
        def _(dve):
            for k in range(2):
                dve.memset(kh[k][:, :, :, :], 0.0)
                dve.memset(qh[k][:, :, :, :], 0.0)
                dve.memset(aT[k][:, :], 0.0)
            dve.memset(dist[:, :, :, :], 0.0).then_inc(s["zeroed"], 1)
            dve.wait_ge(s["w_here"], WTS)
            for e in range(KE):
                mul = dve.tensor_scalar(w_out[:, e, :], w_out[:, e, :], ln_w[:, e:e + 1], None, ALU.mult)
            mul.then_inc(s["lnw_folded"], 1)
            dve.wait_ge(s["zeroed"], 1)

            def step(g, half, k):
                n, nk = g + 1, 1 - k
                if there(n, N):
                    dve.wait_ge(s["lg_ps"], n + 1)
                    after(dve, s["e_done"], n)
                    dve.tensor_scalar(pre[:, 0, :], lg_bank[:, 0:W], -LOG_MAX, None, ALU.max).then_inc(s["pre_lg"], 1)
                    dve.wait_ge(s["q_ps"], n + 1)
                    dve.tensor_scalar(pre[:, 1, :], q_bank[:, 0:W], -GATE_MAX, None, ALU.max).then_inc(s["pre_q"], 1)
                if there(g - 1, N):
                    dve.wait_ge(s["o_ps"], g)
                    dve.wait_ge(s["gate_done"], g)
                    dve.tensor_tensor(og[:, :, :].rearrange("p b e -> p (b e)"), o_bank[0:S, :], gate[nk][:, :], ALU.mult).then_inc(s["og_done"], 1)
                    dve.wait_ge(s["og_done"], g)
                    for b in range(2):
                        bn = dve.bn_stats(st[:, 0, b, :], og[:, b, :])
                    bn.then_inc(s["st_done"], 1)
                    dve.wait_ge(s["st_done"], g)
                    apart(dve, m)
                    for b in range(2):
                        bn = dve.bn_aggr(mv[:, 0, b, :], st[:, 0, b, :])
                    bn.then_inc(s["mv_done"], 1)
                if there(g, N):
                    for l in range(LEVELS):
                        if l == 2 and there(g - 1, N):
                            dve.wait_ge(s["rstd_done"], g)
                            after(dve, s["onT_ps"], g - 1)
                            for b in range(2):
                                ts = dve.tensor_scalar(on[:, b, :], og[:, b, :], mv[:, 0, b, 0:1], rstd[:, 0, b:b + 1], ALU.subtract, ALU.mult)
                            ts.then_inc(s["on_done"], 1)
                        dve.wait_ge(s["a_ps"], g * LEVELS + l + 1)
                        after(dve, s["a_masked"], g * LEVELS + l)
                        if l == 0:
                            after(dve, s["o_ps"], g - 1)
                        apart(dve, m)
                        dve.copy_predicated(aT[k][:, :], masks[:, l, :], a_bank[(k * LEVELS + l) % 2][0:S, 0:W]).then_inc(s["a_masked"], 1)
                elif there(g - 1, N):
                    dve.wait_ge(s["rstd_done"], g)
                    after(dve, s["onT_ps"], g - 1)
                    for b in range(2):
                        ts = dve.tensor_scalar(on[:, b, :], og[:, b, :], mv[:, 0, b, 0:1], rstd[:, 0, b:b + 1], ALU.subtract, ALU.mult)
                    ts.then_inc(s["on_done"], 1)
                if there(n, N):
                    dve.wait_ge(s["l_done"], n + 1)
                    after(dve, s["dist_done"], n)
                    dve.tensor_tensor_scan(cum[:, :, :].rearrange("p g s -> p (g s)"), keep[:, :], lp[:, 0, :], 0.0, ALU.mult, ALU.add).then_inc(s["cum_done"], 1)
                    dve.wait_ge(s["f_done"], n + 1)
                    after(dve, s["hats_done"], n)
                    dve.tensor_scalar(kk[:, :, :].rearrange("p g s -> p (g s)"), sg[:, 0, :], -1.0, 1.0, ALU.mult, ALU.add).then_inc(s["k_done"], 1)
                    dve.tensor_tensor(qq[:, :, :].rearrange("p g s -> p (g s)"), q_bank[:, 0:W], sg[:, 1, :], ALU.mult).then_inc(s["q_done"], 1)
                    dve.wait_ge(s["cum_done"], n + 1)
                    after(dve, s["dec_done"], n)
                    for l in range(LEVELS - 1):
                        for run in LEFT[l]:
                            dve.tensor_tensor(blocks(dist[:, l], run), cuts(cum, run), blocks(cum, run), ALU.subtract)
                        for run in RIGHT[l]:
                            dve.tensor_tensor(blocks(dist[:, l], run), blocks(cum, run), cuts(cum, run), ALU.subtract)
                    run = (0, S // BASE, BASE, BASE, BASE_CUT)
                    dve.tensor_tensor(blocks(dist[:, LEVELS - 1], run), blocks(cum, run), cuts(cum, run), ALU.subtract).then_inc(s["dist_done"], 1)
                    dve.wait_ge(s["gate_ps"], n + 1)
                    after(dve, s["gex_done"], n)
                    dve.tensor_scalar(gpre[:, :], gate_bank[0:S, :], -GATE_MAX, None, ALU.max).then_inc(s["gpre_done"], 1)
                if there(g - 1, N):
                    dve.wait_ge(s["att_ps"], g)
                    dve.wait_ge(xr_in[nk], nhalf_prev(g, half, k) * 16 + 16)
                    dve.tensor_tensor(r1[:, :, :].rearrange("p b e -> p (b e)"), gate_bank[0:S, :], xr[nk][:, :, :].rearrange("p b e -> p (b e)"), ALU.add).then_inc(s["r1_done"], 1)
                    dve.wait_ge(s["r1_done"], g)
                    for b in range(2):
                        bn = dve.bn_stats(st[:, 1, b, :], r1[:, b, :])
                    bn.then_inc(s["st2_done"], 1)
                    dve.wait_ge(s["st2_done"], g)
                    apart(dve, m)
                    for b in range(2):
                        bn = dve.bn_aggr(mv[:, 1, b, :], st[:, 1, b, :])
                    bn.then_inc(s["mv2_done"], 1)
                    dve.wait_ge(s["rstd2_done"], g)
                    after(dve, s["x1T_ps"], g - 2)
                    after(dve, s["x1_kept"], g - 2)
                    for b in range(2):
                        ts = dve.tensor_scalar(x1[nk][:, b, :], r1[:, b, :], mv[:, 1, b, 0:1], rstd[:, 1, b:b + 1], ALU.subtract, ALU.mult)
                    ts.then_inc(s["x1_done"], 1)

            def nhalf_prev(g, half, k):
                return (g - 1) // 2 if isinstance(g, int) else half + (k - 1)
            steps(dve, -1, 2, N - 2, N + 2, step)

        @block.scalar
        def _(act):
            act.preload_act_table_set(LOG_EXP)
            act.wait_ge(s["zeroed"], 1)

            def step(g, half, k):
                n, nk = g + 1, 1 - k
                if there(g - 1, N):
                    act.wait_ge(s["mv_done"], g)
                    act.activation(lnv[:, 0, :], mv[:, 0, :, 1], ACT.Ln, bias=m.eps[0:S, :]).then_inc(s["lnv_done"], 1)
                    act.wait_ge(s["lnv_done"], g)
                    after(act, s["on_done"], g - 1)
                    act.activation(rstd[:, 0, :], lnv[:, 0, :], ACT.Exp, scale=-0.5).then_inc(s["rstd_done"], 1)
                if there(n, N):
                    act.wait_ge(s["pre_lg"], n + 1)
                    act.wait_ge(s["pre_q"], n + 1)
                    act.activation(ex[:, :, :], pre[:, :, :], ACT.Exp, scale=-1.0).then_inc(s["e_done"], 1)
                    act.wait_ge(s["e_done"], n + 1)
                    after(act, s["cum_done"], n)
                    act.activation(lp[:, :, :], ex[:, :, :], ACT.Ln, bias=m.one[:, :]).then_inc(s["l_done"], 1)
                    act.wait_ge(s["l_done"], n + 1)
                    after(act, s["k_done"], n)
                    after(act, s["q_done"], n)
                    act.activation(sg[:, :, :], lp[:, :, :], ACT.Exp, scale=-1.0).then_inc(s["f_done"], 1)
                if there(g - 2, N):
                    act.wait_ge(s["x1T_ps"], g - 1)
                    act.activation(m.x1T[:, :, bass.ds((g - 2) * GT, GT)], v_bank[:, 0:W].rearrange("p (k n) -> p k n", k=KE), ACT.Copy).then_inc(s["x1T_sb"], 1)
                if there(n, N):
                    act.wait_ge(s["g1_ps"], n + 1)
                    after(act, s["gate_ps"], n)
                    act.activation(g1[:, :], g1_bank[:, 0:GT], ACT.Copy).then_inc(s["g1_sb"], 1)
                    act.wait_ge(s["v_ps"], n + 1)
                    after(act, s["o_ps"], n - 1)
                    act.activation(vv[nk][:, :], v_bank[0:S, :], ACT.Copy).then_inc(s["v_sb"], 1)
                    act.wait_ge(s["dist_done"], n + 1)
                    after(act, s["hats_done"], n)
                    act.activation(dec[:, 0:LEVELS, :, :], dist[:, :, :, :], ACT.Exp, scale=-1.0)
                    act.activation(dec[:, LEVELS, :, :], dist[:, LEVELS - 1, :, :], ACT.Exp).then_inc(s["dec_done"], 1)
                if there(g - 1, N):
                    act.wait_ge(s["onT_ps"], g)
                    after(act, s["att_ps"], g - 1)
                    act.activation(onT[:, :, :], g1_bank[:, 0:W].rearrange("p (k n) -> p k n", k=KE), ACT.Copy).then_inc(s["onT_sb"], 1)
                if there(n, N):
                    act.wait_ge(s["gpre_done"], n + 1)
                    act.activation(gex[:, :], gpre[:, :], ACT.Exp, scale=-1.0).then_inc(s["gex_done"], 1)
                    act.wait_ge(s["gex_done"], n + 1)
                    act.activation(gex[:, :], gex[:, :], ACT.Ln, bias=m.one[0:S, :]).then_inc(s["glog_done"], 1)
                    act.wait_ge(s["glog_done"], n + 1)
                    after(act, s["og_done"], n - 1)
                    act.activation(gate[nk][:, :], gex[:, :], ACT.Exp, scale=-1.0).then_inc(s["gate_done"], 1)
                if there(g - 1, N):
                    act.wait_ge(s["mv2_done"], g)
                    act.activation(lnv[:, 1, :], mv[:, 1, :, 1], ACT.Ln, bias=m.eps[0:S, :]).then_inc(s["lnv2_done"], 1)
                    act.wait_ge(s["lnv2_done"], g)
                    after(act, s["x1_done"], g - 1)
                    act.activation(rstd[:, 1, :], lnv[:, 1, :], ACT.Exp, scale=-0.5).then_inc(s["rstd2_done"], 1)
            steps(act, -1, 2, N - 2, N + 2, step)

        @block.gpsimd
        def _(pool):
            pool.wait_ge(s["zeroed"], 1)

            def step(g, half, k):
                n, nk = g + 1, 1 - k
                if there(g - 2, N):
                    pool.wait_ge(s["x1_done"], g - 1)
                    pool.tensor_tensor(m.xres[:, bass.ds((g - 2) * 2, 2), :], x1[k][:, :, :], m.bo_rows[:, :, :], ALU.add).then_inc(s["x1_kept"], 1)
                if there(n, N):
                    pool.wait_ge(s["dec_done"], n + 1)
                    pool.wait_ge(s["k_done"], n + 1)
                    pool.wait_ge(s["q_done"], n + 1)
                    after(pool, s["a_ps"], (n - 1) * LEVELS)
                    for l in range(LEVELS - 1):
                        for run in LEFT[l]:
                            pool.tensor_tensor(blocks(kh[nk][:, l], run), blocks(kk, run), blocks(dec[:, l], run), ALU.mult)
                        for run in RIGHT[l]:
                            pool.tensor_tensor(blocks(qh[nk][:, l], run), blocks(qq, run), blocks(dec[:, l], run), ALU.mult)
                    pool.tensor_tensor(qh[nk][:, LEVELS - 1], qq[:, :, :], dec[:, LEVELS - 1], ALU.mult)
                    pool.tensor_tensor(kh[nk][:, LEVELS - 1], kk[:, :, :], dec[:, LEVELS], ALU.mult).then_inc(s["hats_done"], 1)
            steps(pool, -1, 2, N - 2, N + 2, step)


K_PART = [0, 0, 1, 1, 0, 2]
Q_PART = [0, 1, 0, 1, 2, 0]
TERMS = len(K_PART)
SHIFT_ROW = TERMS * DK
CHUNK = [0, 128, SC - 128]
CHUNKS = len(CHUNK)
UNITS = NH // 4
SLOTS = UNITS * CHUNKS
VW = DK + 1
PIECES = 6
PAIRS = B // 2


def attention_phase(nc, m, ctx, io):
    def sb(name, shape, dt=F32):
        return ctx.enter_context(nc.sbuf_tensor(name, shape, dt))

    def sem(name):
        return ctx.enter_context(nc.semaphore("a_" + name))

    W = 4 * S
    wk = sb("wk", [C, E])
    wv = sb("wv", [C, E])
    wq = sb("wq", [128, KE, E])
    wo = sb("wo", [128, UNITS, E])
    sel = sb("sel", [128, 128])
    vmask = sb("vmask", [128, CHUNKS])
    bk = sb("bk", [128, KE])
    bq = sb("bq", [128, KE])
    bqs = sb("bqs", [128, KE])
    idb = sb("idb", [128, 128], BF16)
    ctxK = sb("ctxK", [C, 2 * SC])
    ctxV = sb("ctxV", [C, 2 * SC])
    kf = sb("kf", [128, KE, 2 * SC])
    kr = sb("kr", [128, KE, 2 * SC])
    kp = sb("kp", [128, 3, KE, 2 * SC], BF16)
    qf = sb("qf", [128, KE, GT])
    qr = sb("qr", [128, KE, GT])
    qp = sb("qp", [128, 3, KE, GT], BF16)
    KS = [sb(f"KS{k}", [SHIFT_ROW + 1, NH, 2 * SC], BF16) for k in range(2)]
    QS = [sb(f"QS{k}", [SHIFT_ROW + 1, NH, GT], BF16) for k in range(2)]
    V = [sb(f"V{k}", [128, 2, CHUNKS, NH, VW]) for k in range(2)]
    RING = 3
    PT = [sb(f"PT{k}", [128, W]) for k in range(RING)]
    nm = sb("nm", [S, NH], BF16)
    mT = sb("mT", [NH, S], BF16)
    aT = sb("aT", [128, W])
    lz = sb("lz", [128, W])
    rz = sb("rz", [128, W])
    aN = sb("aN", [128, W])
    r2 = sb("r2", [S, E])
    x2 = [sb(f"x2{k}", [S, E]) for k in range(2)]
    st = sb("st_a", [S, 6])
    mv = sb("mv_a", [S, 2])
    lnv = sb("lnv_a", [S, 1])
    rstd = sb("rstd_a", [S, 1])
    kscr = nc.dram_tensor("k_parts", (PAIRS, 3, KE, 128, 2 * SC), BF16, kind="Internal").ap()
    qscr = nc.dram_tensor("q_parts", (PAIRS, 3, KE, 128, GT), BF16, kind="Internal").ap()

    names = ("w_here ready bq_scaled ctxK_in ctxV_in k_ps q_ps v_ps k_sb q_sb v_sb k1 k2r k2 k3 q1 q2r q2 q3 "
             "kscr_in qscr_in stack_in max_ps max_done mT_ps mT_sb st_ps pt_done pv_ps aT_done zb_ps lz_done rz_done "
             "aN_done wo_ps r2_done st_done mv_done lnv_done rstd_done x2_done x2T_ps x2T_sb x2_kept").split()
    s = {n: sem(n) for n in names}
    mrow_in = [sem(f"mrow_in{j}") for j in range(2)]
    lt_out = [sem(f"lt_out{j}") for j in range(2)]
    st_bank, mx_bank, pv_bank, pj_bank, misc = m.bank[0:2], m.bank[2:4], m.bank[4], m.bank[5:7], m.bank[7]
    N = PAIRS
    NW = 8 * 16

    def pieces(p, j):
        if j == 0:
            todo = [("k", p + 2, (t, b), t * 2 + b) for t in range(KE) for b in range(2)] + [("q", p + 2, t, t) for t in range(KE)]
        else:
            todo = [("v", p + 1, (b, c), b * CHUNKS + c) for b in range(2) for c in range(CHUNKS)]
        return {2 * i: x + ((i % 2),) for i, x in enumerate(todo)}

    COUNT = {"k": 4, "q": 2, "v": 6}

    with nc.Block() as block:
        @block.sync
        def _(sp):
            for dst, src in ((wk[:, :], io["Wk"]), (wv[:, :], io["Wv"]), (wq[:, :, :], io["Wq"].rearrange("(k p) n -> p k n", p=128)),
                             (wo[:, :, :], io["Wo_units"]), (sel[:, :], io["c_sel"]), (vmask[:, :], io["c_vmask"]),
                             (bk[:, :], io["bk"]), (bq[:, :], io["bq"])):
                sp.dma_start(dst, src).then_inc(s["w_here"], 16)

            def step(p, half, k):
                nk = 1 - k
                if there(p + 2, N):
                    after(sp, s["k_ps"], (p + 2) * 4)
                    apart(sp, m)
                    sp.dma_start(ctxK[:, :], io["ctxT"][:, bass.ds((p + 2) * 2 * SC, 2 * SC)]).then_inc(s["ctxK_in"], 16)
                if there(p + 1, N):
                    after(sp, s["st_ps"], p * 2 * SLOTS)
                    apart(sp, m)
                    sp.wait_ge(s["kscr_in"], (p + 2) * 32)
                    apart(sp, m)
                    sp.wait_ge(s["qscr_in"], (p + 2) * 16)
                    for t in range(TERMS):
                        rows = slice(t * DK, (t + 1) * DK)
                        apart(sp, m)
                        sp.dma_start(KS[nk][rows, :, :], kscr[bass.ds(p + 1, 1), K_PART[t]].rearrange("a t (h d) n -> d (a t h) n", d=DK)).then_inc(s["stack_in"], 16)
                        apart(sp, m)
                        sp.dma_start(QS[nk][rows, :, :], qscr[bass.ds(p + 1, 1), Q_PART[t]].rearrange("a t (h d) n -> d (a t h) n", d=DK)).then_inc(s["stack_in"], 16)
                    after(sp, s["v_ps"], (p + 1) * 6)
                    apart(sp, m)
                    sp.dma_start(ctxV[:, :], io["ctxT"][:, bass.ds((p + 1) * 2 * SC, 2 * SC)]).then_inc(s["ctxV_in"], 16)
                for j in range(2):
                    b = p * 2 + j - 1
                    if there(b, B):
                        sp.wait_ge(s["x2_done"], b + 1)
                        for part in range(2):
                            first = 1 + 2 * LR * part
                            apart(sp, m)
                            sp.dma_start(m.lt[part, bass.ds(b, 1)].rearrange("a t e -> t (a e)"), x2[1 - j][first:first + 2 * LR:2, :]).then_inc(lt_out[1 - j], 16)
                if there(p + 2, N):
                    for t in range(KE):
                        sp.wait_ge(s["k3"], (p + 2) * 2 + t + 1)
                        apart(sp, m)
                        sp.dma_start(kscr[bass.ds(p + 2, 1), :, t].rearrange("a c p n -> p (a c) n"), kp[:, :, t, :]).then_inc(s["kscr_in"], 16)
                    sp.wait_ge(s["q3"], p + 3)
                    apart(sp, m)
                    sp.dma_start(qscr[bass.ds(p + 2, 1)].rearrange("a c t p n -> p (a c t) n"), qp[:, :, :, :].rearrange("p c t n -> p (c t) n")).then_inc(s["qscr_in"], 16)
            steps(sp, -2, 2, N - 2, N + 1, step)
            for k in range(2):
                sp.wait_ge(lt_out[k], (B // 2) * 32)

        @block.tensor
        def _(pe):
            pe.wait_ge(s["w_here"], NW)
            pe.wait_ge(s["ready"], 1)

            def project(kind, q, args, i, turn, prior_sem, prior_value):
                pj = pj_bank[turn]
                after(pe, prior_sem, prior_value)
                if kind == "k":
                    t, b = args
                    pe.wait_ge(s["ctxK_in"], (q + 1) * 16)
                    pe.matmul(pj[:, 0:SC], wk[:, t * 128:(t + 1) * 128], ctxK[:, b * SC:(b + 1) * SC], start=True, stop=True).then_inc(s["k_ps"], 1)
                elif kind == "q":
                    for e in range(KE):
                        mm = pe.matmul(pj[:, 0:GT], wq[:, e, args * 128:(args + 1) * 128], m.x1T[:, e, bass.ds(q * GT, GT)], start=(e == 0), stop=(e == KE - 1))
                    mm.then_inc(s["q_ps"], 1)
                else:
                    b, c = args
                    pe.wait_ge(s["ctxV_in"], (q + 1) * 16)
                    pe.matmul(pj[:, 0:E], ctxV[:, b * SC + CHUNK[c]:b * SC + CHUNK[c] + 128], wv[:, :], start=True, stop=True).then_inc(s["v_ps"], 1)

            def weigh(b, k, j, slot):
                u, c = slot // CHUNKS, slot % CHUNKS
                n = b * SLOTS + slot
                pe.wait_ge(s["pt_done"], n + 1)
                if slot == 0:
                    pe.wait_ge(s["v_sb"], (b + 1) * 3)
                    after(pe, s["aT_done"], b)
                for i in range(4):
                    mm = pe.matmul(pv_bank[32 * i:32 * i + VW, u * S:(u + 1) * S], V[k][:, j, c, u * 4 + i, :], PT[(j * SLOTS + slot) % RING][:, i * S:(i + 1) * S],
                                   start=(c == 0), stop=(c == CHUNKS - 1), skip_group_check=True)
                mm.then_inc(s["pv_ps"], 1)

            def step(p, half, k):
                nk = 1 - k
                for j in range(2):
                    b = p * 2 + j
                    work = pieces(p, j)
                    for slot in range(SLOTS):
                        if there(b, B):
                            n = b * SLOTS + slot
                            if slot == 0:
                                pe.wait_ge(mrow_in[j], (p + 1) * 16)
                            after(pe, s["pt_done"], n - 1)
                            u, c = slot // CHUNKS, slot % CHUNKS
                            for i in range(4):
                                at = j * SC + CHUNK[c]
                                mm = pe.matmul(st_bank[slot % 2][:, i * S:(i + 1) * S], KS[k][:, u * 4 + i, at:at + 128],
                                               QS[k][:, u * 4 + i, j * S:(j + 1) * S], start=True, stop=True)
                            mm.then_inc(s["st_ps"], 1)
                        if there(b - 1, B) and slot == 0:
                            weigh(b - 1, k if j else nk, 1 - j, SLOTS - 1)
                        elif there(b, B) and slot:
                            weigh(b, k, j, slot - 1)
                        if there(b + 1, B) and slot < NH // 2:
                            kk, jj = (k, 1) if j == 0 else (nk, 0)
                            if slot == 0 and j == 1:
                                pe.wait_ge(s["stack_in"], (p + 2) * TERMS * 2 * 16)
                            for h in (2 * slot, 2 * slot + 1):
                                after(pe, s["max_done"], (b + 1) * NH + h - 1)
                                pe.matmul(mx_bank[h % 2][0:S, 0:SC], QS[kk][0:SHIFT_ROW, h, jj * S:(jj + 1) * S],
                                          KS[kk][0:SHIFT_ROW, h, jj * SC:(jj + 1) * SC], start=True, stop=True).then_inc(s["max_ps"], 1)
                        if slot in work and there(work[slot][1], N):
                            kind, q, args, i, turn = work[slot]
                            before = [(x, jj) for jj in range(2) for x in pieces(p - 1 if jj > j else p, jj).values()]
                            project(kind, q, args, i, turn, *last_piece(p, j, slot))
                        if there(b - 1, B):
                            if slot == 1:
                                pe.wait_ge(s["aT_done"], b)
                                after(pe, s["x2T_sb"], b - 1)
                                after(pe, s["mT_sb"], b + 1 if there(b, B) else B)
                                pe.matmul(misc[:, 0:W], sel[:, :], aT[:, :], start=True, stop=True).then_inc(s["zb_ps"], 1)
                            if slot == 5:
                                pe.wait_ge(s["aN_done"], b)
                                pe.wait_ge(s["lz_done"], b)
                                for u in range(UNITS):
                                    mm = pe.matmul(misc[0:S, 0:E], aN[:, u * S:(u + 1) * S], wo[:, u, :], start=(u == 0), stop=(u == UNITS - 1))
                                mm.then_inc(s["wo_ps"], 1)
                            if slot == 10:
                                pe.wait_ge(s["x2_done"], b)
                                after(pe, s["mT_sb"], b + 2 if there(b + 1, B) else B)
                                for e in range(KE):
                                    mm = pe.transpose(misc[:, e * S:(e + 1) * S], x2[1 - j][:, e * 128:(e + 1) * 128], m.ident[0:S, 0:S])
                                mm.then_inc(s["x2T_ps"], 1)
                        if there(b + 1, B) and slot == 8:
                            pe.wait_ge(s["max_done"], (b + 1) * NH + NH)
                            after(pe, s["r2_done"], b if there(b, B) else 0)
                            pe.transpose(misc[0:NH, 0:S // 2].bitcast(BF16), nm[:, :], idb[0:S, 0:S]).then_inc(s["mT_ps"], 1)
            def last_piece(p, j, slot):
                i = slot // 2
                if j == 0:
                    if i < 2:
                        return s["v_sb"], (p + 1) * 6 - 1 + i
                    if i < 4:
                        return s["k_sb"], (p + 2) * 4 + i - 1
                    return s["k_sb"], (p + 2) * 4 + i - 1
                if i < 2:
                    return s["q_sb"], (min(p + 2, N - 1) if isinstance(p, int) else p + 2) * 2 + i + 1
                return s["v_sb"], (p + 1) * 6 + i - 1
            steps(pe, -2, 2, N - 2, N + 1, step)

        @block.vector
        def _(dve):
            dve.wait_ge(s["w_here"], NW)
            dve.memset(pv_bank[:, :], 0.0)
            dve.tensor_copy(idb[:, :], m.ident[:, :])
            for k in range(2):
                dve.memset(KS[k][SHIFT_ROW:SHIFT_ROW + 1, :, :], 1.0)
                for j in range(2):
                    for c in range(CHUNKS):
                        dve.tensor_scalar(V[k][:, j, c, :, DK], V[k][:, j, c, :, DK], 0.0, vmask[:, c:c + 1], ALU.mult, ALU.add) if False else \
                            dve.tensor_copy(V[k][:, j, c, :, DK:DK + 1], vmask[:, c:c + 1].to_broadcast([128, NH, 1]))
            dve.tensor_scalar(bqs[:, :], bq[:, :], DK ** -0.5, None, ALU.mult).then_inc(s["ready"], 1)
            def step(p, half, k):
                for j in range(2):
                    b = p * 2 + j
                    for slot in range(SLOTS):
                        if there(b + 1, B) and slot < NH // 2:
                            for h in (2 * slot, 2 * slot + 1):
                                dve.wait_ge(s["max_ps"], (b + 1) * NH + h + 1)
                                if h == 0:
                                    after(dve, s["mT_ps"], b + 1)
                                dve.tensor_reduce(nm[:, h:h + 1], mx_bank[h % 2][0:S, 0:SC], AX.X, ALU.max, negate=True).then_inc(s["max_done"], 1)
                        if there(b - 1, B):
                            if slot == 4:
                                dve.wait_ge(s["rz_done"], b)
                                after(dve, s["wo_ps"], b - 1)
                                dve.tensor_tensor(aN[:, :], aT[:, :], rz[:, :], ALU.mult).then_inc(s["aN_done"], 1)
                            if slot == 6:
                                dve.wait_ge(s["wo_ps"], b)
                                dve.tensor_tensor(r2[:, :], misc[0:S, 0:E], m.xres[:, bass.ds(b - 1, 1), :].rearrange("p a e -> p (a e)"), ALU.add).then_inc(s["r2_done"], 1)
                                dve.wait_ge(s["r2_done"], b)
                                dve.bn_stats(st[:, :], r2[:, :]).then_inc(s["st_done"], 1)
                                dve.wait_ge(s["st_done"], b)
                                apart(dve, m)
                                dve.bn_aggr(mv[:, :], st[:, :]).then_inc(s["mv_done"], 1)
                            if slot == 8:
                                dve.wait_ge(s["rstd_done"], b)
                                after(dve, s["x2T_ps"], b - 2)
                                after(dve, s["x2_kept"], b - 2)
                                if there(b - 3, B):
                                    dve.wait_ge(lt_out[1 - j], ((b - 1) // 2 if isinstance(b, int) else p + j - 1) * 32)
                                dve.tensor_scalar(x2[1 - j][:, :], r2[:, :], mv[:, 0:1], rstd[:, 0:1], ALU.subtract, ALU.mult).then_inc(s["x2_done"], 1)
            steps(dve, -2, 2, N - 2, N + 1, step)

        @block.scalar
        def _(act):
            act.preload_act_table_set(LOG_EXP)
            act.wait_ge(s["w_here"], NW)
            act.wait_ge(s["ready"], 1)

            def step(p, half, k):
                nk = 1 - k
                for j in range(2):
                    b = p * 2 + j
                    work = pieces(p, j)
                    for slot in range(SLOTS):
                        if there(b, B):
                            n = b * SLOTS + slot
                            act.wait_ge(s["st_ps"], n + 1)
                            after(act, s["pv_ps"], n + 1 - RING)
                            act.activation(PT[(j * SLOTS + slot) % RING][:, :], st_bank[slot % 2][:, 0:W], ACT.Exp).then_inc(s["pt_done"], 1)
                        if there(b - 1, B):
                            if slot == 0:
                                act.wait_ge(s["pv_ps"], b * SLOTS)
                                after(act, s["aN_done"], b - 1)
                                act.activation(aT[:, :], pv_bank[:, 0:W], ACT.Copy).then_inc(s["aT_done"], 1)
                            if slot == 2:
                                act.wait_ge(s["zb_ps"], b)
                                act.activation(lz[:, :], misc[:, 0:W], ACT.Ln).then_inc(s["lz_done"], 1)
                                act.wait_ge(s["lz_done"], b)
                                after(act, s["aN_done"], b - 1)
                                act.activation(rz[:, :], lz[:, :], ACT.Exp, scale=-1.0).then_inc(s["rz_done"], 1)
                            if slot == 7:
                                act.wait_ge(s["mv_done"], b)
                                act.activation(lnv[:, :], mv[:, 1:2], ACT.Ln, bias=m.eps[0:S, :]).then_inc(s["lnv_done"], 1)
                                act.wait_ge(s["lnv_done"], b)
                                after(act, s["x2_done"], b - 1)
                                act.activation(rstd[:, :], lnv[:, :], ACT.Exp, scale=-0.5).then_inc(s["rstd_done"], 1)
                            if slot == 10 and not there(b, B):
                                pass
                        if there(b + 1, B) and slot == 9:
                            jj, kk = (1, k) if j == 0 else (0, nk)
                            act.wait_ge(s["mT_ps"], b + 2)
                            if there(b, B):
                                act.wait_ge(mrow_in[1 - jj], (p + 1 if j == 0 else p + 1) * 16)
                            act.activation(mT[:, :], misc[0:NH, 0:S // 2].bitcast(BF16), ACT.Copy).then_inc(s["mT_sb"], 1)
                            act.wait_ge(s["mT_sb"], b + 2)
                            act.dma_start(QS[kk][SHIFT_ROW:SHIFT_ROW + 1, :, jj * S:(jj + 1) * S], mT[:, :]).then_inc(mrow_in[jj], 16)
                        if there(b - 1, B) and slot == 11:
                            act.wait_ge(s["x2T_ps"], b)
                            act.activation(m.x1T[:, :, bass.ds((b - 1) * S, S)], misc[:, 0:2 * S].rearrange("p (k n) -> p k n", k=KE), ACT.Copy).then_inc(s["x2T_sb"], 1)
                        if slot in work and there(work[slot][1], N):
                            kind, q, args, i, turn = work[slot]
                            act.wait_ge(s[kind + "_ps"], q * COUNT[kind] + i + 1)
                            pj = pj_bank[turn]
                            if kind == "k":
                                t, bb = args
                                after(act, s["k3"], q * 2 - 1 + t)
                                act.activation(kf[:, t, bb * SC:(bb + 1) * SC], pj[:, 0:SC], ACT.Identity, bias=bk[:, t:t + 1]).then_inc(s["k_sb"], 1)
                            elif kind == "q":
                                after(act, s["q3"], q)
                                act.activation(qf[:, args, :], pj[:, 0:GT], ACT.Identity, bias=bqs[:, args:args + 1], scale=DK ** -0.5).then_inc(s["q_sb"], 1)
                            else:
                                bb, c = args
                                after(act, s["pv_ps"], (q - 1) * 2 * SLOTS)
                                act.activation(V[nk][:, bb, c, :, 0:DK], pj[:, 0:E].rearrange("p (h d) -> p h d", h=NH), ACT.Identity, scale=vmask[:, c:c + 1]).then_inc(s["v_sb"], 1)
            steps(act, -2, 2, N - 2, N + 1, step)

        @block.gpsimd
        def _(pool):
            def split(whole, rest, parts, first, second_rest, second, third, n):
                apart(pool, m)
                pool.tensor_scalar(parts[0], whole, 1.0, None, ALU.mult).then_inc(first, 1)
                pool.wait_ge(first, n)
                pool.tensor_tensor(rest, whole, parts[0], ALU.subtract).then_inc(second_rest, 1)
                pool.wait_ge(second_rest, n)
                apart(pool, m)
                pool.tensor_scalar(parts[1], rest, 1.0, None, ALU.mult).then_inc(second, 1)
                pool.wait_ge(second, n)
                pool.tensor_tensor(parts[2], rest, parts[1], ALU.subtract).then_inc(third, 1)

            def step(p, half, k):
                if there(p + 2, N):
                    q = p + 2
                    for t in range(KE):
                        pool.wait_ge(s["k_sb"], q * 4 + 2 * t + 2)
                        after(pool, s["kscr_in"], q * 32)
                        split(kf[:, t, :], kr[:, t, :], [kp[:, c, t, :] for c in range(3)], s["k1"], s["k2r"], s["k2"], s["k3"], q * 2 + t + 1)
                    pool.wait_ge(s["q_sb"], q * 2 + 2)
                    after(pool, s["qscr_in"], q * 16)
                    split(qf[:, :, :], qr[:, :, :], [qp[:, c] for c in range(3)], s["q1"], s["q2r"], s["q2"], s["q3"], q + 1)
                for j in range(2):
                    b = p * 2 + j - 1
                    if there(b, B):
                        pool.wait_ge(s["x2_done"], b + 1)
                        pool.tensor_tensor(m.xres[:, bass.ds(b, 1), :].rearrange("p a e -> p (a e)"), x2[1 - j][:, :], m.b2_rows[:, :], ALU.add).then_inc(s["x2_kept"], 1)
            steps(pool, -2, 2, N - 2, N + 1, step)


FB = 4
FT = FB * S
FGROUPS = B // FB
LR = 4
TILES = HID // 128


def ffn_phase(nc, m, ctx, io):
    def sb(name, shape, dt=F32):
        return ctx.enter_context(nc.sbuf_tensor(name, shape, dt))

    def sem(name):
        return ctx.enter_context(nc.semaphore("f_" + name))

    R = FB * LR
    w1 = sb("w1", [128, KE, HID])
    w2 = sb("w2", [128, TILES, E])
    b1 = sb("b1", [128, TILES])
    scale = sb("scale", [128, 1])
    own_batch = sb("own_batch", [128, FT])
    own_rows = sb("own_rows", [128, LR, E // LR])
    odd1 = sb("odd1", [128, KE, FB, LR])
    odd2 = sb("odd2", [128, KE, FB, LR])
    even1 = sb("even1", [128, LR, E])
    even2 = sb("even2", [128, E])
    spread2 = sb("spread2", [128, LR, E // LR])
    cm = sb("cm", [128, FT])
    tm = sb("tm", [128, FT])
    hT = sb("hT", [128, TILES, FT])
    r3 = sb("r3", [S, FB, E])
    x3 = sb("x3", [S, FB, E])
    st = sb("st_f", [S, FB, 6])
    mv = sb("mv_f", [S, FB, 2])
    lnv = sb("lnv_f", [S, FB])
    rstd = sb("rstd_f", [S, FB])
    names = ("w_here zeroed even1_in even2_in odd1_done odd2_done c_ps cm_done h_ps gelu_done t_ps tm_done spread_done "
             "y_ps r3_done st_done mv_done lnv_done rstd_done x3_done out_done").split()
    s = {n: sem(n) for n in names}
    h_bank = [m.bank[0], m.bank[1], m.bank[6], m.bank[7]]
    c_bank, t_bank, y_bank = m.bank[2], m.bank[3], m.bank[4:6]
    N = FGROUPS
    NW = 6 * 16

    def steps1(eng, step):
        for g in range(-1, 1):
            step(g)
        with eng.Fori(1, N - 1) as g:
            step(g)
        for g in range(N - 1, N + 1):
            step(g)

    with nc.Block() as block:
        @block.sync
        def _(sp):
            for dst, src in ((w1[:, :, :], io["W1T"].rearrange("(k p) n -> p k n", p=128)), (w2[:, :, :], io["W2T"].rearrange("(k p) n -> p k n", p=128)),
                             (b1[:, :], io["b1"]), (scale[:, :], io["scale"]), (own_batch[:, :], io["c_own_batch"]),
                             (own_rows[:, :, :], io["c_own_rows"])):
                sp.dma_start(dst, src).then_inc(s["w_here"], 16)
            sp.wait_ge(s["zeroed"], 1)

            def step(g):
                if there(g + 1, N):
                    n = g + 1
                    after(sp, s["h_ps"], n * TILES)
                    for i in range(LR):
                        apart(sp, m)
                        sp.dma_start(even1[i:R:LR, i, :], m.lt[0, bass.ds(n * FB, FB), i, :]).then_inc(s["even1_in"], 16)
                    after(sp, s["spread_done"], n)
                    for r in range(LR):
                        apart(sp, m)
                        sp.dma_start(even2[32 * r:32 * r + R, :], m.lt[1, bass.ds(n * FB, FB), :, :].rearrange("b i e -> (b i) e")).then_inc(s["even2_in"], 16)
                if there(g - 1, N):
                    sp.wait_ge(s["x3_done"], g)
                    apart(sp, m)
                    sp.dma_start(io["out"][bass.ds((g - 1) * FB, FB), :, :].rearrange("b s e -> s b e"), x3[:, :, :]).then_inc(s["out_done"], 16)
            steps1(sp, step)
            sp.wait_ge(s["out_done"], N * 16)

        @block.tensor
        def _(pe):
            pe.wait_ge(s["w_here"], NW)
            pe.wait_ge(s["zeroed"], 1)

            def step(g):
                if there(g, N):
                    pe.wait_ge(s["cm_done"], g + 1)
                    pe.wait_ge(s["even1_in"], (g + 1) * LR * 16)
                    for t in range(TILES):
                        after(pe, s["gelu_done"], g * TILES + t + 1 - len(h_bank))
                        out = h_bank[t % len(h_bank)][:, 0:FT]
                        for e in range(KE):
                            pe.matmul(out, w1[:, e, t * 128:(t + 1) * 128], m.x1T[:, e, bass.ds(g * FT, FT)], start=(e == 0), stop=False)
                        pe.matmul(out, even1[:, t // 2, (t % 2) * 128:(t % 2 + 1) * 128], cm[:, :], start=False, stop=True).then_inc(s["h_ps"], 1)
                if there(g + 1, N):
                    pe.wait_ge(s["odd1_done"], g + 2)
                    for e in range(KE):
                        mm = pe.matmul(c_bank[0:R, 0:FT], odd1[:, e, :, :].rearrange("p b i -> p (b i)"), m.x1T[:, e, bass.ds((g + 1) * FT, FT)],
                                       start=(e == 0), stop=(e == KE - 1))
                    mm.then_inc(s["c_ps"], 1)
                if there(g, N):
                    pe.wait_ge(s["gelu_done"], (g + 1) * TILES)
                    pe.wait_ge(s["odd2_done"], g + 1)
                    after(pe, s["tm_done"], g)
                    for e in range(KE):
                        for r in range(LR):
                            mm = pe.matmul(t_bank[32 * r:32 * r + R, 0:FT], odd2[:, e, :, :].rearrange("p b i -> p (b i)"), hT[:, 2 * r + e, :],
                                           start=(e == 0), stop=(e == KE - 1), skip_group_check=True)
                    mm.then_inc(s["t_ps"], 1)
                    after(pe, s["r3_done"], 2 * g)
                    for y in range(2):
                        for b in range(2):
                            out = y_bank[y][0:S, b * E:(b + 1) * E]
                            tok = slice((y * 2 + b) * S, (y * 2 + b + 1) * S)
                            for t in range(TILES):
                                pe.matmul(out, hT[:, t, tok], w2[:, t, :], start=(t == 0), stop=False)
                            if y == 0 and b == 0:
                                pe.wait_ge(s["tm_done"], g + 1)
                                pe.wait_ge(s["spread_done"], g + 1)
                            mm = pe.matmul(out, tm[:, tok], spread2[:, :, :].rearrange("p i n -> p (i n)"), start=False, stop=True)
                        mm.then_inc(s["y_ps"], 1)
            steps1(pe, step)

        @block.vector
        def _(dve):
            dve.memset(even1[:, :, :], 0.0)
            dve.memset(even2[:, :], 0.0)
            dve.memset(spread2[:, :, :], 0.0)
            dve.memset(t_bank[:, :], 0.0)
            dve.memset(cm[:, :], 0.0).then_inc(s["zeroed"], 1)
            dve.wait_ge(s["zeroed"], 1)
            dve.wait_ge(s["w_here"], NW)

            def step(g):
                if there(g - 1, N):
                    after(dve, s["x3_done"], g - 1)
                    for y in range(2):
                        dve.wait_ge(s["y_ps"], (g - 1) * 2 + y + 1)
                        dve.tensor_tensor(r3[:, 2 * y:2 * y + 2, :], y_bank[y][0:S, :].rearrange("p (b e) -> p b e", b=2),
                                          m.xres[:, bass.ds((g - 1) * FB + 2 * y, 2), :], ALU.add).then_inc(s["r3_done"], 1)
                    for b in range(FB):
                        dve.wait_ge(s["r3_done"], (g - 1) * 2 + b // 2 + 1)
                        bn = dve.bn_stats(st[:, b, :], r3[:, b, :])
                    bn.then_inc(s["st_done"], 1)
                    dve.wait_ge(s["st_done"], g)
                    apart(dve, m)
                    for b in range(FB):
                        bn = dve.bn_aggr(mv[:, b, :], st[:, b, :])
                    bn.then_inc(s["mv_done"], 1)
                if there(g, N):
                    dve.wait_ge(s["even2_in"], (g + 1) * LR * 16)
                    for r in range(LR):
                        rows = slice(32 * r, 32 * r + R)
                        a = even2[rows, r:E:LR]
                        src = bass.AP(tensor=a.tensor, offset=a.offset, ap=[list(a.ap[0]), [0, LR], list(a.ap[1])])
                        tt = dve.tensor_tensor(spread2[rows, :, :], src, own_rows[rows, :, :], ALU.mult)
                    tt.then_inc(s["spread_done"], 1)
                if there(g + 1, N):
                    dve.wait_ge(s["c_ps"], g + 2)
                    dve.scalar_tensor_tensor(cm[0:R, :], c_bank[0:R, 0:FT], scale[0:R, 0:1], own_batch[0:R, :], ALU.mult, ALU.mult).then_inc(s["cm_done"], 1)
                if there(g, N):
                    dve.wait_ge(s["t_ps"], g + 1)
                    dve.scalar_tensor_tensor(tm[:, :], t_bank[:, 0:FT], scale[:, 0:1], own_batch[:, :], ALU.mult, ALU.mult).then_inc(s["tm_done"], 1)
                if there(g - 1, N):
                    dve.wait_ge(s["rstd_done"], g)
                    after(dve, s["out_done"], (g - 1) * 16)
                    for b in range(FB):
                        ts = dve.tensor_scalar(x3[:, b, :], r3[:, b, :], mv[:, b, 0:1], rstd[:, b:b + 1], ALU.subtract, ALU.mult)
                    ts.then_inc(s["x3_done"], 1)
            steps1(dve, step)

        @block.scalar
        def _(act):
            act.wait_ge(s["w_here"], NW)

            def odd(n, first):
                a = m.x1T[:, :, bass.ds(n * FT, FT)].rearrange("p k (b s) -> p k b s", b=FB)
                return a[:, :, :, first:first + 2 * LR:2]

            def step(g):
                if there(g, N):
                    act.preload_act_table_set(GELU)
                    for t in range(TILES):
                        act.wait_ge(s["h_ps"], g * TILES + t + 1)
                        act.activation(hT[:, t, :], h_bank[t % len(h_bank)][:, 0:FT], ACT.Gelu, bias=b1[:, t:t + 1]).then_inc(s["gelu_done"], 1)
                        if t == 0:
                            after(act, s["t_ps"], g)
                            for e in range(KE):
                                cp = act.activation(odd2[:, e], odd(g, 10)[:, e], ACT.Copy)
                            cp.then_inc(s["odd2_done"], 1)
                            if there(g + 1, N):
                                after(act, s["c_ps"], g + 1)
                                for e in range(KE):
                                    cp = act.activation(odd1[:, e], odd(g + 1, 2)[:, e], ACT.Copy)
                                cp.then_inc(s["odd1_done"], 1)
                elif there(g + 1, N):
                    for e in range(KE):
                        cp = act.activation(odd1[:, e], odd(g + 1, 2)[:, e], ACT.Copy)
                    cp.then_inc(s["odd1_done"], 1)
                if there(g - 1, N):
                    act.preload_act_table_set(LOG_EXP)
                    act.wait_ge(s["mv_done"], g)
                    act.activation(lnv[:, :], mv[:, :, 1], ACT.Ln, bias=m.eps[0:S, :]).then_inc(s["lnv_done"], 1)
                    act.wait_ge(s["lnv_done"], g)
                    after(act, s["x3_done"], g - 1)
                    act.activation(rstd[:, :], lnv[:, :], ACT.Exp, scale=-0.5).then_inc(s["rstd_done"], 1)
            steps1(act, step)


def setup_phase(nc, m, ctx, io):
    def sb(name, shape, dt=F32):
        return ctx.enter_context(nc.sbuf_tensor(name, shape, dt))

    with ExitStack() as own:
        here = own.enter_context(nc.semaphore("s_here"))
        filled = own.enter_context(nc.semaphore("s_filled"))
        spread = own.enter_context(nc.semaphore("s_spread"))
        rows_ps = own.enter_context(nc.semaphore("s_rows_ps"))
        kept = own.enter_context(nc.semaphore("s_kept"))
        m.passed = ctx.enter_context(nc.semaphore("passed"))
        wo = own.enter_context(nc.sbuf_tensor("s_wo", [128, KE, E], F32))
        bv = own.enter_context(nc.sbuf_tensor("s_bv", [128, KE], F32))
        bvs = own.enter_context(nc.sbuf_tensor("s_bvs", [128, KE, S], F32))
        row = own.enter_context(nc.sbuf_tensor("s_row", [1, 2 * E], F32))
        ones = own.enter_context(nc.sbuf_tensor("s_ones", [128, S], F32))
        with nc.Block() as block:
            @block.sync
            def _(sp):
                sp.dma_start(m.ident[:, :], io["c_ident"]).then_inc(here, 16)
                sp.dma_start(wo[:, :, :], io["Wo"].rearrange("(k p) n -> p k n", p=128)).then_inc(here, 16)
                sp.dma_start(bv[:, :], io["bv"]).then_inc(here, 16)
                sp.dma_start(row[0:1, 0:E], io["bo"].rearrange("(a n) -> a n", a=1)).then_inc(here, 16)
                sp.dma_start(row[0:1, E:2 * E], io["b2"].rearrange("(a n) -> a n", a=1)).then_inc(here, 16)

            @block.vector
            def _(dve):
                dve.memset(m.eps[:, :], EPS)
                dve.memset(m.one[:, :], 1.0)
                dve.memset(ones[:, :], 1.0).then_inc(filled, 1)
                dve.wait_ge(filled, 1)
                dve.wait_ge(here, 5 * 16)
                for e in range(KE):
                    ts = dve.tensor_scalar(bvs[:, e, :], ones[:, :], bv[:, e:e + 1], None, ALU.mult)
                ts.then_inc(spread, 1)
                dve.wait_ge(rows_ps, 1)
                for b in range(2):
                    cp = dve.tensor_copy(m.bo_rows[:, b, :], m.bank[0][0:S, 0:E])
                cp.then_inc(kept, 1)
                dve.tensor_copy(m.b2_rows[:, :], m.bank[1][0:S, 0:E]).then_inc(kept, 1)
                dve.wait_ge(kept, 2)

            @block.tensor
            def _(pe):
                pe.wait_ge(spread, 1)
                for e in range(KE):
                    pe.matmul(m.bank[0][0:S, 0:E], bvs[:, e, :], wo[:, e, :], start=(e == 0), stop=False)
                pe.matmul(m.bank[0][0:S, 0:E], ones[0:1, :], row[0:1, 0:E], start=False, stop=True)
                pe.matmul(m.bank[1][0:S, 0:E], ones[0:1, :], row[0:1, E:2 * E], start=True, stop=True).then_inc(rows_ps, 1)


def program(nc, io):
    with ExitStack() as ctx:
        m = Memory()
        m.bank = [ctx.enter_context(nc.psum_tensor(f"bank{i}", [128, 512], F32)) for i in range(8)]
        m.ident = ctx.enter_context(nc.sbuf_tensor("ident", [128, 128], F32))
        m.eps = ctx.enter_context(nc.sbuf_tensor("eps", [128, 1], F32))
        m.one = ctx.enter_context(nc.sbuf_tensor("one", [128, 1], F32))
        m.bo_rows = ctx.enter_context(nc.sbuf_tensor("bo_rows", [S, 2, E], F32))
        m.b2_rows = ctx.enter_context(nc.sbuf_tensor("b2_rows", [S, E], F32))
        m.xres = ctx.enter_context(nc.sbuf_tensor("xres", [S, B, E], F32))
        m.lt = nc.dram_tensor("lora_tokens", (2, B, LR, E), F32, kind="Internal").ap()
        m.x1T = ctx.enter_context(nc.sbuf_tensor("x1T", [128, KE, B * S], F32))
        setup_phase(nc, m, ctx, io)
        with ExitStack() as own:
            gla_phase(nc, m, own, io)
        with ExitStack() as own:
            attention_phase(nc, m, own, io)
        with ExitStack() as own:
            ffn_phase(nc, m, own, io)


def laid_out(inputs):
    a = {k: np.asarray(v) for k, v in inputs.items()}
    out = {
        "x": a["x"],
        "xT": a["x"].reshape(B * S, KE, 128).transpose(1, 2, 0),
        "W_inT": a["L0_attn_W_in"].T, "W_outT": a["L0_attn_W_out"].T,
        "W_g1T": a["L0_attn_W_g1"].T, "W_g2T": a["L0_attn_W_g2"].T, "ln_w": a["L0_attn_ln_w"].reshape(KE, 128).T,
        "Wo": a["L0_xattn_Wo"], "bv": a["L0_xattn_bv"].reshape(KE, 128).T, "bo": a["L0_xattn_bo"], "b2": a["L0_ffn_b2"],
    }
    wo = np.zeros((4, 32, UNITS, E), np.float32)
    wo[:, 0:DK] = a["L0_xattn_Wo"].reshape(UNITS, 4, DK, E).transpose(1, 2, 0, 3)
    out.update({
        "W1T": a["L0_ffn_W1"].T, "W2T": a["L0_ffn_W2"].T, "b1": a["L0_ffn_b1"].reshape(TILES, 128).T,
        "scale": np.broadcast_to(a["L0_ffn_scale"], (128, 1)),
        "ctxT": a["ctx_512"].reshape(B * SC, C).T, "Wk": a["L0_xattn_Wk"], "Wv": a["L0_xattn_Wv"], "Wq": a["L0_xattn_Wq"],
        "Wo_units": wo.reshape(128, UNITS, E), "bk": a["L0_xattn_bk"].reshape(KE, 128).T, "bq": a["L0_xattn_bq"].reshape(KE, 128).T,
    })
    out.update(constants())
    return {k: np.ascontiguousarray(v) for k, v in out.items()}


def kernel(**inputs):
    import concourse.bacc as bacc
    from concourse.bass_utils import run_bass_kernel_spmd

    nc = bacc.Bacc("TRN2", target_bir_lowering=False, num_devices=1)
    arrays = laid_out(inputs)
    io = {k: nc.dram_tensor("in_" + k, v.shape, mybir.dt.from_np(v.dtype), kind="ExternalInput").ap() for k, v in arrays.items()}
    io["out"] = nc.dram_tensor("out", (B, S, E), F32, kind="ExternalOutput").ap()
    program(nc, io)
    r = run_bass_kernel_spmd(nc, [{"in_" + k: v for k, v in arrays.items()}], core_ids=[0])
    return r.results[0]["out"]
```

```python
import numpy as np
import concourse.bass as bass
from concourse import mybir
from contextlib import ExitStack

F32 = mybir.dt.float32
BF16 = mybir.dt.bfloat16
I32 = mybir.dt.int32
ALU = mybir.AluOpType
ACT = mybir.ActivationFunctionType
AX = mybir.AxisListType

B, S, E = 32, 112, 256
D = 128
H = E // D
KE = E // 128
SC, C = 375, 128
NH, DK = 16, 16
HID = 1024
EPS = 1e-5
GELU = "gelu_and_others"
LOG_EXP = "natural_log_exp_and_others"

LEFT = [[(0, 1, 112, 64, 63)], [(0, 2, 64, 32, 31)], [(0, 3, 32, 16, 15)], [(0, 7, 16, 8, 7)]]
RIGHT = [[(64, 1, 112, 48, 63)], [(32, 2, 64, 16, 31), (48, 1, 112, 16, 31)], [(16, 3, 32, 16, 15)], [(8, 7, 16, 8, 7)]]
BASE = 8
BASE_CUT = 3
LEVELS = len(LEFT) + 1
LOG_MAX = 20.0
GATE_MAX = 40.0
SEG = 4
GT = 2 * S
GROUPS = B // 2


def tokens_of(run):
    first, blocks, stride, length, _ = run
    return [first + n * stride + i for n in range(blocks) for i in range(length)]


def constants():
    f = np.float32
    ident = np.eye(128, dtype=f)
    mask = np.zeros((S, LEVELS, S), np.int32)
    for n in range(LEVELS - 1):
        for l in LEFT[n]:
            for r in RIGHT[n]:
                for lb in range(l[1]):
                    for rb in range(r[1]):
                        if lb == rb:
                            s0, t0 = l[0] + lb * l[2], r[0] + rb * r[2]
                            mask[s0:s0 + l[3], n, t0:t0 + r[3]] = 1
    s, t = np.arange(S)[:, None], np.arange(S)[None, :]
    mask[:, LEVELS - 1, :] = (s // BASE == t // BASE) & (s <= t)
    assert (mask.sum(1) == (s <= t)).all()
    masks = np.repeat(mask[:, :, None, :], SEG, axis=2).reshape(S, LEVELS * SEG * S)
    keep = np.ones((128, SEG, S), f)
    keep[:, :, 0] = 0
    sel = np.zeros((128, 128), f)
    for i in range(4):
        sel[32 * i + DK, 32 * i:32 * i + 32] = 1
    vmask = np.ones((128, CHUNKS), f)
    vmask[0:CHUNK[1] + 128 - CHUNK[2], 2] = 0
    row = np.arange(128)
    batch_of = np.where(row % 32 < FB * LR, row % 32 // LR, -1)
    own_batch = (batch_of[:, None] == np.arange(FT)[None, :] // S).astype(f)
    own_rows = np.repeat((row[:, None] % LR == np.arange(LR)[None, :]).astype(f)[:, :, None], E // LR, axis=2)
    return {"c_own_batch": own_batch, "c_own_rows": own_rows, "c_sel": sel, "c_vmask": vmask, "c_ident": ident, "c_masks": np.ascontiguousarray(masks), "c_keep": keep.reshape(128, SEG * S)}


def after(eng, sem, value):
    if not isinstance(value, int) or value > 0:
        eng.wait_ge(sem, value)


def apart(eng, m):
    eng.sem_inc(m.passed, 1)


def there(g, n):
    return not isinstance(g, int) or 0 <= g < n


def steps(eng, first, lo, hi, last, step):
    for g in range(first, lo):
        step(g, g // 2, g % 2)
    with eng.Fori(0, (hi - lo) // 2) as i:
        for k in range(2):
            step(i * 2 + (lo + k), i + lo // 2, k)
    for g in range(hi, last):
        step(g, g // 2, g % 2)


def blocks(seg, run):
    first, n, stride, length, _ = run
    a = seg[:, :, first:first + length]
    return bass.AP(tensor=a.tensor, offset=a.offset, ap=[list(a.ap[0]), list(a.ap[1]), [stride, n], list(a.ap[2])])


def cuts(seg, run):
    _, n, stride, length, cut = run
    a = seg[:, :, cut:cut + 1]
    return bass.AP(tensor=a.tensor, offset=a.offset, ap=[list(a.ap[0]), list(a.ap[1]), [stride, n], [0, length]])


class Memory:
    pass


def gla_phase(nc, m, ctx, io):
    def sb(name, shape, dt=F32):
        return ctx.enter_context(nc.sbuf_tensor(name, shape, dt))

    def sem(name):
        return ctx.enter_context(nc.semaphore(name))

    W = SEG * S
    w_in = sb("w_in", [128, KE, 3 * E])
    w_out = sb("w_out", [128, KE, E])
    w_g1 = sb("w_g1", [128, KE, D])
    w_g2 = sb("w_g2", [128, E])
    ln_w = sb("ln_w", [128, KE])
    masks = sb("masks", [S, LEVELS, W], I32)
    keep = sb("keep", [128, W])
    xT = [sb(f"xT{k}", [128, KE, GT]) for k in range(2)]
    xr = [sb(f"xr{k}", [S, 2, E]) for k in range(2)]
    pre = sb("pre", [128, 2, W])
    ex = sb("ex", [128, 2, W])
    lp = sb("lp", [128, 2, W])
    sg = sb("sg", [128, 2, W])
    kk = sb("kk", [128, SEG, S])
    qq = sb("qq", [128, SEG, S])
    cum = sb("cum", [128, SEG, S])
    dist = sb("dist", [128, LEVELS, SEG, S])
    dec = sb("dec", [128, LEVELS + 1, SEG, S])
    kh = [sb(f"kh{k}", [128, LEVELS, SEG, S]) for k in range(2)]
    qh = [sb(f"qh{k}", [128, LEVELS, SEG, S]) for k in range(2)]
    aT = [sb(f"aT{k}", [S, W]) for k in range(2)]
    vv = [sb(f"vv{k}", [S, 2 * E]) for k in range(2)]
    g1 = sb("g1", [128, GT])
    gpre = sb("gpre", [S, 2 * E])
    gex = sb("gex", [S, 2 * E])
    gate = [sb(f"gate{k}", [S, 2 * E]) for k in range(2)]
    og = sb("og", [S, 2, E])
    on = sb("on", [S, 2, E])
    onT = sb("onT", [128, KE, GT])
    r1 = sb("r1", [S, 2, E])
    x1 = [sb(f"x1{k}", [S, 2, E]) for k in range(2)]
    st = sb("st", [S, 2, 2, 6])
    mv = sb("mv", [S, 2, 2, 2])
    lnv = sb("lnv", [S, 2, 2])
    rstd = sb("rstd", [S, 2, 2])

    names = ("w_here zeroed lnw_folded q_ps lg_ps v_ps g1_ps gate_ps a_ps o_ps onT_ps att_ps x1T_ps "
             "pre_lg pre_q e_done l_done f_done k_done q_done cum_done dist_done dec_done hats_done a_masked "
             "gpre_done gex_done glog_done gate_done v_sb g1_sb og_done st_done mv_done lnv_done rstd_done on_done "
             "onT_sb r1_done x1_done x1T_sb x1_kept").split()
    s = {n: sem("g_" + n) for n in names}
    xT_in = [sem(f"g_xT_in{k}") for k in range(2)]
    xr_in = [sem(f"g_xr_in{k}") for k in range(2)]
    q_bank, lg_bank, v_bank, g1_bank, gate_bank, a0, a1, o_bank = m.bank
    a_bank = [a0, a1]
    N = GROUPS

    def kinds(g):
        return [i for i in range(2) if there(g - 1 - i, N)]

    with nc.Block() as block:
        @block.sync
        def _(sp):
            sp.dma_start(w_in[:, :, :], io["W_inT"].rearrange("(k p) n -> p k n", p=128)).then_inc(s["w_here"], 16)
            sp.dma_start(w_g1[:, :, :], io["W_g1T"].rearrange("(k p) n -> p k n", p=128)).then_inc(s["w_here"], 16)
            sp.dma_start(w_g2[:, :], io["W_g2T"]).then_inc(s["w_here"], 16)
            sp.dma_start(w_out[:, :, :], io["W_outT"].rearrange("(k p) n -> p k n", p=128)).then_inc(s["w_here"], 16)
            sp.dma_start(ln_w[:, :], io["ln_w"]).then_inc(s["w_here"], 16)
            sp.dma_start(masks[:, :, :], io["c_masks"].rearrange("p (l n) -> p l n", l=LEVELS)).then_inc(s["w_here"], 16)
            sp.dma_start(keep[:, :], io["c_keep"]).then_inc(s["w_here"], 16)

            def step(g, half, k):
                if there(g + 2, N):
                    after(sp, s["v_ps"], g + 1)
                    apart(sp, m)
                    sp.dma_start(xT[k][:, :, :], io["xT"][:, :, bass.ds((g + 2) * GT, GT)].rearrange("k p n -> p k n")).then_inc(xT_in[k], 16)
                if there(g, N):
                    after(sp, s["r1_done"], g - 1)
                    apart(sp, m)
                    sp.dma_start(xr[k][:, :, :], io["x"][bass.ds(g * 2, 2), :, :].rearrange("b s e -> s b e")).then_inc(xr_in[k], 16)
            steps(sp, -2, 2, N - 2, N, step)

        WTS = 7 * 16

        @block.tensor
        def _(pe):
            pe.wait_ge(s["w_here"], WTS)

            def step(g, half, k):
                n, nk = g + 1, 1 - k
                if there(g + 2, N):
                    pe.wait_ge(xT_in[k], half * 16 + 32)
                    after(pe, s["pre_lg"], g + 2)
                    for h in range(H):
                        for e in range(KE):
                            mm = pe.matmul(lg_bank[:, h * GT:(h + 1) * GT], w_in[:, e, 2 * E + h * D:2 * E + (h + 1) * D],
                                           xT[k][:, e, :], start=(e == 0), stop=(e == KE - 1))
                    mm.then_inc(s["lg_ps"], 1)
                    after(pe, s["q_done"], g + 2)
                    for h in range(H):
                        for e in range(KE):
                            mm = pe.matmul(q_bank[:, h * GT:(h + 1) * GT], w_in[:, e, E + h * D:E + (h + 1) * D],
                                           xT[k][:, e, :], start=(e == 0), stop=(e == KE - 1))
                    mm.then_inc(s["q_ps"], 1)
                def transpose_x1():
                    pe.wait_ge(s["x1_done"], g - 1)
                    after(pe, s["v_sb"], g + 1 if there(g, N) else N)
                    for e in range(KE):
                        for b in range(2):
                            mm = pe.transpose(v_bank[:, (e * 2 + b) * S:(e * 2 + b + 1) * S], x1[k][:, b, e * 128:(e + 1) * 128],
                                              m.ident[0:S, 0:S])
                    mm.then_inc(s["x1T_ps"], 1)
                if there(g, N):
                    pe.wait_ge(s["hats_done"], g + 1)
                    for l in range(LEVELS):
                        if l == LEVELS - 1 and there(g - 2, N):
                            transpose_x1()
                        turn = g * LEVELS + l
                        after(pe, s["a_masked"], turn - 1)
                        for j in range(SEG):
                            mm = pe.matmul(a_bank[(k * LEVELS + l) % 2][0:S, j * S:(j + 1) * S], kh[k][:, l, j, :], qh[k][:, l, j, :],
                                           start=True, stop=True)
                        mm.then_inc(s["a_ps"], 1)
                elif there(g - 2, N):
                    transpose_x1()
                if there(n, N):
                    after(pe, s["onT_sb"], n - 2)
                    for e in range(KE):
                        mm = pe.matmul(g1_bank[:, 0:GT], w_g1[:, e, :], xT[nk][:, e, :], start=(e == 0), stop=(e == KE - 1))
                    mm.then_inc(s["g1_ps"], 1)
                    after(pe, s["x1T_sb"], n - 2)
                    after(pe, s["v_sb"], n)
                    for b in range(2):
                        for e in range(KE):
                            mm = pe.matmul(v_bank[0:S, b * E:(b + 1) * E], xT[nk][:, e, b * S:(b + 1) * S], w_in[:, e, 0:E],
                                           start=(e == 0), stop=(e == KE - 1))
                    mm.then_inc(s["v_ps"], 1)
                    pe.wait_ge(s["g1_sb"], n + 1)
                    after(pe, s["r1_done"], n - 2)
                    for b in range(2):
                        mm = pe.matmul(gate_bank[0:S, b * E:(b + 1) * E], g1[:, b * S:(b + 1) * S], w_g2[:, :], start=True, stop=True)
                    mm.then_inc(s["gate_ps"], 1)
                if there(g - 1, N):
                    pe.wait_ge(s["on_done"], g)
                    for e in range(KE):
                        for b in range(2):
                            mm = pe.transpose(g1_bank[:, (e * 2 + b) * S:(e * 2 + b + 1) * S], on[:, b, e * 128:(e + 1) * 128],
                                              m.ident[0:S, 0:S])
                    mm.then_inc(s["onT_ps"], 1)
                if there(g, N):
                    pe.wait_ge(s["a_masked"], g * LEVELS + LEVELS)
                    pe.wait_ge(s["v_sb"], g + 1)
                    after(pe, s["og_done"], g)
                    for b in range(2):
                        for h in range(H):
                            j = h * 2 + b
                            c = b * E + h * D
                            mm = pe.matmul(o_bank[0:S, c:c + D], aT[k][:, j * S:(j + 1) * S], vv[k][:, c:c + D], start=True, stop=True)
                    mm.then_inc(s["o_ps"], 1)
                if there(g - 1, N):
                    pe.wait_ge(s["onT_sb"], g)
                    pe.wait_ge(s["gpre_done"], g + 2 if there(g + 1, N) else N)
                    for b in range(2):
                        for e in range(KE):
                            mm = pe.matmul(gate_bank[0:S, b * E:(b + 1) * E], onT[:, e, b * S:(b + 1) * S], w_out[:, e, :],
                                           start=(e == 0), stop=(e == KE - 1))
                    mm.then_inc(s["att_ps"], 1)
            pe.wait_ge(s["lnw_folded"], 1)
            steps(pe, -2, 2, N - 2, N + 2, step)

        @block.vector
        def _(dve):
            for k in range(2):
                dve.memset(kh[k][:, :, :, :], 0.0)
                dve.memset(qh[k][:, :, :, :], 0.0)
                dve.memset(aT[k][:, :], 0.0)
            dve.memset(dist[:, :, :, :], 0.0).then_inc(s["zeroed"], 1)
            dve.wait_ge(s["w_here"], WTS)
            for e in range(KE):
                mul = dve.tensor_scalar(w_out[:, e, :], w_out[:, e, :], ln_w[:, e:e + 1], None, ALU.mult)
            mul.then_inc(s["lnw_folded"], 1)
            dve.wait_ge(s["zeroed"], 1)

            def step(g, half, k):
                n, nk = g + 1, 1 - k
                f = g + 2

                def normalise():
                    if there(g - 1, N):
                        dve.wait_ge(s["rstd_done"], g)
                        after(dve, s["onT_ps"], g - 1)
                        for b in range(2):
                            ts = dve.tensor_scalar(on[:, b, :], og[:, b, :], mv[:, 0, b, 0:1], rstd[:, 0, b:b + 1], ALU.subtract, ALU.mult)
                        ts.then_inc(s["on_done"], 1)
                    if there(g - 2, N):
                        dve.wait_ge(s["rstd_done"], g)
                        after(dve, s["x1T_ps"], g - 3)
                        after(dve, s["x1_kept"], g - 3)
                        for b in range(2):
                            ts = dve.tensor_scalar(x1[k][:, b, :], r1[:, b, :], mv[:, 1, b, 0:1], rstd[:, 1, b:b + 1], ALU.subtract, ALU.mult)
                        ts.then_inc(s["x1_done"], 1)

                if there(g - 2, N):
                    dve.wait_ge(s["att_ps"], g - 1)
                    dve.wait_ge(xr_in[k], half * 16)
                    dve.tensor_tensor(r1[:, :, :].rearrange("p b e -> p (b e)"), gate_bank[0:S, :], xr[k][:, :, :].rearrange("p b e -> p (b e)"), ALU.add).then_inc(s["r1_done"], 1)
                if there(g - 1, N):
                    dve.wait_ge(s["o_ps"], g)
                    dve.wait_ge(s["gate_done"], g)
                    dve.tensor_tensor(og[:, :, :].rearrange("p b e -> p (b e)"), o_bank[0:S, :], gate[nk][:, :], ALU.mult).then_inc(s["og_done"], 1)
                if there(g - 2, N):
                    dve.wait_ge(s["r1_done"], g - 1)
                    for b in range(2):
                        bn = dve.bn_stats(st[:, 1, b, :], r1[:, b, :])
                    if not there(g - 1, N):
                        bn.then_inc(s["st_done"], 1)
                if there(g - 1, N):
                    dve.wait_ge(s["og_done"], g)
                    for b in range(2):
                        bn = dve.bn_stats(st[:, 0, b, :], og[:, b, :])
                    bn.then_inc(s["st_done"], 1)
                if there(g - 1, N) or there(g - 2, N):
                    dve.wait_ge(s["st_done"], g)
                    apart(dve, m)
                    for i in kinds(g):
                        for b in range(2):
                            bn = dve.bn_aggr(mv[:, i, b, :], st[:, i, b, :])
                    bn.then_inc(s["mv_done"], 1)
                if there(f, N):
                    dve.wait_ge(s["lg_ps"], f + 1)
                    after(dve, s["e_done"], f)
                    dve.tensor_scalar(pre[:, 0, :], lg_bank[:, 0:W], -LOG_MAX, None, ALU.max).then_inc(s["pre_lg"], 1)
                    dve.wait_ge(s["q_ps"], f + 1)
                    dve.tensor_scalar(pre[:, 1, :], q_bank[:, 0:W], -GATE_MAX, None, ALU.max).then_inc(s["pre_q"], 1)
                if there(g, N):
                    for l in range(LEVELS):
                        if l == 2:
                            normalise()
                        dve.wait_ge(s["a_ps"], g * LEVELS + l + 1)
                        after(dve, s["a_masked"], g * LEVELS + l)
                        if l == 0:
                            after(dve, s["o_ps"], g - 1)
                        apart(dve, m)
                        dve.copy_predicated(aT[k][:, :], masks[:, l, :], a_bank[(k * LEVELS + l) % 2][0:S, 0:W]).then_inc(s["a_masked"], 1)
                else:
                    normalise()
                if there(f, N):
                    dve.wait_ge(s["l_done"], f + 1)
                    after(dve, s["dist_done"], f)
                    dve.tensor_tensor_scan(cum[:, :, :].rearrange("p g s -> p (g s)"), keep[:, :], lp[:, 0, :], 0.0, ALU.mult, ALU.add).then_inc(s["cum_done"], 1)
                    dve.wait_ge(s["f_done"], f + 1)
                    after(dve, s["hats_done"], f)
                    dve.tensor_tensor(qq[:, :, :].rearrange("p g s -> p (g s)"), q_bank[:, 0:W], sg[:, 1, :], ALU.mult).then_inc(s["q_done"], 1)
                    dve.wait_ge(s["cum_done"], f + 1)
                    after(dve, s["dec_done"], f)
                for l in range(LEVELS - 1):
                    if l == LEVELS - 2 and there(n, N):
                        dve.wait_ge(s["gate_ps"], n + 1)
                        after(dve, s["gex_done"], n)
                        dve.tensor_scalar(gpre[:, :], gate_bank[0:S, :], -GATE_MAX, None, ALU.max).then_inc(s["gpre_done"], 1)
                    if there(f, N):
                        for run in LEFT[l]:
                            dve.tensor_tensor(blocks(dist[:, l], run), cuts(cum, run), blocks(cum, run), ALU.subtract)
                        for run in RIGHT[l]:
                            dve.tensor_tensor(blocks(dist[:, l], run), blocks(cum, run), cuts(cum, run), ALU.subtract)
                if there(f, N):
                    run = (0, S // BASE, BASE, BASE, BASE_CUT)
                    dve.tensor_tensor(blocks(dist[:, LEVELS - 1], run), blocks(cum, run), cuts(cum, run), ALU.subtract).then_inc(s["dist_done"], 1)
            steps(dve, -2, 4, N - 2, N + 2, step)

        @block.scalar
        def _(act):
            act.preload_act_table_set(LOG_EXP)
            act.wait_ge(s["zeroed"], 1)

            def step(g, half, k):
                n, nk = g + 1, 1 - k
                if there(g - 1, N) or there(g - 2, N):
                    of = slice(kinds(g)[0], kinds(g)[-1] + 1)
                    act.wait_ge(s["mv_done"], g)
                    act.activation(lnv[:, of, :], mv[:, of, :, 1], ACT.Ln, bias=m.eps[0:S, :]).then_inc(s["lnv_done"], 1)
                    act.wait_ge(s["lnv_done"], g)
                    after(act, s["on_done"], g - 1)
                    after(act, s["x1_done"], g - 2)
                    act.activation(rstd[:, of, :], lnv[:, of, :], ACT.Exp, scale=-0.5).then_inc(s["rstd_done"], 1)
                f = g + 2
                if there(f, N):
                    act.wait_ge(s["pre_lg"], f + 1)
                    act.wait_ge(s["pre_q"], f + 1)
                    act.activation(ex[:, :, :], pre[:, :, :], ACT.Exp, scale=-1.0).then_inc(s["e_done"], 1)
                    act.wait_ge(s["e_done"], f + 1)
                    after(act, s["cum_done"], f)
                    act.activation(lp[:, :, :], ex[:, :, :], ACT.Ln, bias=m.one[:, :]).then_inc(s["l_done"], 1)
                    act.wait_ge(s["l_done"], f + 1)
                    after(act, s["k_done"], f)
                    after(act, s["q_done"], f)
                    act.activation(sg[:, :, :], lp[:, :, :], ACT.Exp, scale=-1.0).then_inc(s["f_done"], 1)
                if there(g - 2, N):
                    act.wait_ge(s["x1T_ps"], g - 1)
                    act.activation(m.x1T[:, :, bass.ds((g - 2) * GT, GT)], v_bank[:, 0:W].rearrange("p (k n) -> p k n", k=KE), ACT.Copy).then_inc(s["x1T_sb"], 1)
                if there(n, N):
                    act.wait_ge(s["g1_ps"], n + 1)
                    after(act, s["gate_ps"], n)
                    act.activation(g1[:, :], g1_bank[:, 0:GT], ACT.Copy).then_inc(s["g1_sb"], 1)
                    act.wait_ge(s["v_ps"], n + 1)
                    after(act, s["o_ps"], n - 1)
                    act.activation(vv[nk][:, :], v_bank[0:S, :], ACT.Copy).then_inc(s["v_sb"], 1)
                if there(g - 1, N):
                    act.wait_ge(s["onT_ps"], g)
                    after(act, s["att_ps"], g - 1)
                    act.activation(onT[:, :, :], g1_bank[:, 0:W].rearrange("p (k n) -> p k n", k=KE), ACT.Copy).then_inc(s["onT_sb"], 1)
                if there(n, N):
                    act.wait_ge(s["gpre_done"], n + 1)
                    act.activation(gex[:, :], gpre[:, :], ACT.Exp, scale=-1.0).then_inc(s["gex_done"], 1)
                    act.wait_ge(s["gex_done"], n + 1)
                    act.activation(gex[:, :], gex[:, :], ACT.Ln, bias=m.one[0:S, :]).then_inc(s["glog_done"], 1)
                    act.wait_ge(s["glog_done"], n + 1)
                    after(act, s["og_done"], n - 1)
                    act.activation(gate[nk][:, :], gex[:, :], ACT.Exp, scale=-1.0).then_inc(s["gate_done"], 1)
                if there(f, N):
                    act.wait_ge(s["dist_done"], f + 1)
                    after(act, s["hats_done"], f)
                    act.activation(dec[:, 0:LEVELS, :, :], dist[:, :, :, :], ACT.Exp, scale=-1.0)
                    act.activation(dec[:, LEVELS, :, :], dist[:, LEVELS - 1, :, :], ACT.Exp).then_inc(s["dec_done"], 1)
            steps(act, -2, 4, N - 2, N + 2, step)

        @block.gpsimd
        def _(pool):
            pool.wait_ge(s["zeroed"], 1)

            def step(g, half, k):
                n, nk = g + 1, 1 - k
                f = g + 2
                if there(f, N):
                    after(pool, s["hats_done"], f)
                    pool.wait_ge(s["f_done"], f + 1)
                    apart(pool, m)
                    pool.tensor_scalar(kk[:, :, :].rearrange("p g s -> p (g s)"), sg[:, 0, :], -1.0, 1.0, ALU.mult, ALU.add).then_inc(s["k_done"], 1)
                if there(g - 2, N):
                    pool.wait_ge(s["x1_done"], g - 1)
                    pool.tensor_tensor(m.xres[:, bass.ds((g - 2) * 2, 2), :], x1[k][:, :, :], m.bo_rows[:, :, :], ALU.add).then_inc(s["x1_kept"], 1)
                if there(f, N):
                    pool.wait_ge(s["dec_done"], f + 1)
                    pool.wait_ge(s["k_done"], f + 1)
                    pool.wait_ge(s["q_done"], f + 1)
                    after(pool, s["a_ps"], (f - 1) * LEVELS)
                    for l in range(LEVELS - 1):
                        for run in LEFT[l]:
                            pool.tensor_tensor(blocks(kh[k][:, l], run), blocks(kk, run), blocks(dec[:, l], run), ALU.mult)
                        for run in RIGHT[l]:
                            pool.tensor_tensor(blocks(qh[k][:, l], run), blocks(qq, run), blocks(dec[:, l], run), ALU.mult)
                    pool.tensor_tensor(qh[k][:, LEVELS - 1], qq[:, :, :], dec[:, LEVELS - 1], ALU.mult)
                    pool.tensor_tensor(kh[k][:, LEVELS - 1], kk[:, :, :], dec[:, LEVELS], ALU.mult).then_inc(s["hats_done"], 1)
            steps(pool, -2, 2, N - 2, N + 2, step)


K_PART = [0, 0, 1, 1, 0, 2]
Q_PART = [0, 1, 0, 1, 2, 0]
TERMS = len(K_PART)
SHIFT_ROW = TERMS * DK
CHUNK = [0, 128, SC - 128]
CHUNKS = len(CHUNK)
UNITS = NH // 4
SLOTS = UNITS * CHUNKS
VW = DK + 1
PIECES = 6
PAIRS = B // 2


def attention_phase(nc, m, ctx, io):
    def sb(name, shape, dt=F32):
        return ctx.enter_context(nc.sbuf_tensor(name, shape, dt))

    def sem(name):
        return ctx.enter_context(nc.semaphore("a_" + name))

    W = 4 * S
    wk = sb("wk", [C, E])
    wv = sb("wv", [C, E])
    wq = sb("wq", [128, KE, E])
    wo = sb("wo", [128, UNITS, E])
    sel = sb("sel", [128, 128])
    vmask = sb("vmask", [128, CHUNKS])
    bk = sb("bk", [128, KE])
    bq = sb("bq", [128, KE])
    bqs = sb("bqs", [128, KE])
    idb = sb("idb", [128, 128], BF16)
    ctxK = sb("ctxK", [C, 2 * SC])
    ctxV = sb("ctxV", [C, 2 * SC])
    kf = sb("kf", [128, KE, 2 * SC])
    kr = sb("kr", [128, KE, 2 * SC])
    kp = sb("kp", [128, 3, KE, 2 * SC], BF16)
    qf = sb("qf", [128, KE, GT])
    qr = sb("qr", [128, KE, GT])
    qp = sb("qp", [128, 3, KE, GT], BF16)
    KS = [sb(f"KS{k}", [SHIFT_ROW + 1, NH, 2 * SC], BF16) for k in range(2)]
    QS = [sb(f"QS{k}", [SHIFT_ROW + 1, NH, GT], BF16) for k in range(2)]
    V = [sb(f"V{k}", [128, 2, CHUNKS, NH, VW]) for k in range(2)]
    RING = 4
    EARLY = 2
    LAG = 2
    PT = [sb(f"PT{k}", [128, W]) for k in range(RING)]
    nm = sb("nm", [S, NH], BF16)
    mT = sb("mT", [NH, S], BF16)
    aT = sb("aT", [128, W])
    lz = sb("lz", [128, W])
    rz = sb("rz", [128, W])
    aN = sb("aN", [128, W])
    r2 = sb("r2", [S, E])
    x2 = [sb(f"x2{k}", [S, E]) for k in range(2)]
    st = sb("st_a", [S, 6])
    mv = sb("mv_a", [S, 2])
    lnv = sb("lnv_a", [S, 1])
    rstd = sb("rstd_a", [S, 1])
    kscr = nc.dram_tensor("k_parts", (PAIRS, 3, KE, 128, 2 * SC), BF16, kind="Internal").ap()
    qscr = nc.dram_tensor("q_parts", (PAIRS, 3, KE, 128, GT), BF16, kind="Internal").ap()

    names = ("w_here ready bq_scaled ctxK_in ctxV_in k_ps q_ps v_ps k_sb q_sb v_sb k_rest k2 k3 q_rest q2 q3 "
             "kscr_in qscr_in stack_in max_ps max_done mT_ps mT_sb st_ps pt_done pv_ps aT_done zb_ps lz_done rz_done "
             "aN_done wo_ps r2_done st_done mv_done lnv_done rstd_done x2_done x2T_ps x2T_sb x2_kept").split()
    s = {n: sem(n) for n in names}
    mrow_in = [sem(f"mrow_in{j}") for j in range(2)]
    lt_out = [sem(f"lt_out{j}") for j in range(2)]
    st_bank, mx_bank, pv_bank, pj_bank, misc = m.bank[0:2], m.bank[2:4], m.bank[4], m.bank[5:7], m.bank[7]
    N = PAIRS
    NW = 8 * 16

    def pieces(p, j):
        if j == 0:
            todo = [("k", p + 2, (t, b), t * 2 + b) for t in range(KE) for b in range(2)] + [("q", p + 2, t, t) for t in range(KE)]
        else:
            todo = [("v", p + 1, (b, c), b * CHUNKS + c) for b in range(2) for c in range(CHUNKS)]
        return {2 * i: x + ((i % 2),) for i, x in enumerate(todo)}

    COUNT = {"k": 4, "q": 2, "v": 6}

    def maxima(b, j, slot, k):
        if slot < NH // 2 - EARLY:
            return (b + 1, 1 - j, k if j == 0 else 1 - k, 2 * (slot + EARLY))
        if slot >= SLOTS - EARLY:
            return (b + 2, j, 1 - k, 2 * (slot - SLOTS + EARLY))
        return (B, None, None, None)

    with nc.Block() as block:
        @block.sync
        def _(sp):
            for dst, src in ((wk[:, :], io["Wk"]), (wv[:, :], io["Wv"]), (wq[:, :, :], io["Wq"].rearrange("(k p) n -> p k n", p=128)),
                             (wo[:, :, :], io["Wo_units"]), (sel[:, :], io["c_sel"]), (vmask[:, :], io["c_vmask"]),
                             (bk[:, :], io["bk"]), (bq[:, :], io["bq"])):
                sp.dma_start(dst, src).then_inc(s["w_here"], 16)

            def step(p, half, k):
                nk = 1 - k
                def keep_tokens(b, j):
                    if there(b, B):
                        sp.wait_ge(s["x2_done"], b + 1)
                        for part in range(2):
                            first = 1 + 2 * LR * part
                            apart(sp, m)
                            sp.dma_start(m.lt[part, bass.ds(b, 1)].rearrange("a t e -> t (a e)"), x2[j][first:first + 2 * LR:2, :]).then_inc(lt_out[j], 16)

                if there(p + 1, N):
                    after(sp, s["v_ps"], (p + 1) * 6)
                    apart(sp, m)
                    sp.dma_start(ctxV[:, :], io["ctxT"][:, bass.ds((p + 1) * 2 * SC, 2 * SC)]).then_inc(s["ctxV_in"], 16)
                    after(sp, s["st_ps"], p * 2 * SLOTS)
                    apart(sp, m)
                    sp.wait_ge(s["kscr_in"], (p + 2) * 32)
                    apart(sp, m)
                    sp.wait_ge(s["qscr_in"], (p + 2) * 16)
                    for t in range(TERMS):
                        rows = slice(t * DK, (t + 1) * DK)
                        apart(sp, m)
                        sp.dma_start(KS[nk][rows, :, :], kscr[bass.ds(p + 1, 1), K_PART[t]].rearrange("a t (h d) n -> d (a t h) n", d=DK)).then_inc(s["stack_in"], 16)
                        apart(sp, m)
                        sp.dma_start(QS[nk][rows, :, :], qscr[bass.ds(p + 1, 1), Q_PART[t]].rearrange("a t (h d) n -> d (a t h) n", d=DK)).then_inc(s["stack_in"], 16)
                keep_tokens(p * 2 - 1, 1)
                if there(p + 2, N):
                    for t in range(KE):
                        sp.wait_ge(s["k3"], (p + 2) * 2 + t + 1)
                        apart(sp, m)
                        sp.dma_start(kscr[bass.ds(p + 2, 1), :, t].rearrange("a c p n -> p (a c) n"), kp[:, :, t, :]).then_inc(s["kscr_in"], 16)
                    sp.wait_ge(s["q3"], p + 3)
                    apart(sp, m)
                    sp.dma_start(qscr[bass.ds(p + 2, 1)].rearrange("a c t p n -> p (a c t) n"), qp[:, :, :, :].rearrange("p c t n -> p (c t) n")).then_inc(s["qscr_in"], 16)
                keep_tokens(p * 2, 0)
            steps(sp, -2, 2, N - 2, N + 1, step)
            for k in range(2):
                sp.wait_ge(lt_out[k], (B // 2) * 32)

        @block.tensor
        def _(pe):
            pe.wait_ge(s["w_here"], NW)
            pe.wait_ge(s["ready"], 1)

            def project(kind, q, args, i, turn, prior_sem, prior_value):
                pj = pj_bank[turn]
                after(pe, prior_sem, prior_value)
                if kind == "k":
                    t, b = args
                    pe.wait_ge(s["ctxK_in"], (q + 1) * 16)
                    pe.matmul(pj[:, 0:SC], wk[:, t * 128:(t + 1) * 128], ctxK[:, b * SC:(b + 1) * SC], start=True, stop=True).then_inc(s["k_ps"], 1)
                elif kind == "q":
                    for e in range(KE):
                        mm = pe.matmul(pj[:, 0:GT], wq[:, e, args * 128:(args + 1) * 128], m.x1T[:, e, bass.ds(q * GT, GT)], start=(e == 0), stop=(e == KE - 1))
                    mm.then_inc(s["q_ps"], 1)
                else:
                    b, c = args
                    pe.wait_ge(s["ctxV_in"], (q + 1) * 16)
                    pe.matmul(pj[:, 0:E], ctxV[:, b * SC + CHUNK[c]:b * SC + CHUNK[c] + 128], wv[:, :], start=True, stop=True).then_inc(s["v_ps"], 1)

            def weigh(b, k, j, slot):
                u, c = slot // CHUNKS, slot % CHUNKS
                n = b * SLOTS + slot
                pe.wait_ge(s["pt_done"], n + 1)
                if slot == 0:
                    pe.wait_ge(s["v_sb"], (b + 1) * 3)
                    after(pe, s["aT_done"], b)
                for i in range(4):
                    mm = pe.matmul(pv_bank[32 * i:32 * i + VW, u * S:(u + 1) * S], V[k][:, j, c, u * 4 + i, :], PT[(j * SLOTS + slot) % RING][:, i * S:(i + 1) * S],
                                   start=(c == 0), stop=(c == CHUNKS - 1), skip_group_check=True)
                mm.then_inc(s["pv_ps"], 1)

            def step(p, half, k):
                nk = 1 - k
                for j in range(2):
                    b = p * 2 + j
                    work = pieces(p, j)
                    for slot in range(SLOTS):
                        if there(b, B):
                            n = b * SLOTS + slot
                            if slot == 0:
                                pe.wait_ge(mrow_in[j], (p + 1) * 16)
                            after(pe, s["pt_done"], n - 1)
                            u, c = slot // CHUNKS, slot % CHUNKS
                            for i in range(4):
                                at = j * SC + CHUNK[c]
                                mm = pe.matmul(st_bank[slot % 2][:, i * S:(i + 1) * S], KS[k][:, u * 4 + i, at:at + 128],
                                               QS[k][:, u * 4 + i, j * S:(j + 1) * S], start=True, stop=True)
                            mm.then_inc(s["st_ps"], 1)
                        if there(b - 1, B) and slot < LAG:
                            weigh(b - 1, k if j else nk, 1 - j, SLOTS - LAG + slot)
                        elif there(b, B) and slot >= LAG:
                            weigh(b, k, j, slot - LAG)
                        a, jj, kk, first = maxima(b, j, slot, k)
                        if there(a, B):
                            if jj == 0 and first == 0:
                                pe.wait_ge(s["stack_in"], (p + 2) * TERMS * 2 * 16)
                            for h in (first, first + 1):
                                after(pe, s["max_done"], a * NH + h - 1)
                                pe.matmul(mx_bank[h % 2][0:S, 0:SC], QS[kk][0:SHIFT_ROW, h, jj * S:(jj + 1) * S],
                                          KS[kk][0:SHIFT_ROW, h, jj * SC:(jj + 1) * SC], start=True, stop=True).then_inc(s["max_ps"], 1)
                        if slot in work and there(work[slot][1], N):
                            kind, q, args, i, turn = work[slot]
                            project(kind, q, args, i, turn, *last_piece(p, j, slot))
                        if there(b - 2, B) and slot == 0:
                            pe.wait_ge(s["x2_done"], b - 1)
                            after(pe, s["mT_sb"], b + 1 if there(b, B) else B)
                            for e in range(KE):
                                mm = pe.transpose(misc[:, e * S:(e + 1) * S], x2[j][:, e * 128:(e + 1) * 128], m.ident[0:S, 0:S])
                            mm.then_inc(s["x2T_ps"], 1)
                        if there(b - 1, B):
                            if slot == 2:
                                pe.wait_ge(s["aT_done"], b)
                                after(pe, s["x2T_sb"], b - 1)
                                pe.matmul(misc[:, 0:W], sel[:, :], aT[:, :], start=True, stop=True).then_inc(s["zb_ps"], 1)
                            if slot == 6:
                                pe.wait_ge(s["aN_done"], b)
                                pe.wait_ge(s["lz_done"], b)
                                for u in range(UNITS):
                                    mm = pe.matmul(misc[0:S, 0:E], aN[:, u * S:(u + 1) * S], wo[:, u, :], start=(u == 0), stop=(u == UNITS - 1))
                                mm.then_inc(s["wo_ps"], 1)
                        if there(b + 1, B) and slot == 8:
                            pe.wait_ge(s["max_done"], (b + 1) * NH + NH)
                            after(pe, s["r2_done"], b if there(b, B) else 0)
                            pe.transpose(misc[0:NH, 0:S // 2].bitcast(BF16), nm[:, :], idb[0:S, 0:S]).then_inc(s["mT_ps"], 1)
            def last_piece(p, j, slot):
                i = slot // 2
                if j == 0:
                    if isinstance(p, int) and p == -1 and i < 2:
                        return s["q_sb"], i + 1
                    if i < 2:
                        return s["v_sb"], (p + 1) * 6 - 1 + i
                    if i < 4:
                        return s["k_sb"], (p + 2) * 4 + i - 1
                    return s["k_sb"], (p + 2) * 4 + i - 1
                if i < 2:
                    return s["q_sb"], (min(p + 2, N - 1) if isinstance(p, int) else p + 2) * 2 + i + 1
                return s["v_sb"], (p + 1) * 6 + i - 1
            steps(pe, -2, 2, N - 2, N + 1, step)

        @block.vector
        def _(dve):
            dve.wait_ge(s["w_here"], NW)
            dve.memset(pv_bank[:, :], 0.0)
            dve.tensor_copy(idb[:, :], m.ident[:, :])
            for k in range(2):
                dve.memset(KS[k][SHIFT_ROW:SHIFT_ROW + 1, :, :], 1.0)
                for j in range(2):
                    for c in range(CHUNKS):
                        dve.tensor_copy(V[k][:, j, c, :, DK:DK + 1], vmask[:, c:c + 1].to_broadcast([128, NH, 1]))
            dve.tensor_scalar(bqs[:, :], bq[:, :], DK ** -0.5, None, ALU.mult).then_inc(s["ready"], 1)
            def step(p, half, k):
                for j in range(2):
                    b = p * 2 + j
                    for slot in range(SLOTS):
                        a, _, _, first = maxima(b, j, slot, k)
                        if there(a, B):
                            for h in (first, first + 1):
                                dve.wait_ge(s["max_ps"], a * NH + h + 1)
                                if h == 0:
                                    after(dve, s["mT_ps"], a)
                                dve.tensor_reduce(nm[:, h:h + 1], mx_bank[h % 2][0:S, 0:SC], AX.X, ALU.max, negate=True).then_inc(s["max_done"], 1)
                        if there(p + 2, N):
                            q = p + 2
                            for t in range(KE):
                                if j == 0 and slot == (7, 11)[t]:
                                    dve.wait_ge(s["k_rest"], q * 2 + t + 1)
                                    dve.tensor_copy(kp[:, 1, t, :], kr[:, t, :]).then_inc(s["k2"], 1)
                            if j == 1 and slot == 4:
                                dve.wait_ge(s["q_rest"], q + 1)
                                dve.tensor_copy(qp[:, 1], qr[:, :, :]).then_inc(s["q2"], 1)
                        if there(b - 1, B):
                            if slot == 5:
                                dve.wait_ge(s["rz_done"], b)
                                after(dve, s["wo_ps"], b - 1)
                                dve.tensor_tensor(aN[:, :], aT[:, :], rz[:, :], ALU.mult).then_inc(s["aN_done"], 1)
                            if slot == 7:
                                dve.wait_ge(s["wo_ps"], b)
                                dve.tensor_tensor(r2[:, :], misc[0:S, 0:E], m.xres[:, bass.ds(b - 1, 1), :].rearrange("p a e -> p (a e)"), ALU.add).then_inc(s["r2_done"], 1)
                                dve.wait_ge(s["r2_done"], b)
                                dve.bn_stats(st[:, :], r2[:, :]).then_inc(s["st_done"], 1)
                                dve.wait_ge(s["st_done"], b)
                                apart(dve, m)
                                dve.bn_aggr(mv[:, :], st[:, :]).then_inc(s["mv_done"], 1)
                            if slot == 10:
                                dve.wait_ge(s["rstd_done"], b)
                                after(dve, s["x2T_ps"], b - 2)
                                after(dve, s["x2_kept"], b - 2)
                                if there(b - 3, B):
                                    dve.wait_ge(lt_out[1 - j], ((b - 1) // 2 if isinstance(b, int) else p + j - 1) * 32)
                                dve.tensor_scalar(x2[1 - j][:, :], r2[:, :], mv[:, 0:1], rstd[:, 0:1], ALU.subtract, ALU.mult).then_inc(s["x2_done"], 1)
            steps(dve, -2, 2, N - 2, N + 1, step)

        @block.scalar
        def _(act):
            act.preload_act_table_set(LOG_EXP)
            act.wait_ge(s["w_here"], NW)
            act.wait_ge(s["ready"], 1)
            act.dma_start(ctxK[:, :], io["ctxT"][:, 0:2 * SC]).then_inc(s["ctxK_in"], 16)

            def step(p, half, k):
                nk = 1 - k
                for j in range(2):
                    b = p * 2 + j
                    work = pieces(p, j)
                    for slot in range(SLOTS):
                        if there(p + 3, N) and j == 1 and slot == 0:
                            act.wait_ge(s["k_ps"], (p + 3) * 4)
                            act.dma_start(ctxK[:, :], io["ctxT"][:, bass.ds((p + 3) * 2 * SC, 2 * SC)]).then_inc(s["ctxK_in"], 16)
                        if there(b, B):
                            n = b * SLOTS + slot
                            act.wait_ge(s["st_ps"], n + 1)
                            after(act, s["pv_ps"], n + 1 - RING)
                            act.activation(PT[(j * SLOTS + slot) % RING][:, :], st_bank[slot % 2][:, 0:W], ACT.Exp).then_inc(s["pt_done"], 1)
                        if there(b - 1, B):
                            if slot == LAG - 1:
                                act.wait_ge(s["pv_ps"], b * SLOTS)
                                after(act, s["aN_done"], b - 1)
                                act.activation(aT[:, :], pv_bank[:, 0:W], ACT.Copy).then_inc(s["aT_done"], 1)
                            if slot == 3:
                                act.wait_ge(s["zb_ps"], b)
                                act.activation(lz[:, :], misc[:, 0:W], ACT.Ln).then_inc(s["lz_done"], 1)
                                act.wait_ge(s["lz_done"], b)
                                after(act, s["aN_done"], b - 1)
                                act.activation(rz[:, :], lz[:, :], ACT.Exp, scale=-1.0).then_inc(s["rz_done"], 1)
                            if slot == 9:
                                act.wait_ge(s["mv_done"], b)
                                act.activation(lnv[:, :], mv[:, 1:2], ACT.Ln, bias=m.eps[0:S, :]).then_inc(s["lnv_done"], 1)
                                act.wait_ge(s["lnv_done"], b)
                                after(act, s["x2_done"], b - 1)
                                act.activation(rstd[:, :], lnv[:, :], ACT.Exp, scale=-0.5).then_inc(s["rstd_done"], 1)
                        if there(b + 1, B) and slot == 9:
                            jj, kk = (1, k) if j == 0 else (0, nk)
                            act.wait_ge(s["mT_ps"], b + 2)
                            if there(b, B):
                                act.wait_ge(mrow_in[1 - jj], (p + 1) * 16)
                            act.activation(mT[:, :], misc[0:NH, 0:S // 2].bitcast(BF16), ACT.Copy).then_inc(s["mT_sb"], 1)
                            act.wait_ge(s["mT_sb"], b + 2)
                            act.dma_start(QS[kk][SHIFT_ROW:SHIFT_ROW + 1, :, jj * S:(jj + 1) * S], mT[:, :]).then_inc(mrow_in[jj], 16)
                        if there(b - 2, B) and slot == 1:
                            act.wait_ge(s["x2T_ps"], b - 1)
                            act.activation(m.x1T[:, :, bass.ds((b - 2) * S, S)], misc[:, 0:2 * S].rearrange("p (k n) -> p k n", k=KE), ACT.Copy).then_inc(s["x2T_sb"], 1)
                        if slot - 1 in work and there(work[slot - 1][1], N):
                            kind, q, args, i, turn = work[slot - 1]
                            act.wait_ge(s[kind + "_ps"], q * COUNT[kind] + i + 1)
                            pj = pj_bank[turn]
                            if kind == "k":
                                t, bb = args
                                after(act, s["k3"], q * 2 - 1 + t)
                                after(act, s["kscr_in"], q * 32)
                                act.activation(kf[:, t, bb * SC:(bb + 1) * SC], pj[:, 0:SC], ACT.Identity, bias=bk[:, t:t + 1])
                                act.activation(kp[:, 0, t, bb * SC:(bb + 1) * SC], pj[:, 0:SC], ACT.Identity, bias=bk[:, t:t + 1]).then_inc(s["k_sb"], 1)
                            elif kind == "q":
                                after(act, s["q3"], q)
                                after(act, s["qscr_in"], q * 16)
                                act.activation(qf[:, args, :], pj[:, 0:GT], ACT.Identity, bias=bqs[:, args:args + 1], scale=DK ** -0.5)
                                act.activation(qp[:, 0, args, :], pj[:, 0:GT], ACT.Identity, bias=bqs[:, args:args + 1], scale=DK ** -0.5).then_inc(s["q_sb"], 1)
                            else:
                                bb, c = args
                                after(act, s["pv_ps"], (q - 1) * 2 * SLOTS)
                                act.activation(V[nk][:, bb, c, :, 0:DK], pj[:, 0:E].rearrange("p (h d) -> p h d", h=NH), ACT.Identity, scale=vmask[:, c:c + 1]).then_inc(s["v_sb"], 1)
            steps(act, -2, 2, N - 4, N + 1, step)

        @block.gpsimd
        def _(pool):
            def step(p, half, k):
                if there(p + 2, N):
                    q = p + 2
                    for t in range(KE):
                        pool.wait_ge(s["k_sb"], q * 4 + 2 * t + 2)
                        pool.tensor_tensor(kr[:, t, :], kf[:, t, :], kp[:, 0, t, :], ALU.subtract).then_inc(s["k_rest"], 1)
                        pool.wait_ge(s["k2"], q * 2 + t + 1)
                        pool.tensor_tensor(kp[:, 2, t, :], kr[:, t, :], kp[:, 1, t, :], ALU.subtract).then_inc(s["k3"], 1)
                    pool.wait_ge(s["q_sb"], q * 2 + 2)
                    pool.tensor_tensor(qr[:, :, :], qf[:, :, :], qp[:, 0], ALU.subtract).then_inc(s["q_rest"], 1)
                    pool.wait_ge(s["q2"], q + 1)
                    pool.tensor_tensor(qp[:, 2], qr[:, :, :], qp[:, 1], ALU.subtract).then_inc(s["q3"], 1)
                for j in range(2):
                    b = p * 2 + j - 1
                    if there(b, B):
                        pool.wait_ge(s["x2_done"], b + 1)
                        pool.tensor_tensor(m.xres[:, bass.ds(b, 1), :].rearrange("p a e -> p (a e)"), x2[1 - j][:, :], m.b2_rows[:, :], ALU.add).then_inc(s["x2_kept"], 1)
            steps(pool, -2, 2, N - 2, N + 1, step)


FB = 4
FT = FB * S
FGROUPS = B // FB
LR = 4
TILES = HID // 128


def ffn_phase(nc, m, ctx, io):
    def sb(name, shape, dt=F32):
        return ctx.enter_context(nc.sbuf_tensor(name, shape, dt))

    def sem(name):
        return ctx.enter_context(nc.semaphore("f_" + name))

    R = FB * LR
    w1 = sb("w1", [128, KE, HID])
    w2 = sb("w2", [128, TILES, E])
    b1 = sb("b1", [128, TILES])
    scale = sb("scale", [128, 1])
    own_batch = sb("own_batch", [128, FT])
    own_rows = sb("own_rows", [128, LR, E // LR])
    odd1 = sb("odd1", [128, KE, FB, LR])
    odd2 = sb("odd2", [128, KE, FB, LR])
    even1 = sb("even1", [128, LR, E])
    even2 = sb("even2", [128, E])
    spread2 = sb("spread2", [128, LR, E // LR])
    cm = sb("cm", [128, FT])
    tm = sb("tm", [128, FT])
    hT = sb("hT", [128, TILES, FT])
    r3 = sb("r3", [S, FB, E])
    x3 = sb("x3", [S, FB, E])
    st = sb("st_f", [S, FB, 6])
    mv = sb("mv_f", [S, FB, 2])
    lnv = sb("lnv_f", [S, FB])
    rstd = sb("rstd_f", [S, FB])
    names = ("w_here zeroed even1_in even2_in odd1_done odd2_done c_ps cm_done h_ps gelu_done t_ps tm_done spread_done "
             "y_ps r3_done st_done mv_done lnv_done rstd_done x3_done out_done").split()
    s = {n: sem(n) for n in names}
    h_bank = [m.bank[0], m.bank[1], m.bank[6], m.bank[7]]
    c_bank, t_bank, y_bank = m.bank[2], m.bank[3], m.bank[4:6]
    N = FGROUPS
    NW = 6 * 16

    def steps1(eng, step):
        for g in range(-1, 1):
            step(g)
        with eng.Fori(1, N - 1) as g:
            step(g)
        for g in range(N - 1, N + 1):
            step(g)

    with nc.Block() as block:
        @block.sync
        def _(sp):
            for dst, src in ((w1[:, :, :], io["W1T"].rearrange("(k p) n -> p k n", p=128)), (w2[:, :, :], io["W2T"].rearrange("(k p) n -> p k n", p=128)),
                             (b1[:, :], io["b1"]), (scale[:, :], io["scale"]), (own_batch[:, :], io["c_own_batch"]),
                             (own_rows[:, :, :], io["c_own_rows"])):
                sp.dma_start(dst, src).then_inc(s["w_here"], 16)
            sp.wait_ge(s["zeroed"], 1)

            def step(g):
                if there(g + 1, N):
                    n = g + 1
                    after(sp, s["h_ps"], n * TILES)
                    for i in range(LR):
                        apart(sp, m)
                        sp.dma_start(even1[i:R:LR, i, :], m.lt[0, bass.ds(n * FB, FB), i, :]).then_inc(s["even1_in"], 16)
                    after(sp, s["spread_done"], n)
                    for r in range(LR):
                        apart(sp, m)
                        sp.dma_start(even2[32 * r:32 * r + R, :], m.lt[1, bass.ds(n * FB, FB), :, :].rearrange("b i e -> (b i) e")).then_inc(s["even2_in"], 16)
                if there(g - 1, N):
                    sp.wait_ge(s["x3_done"], g)
                    apart(sp, m)
                    sp.dma_start(io["out"][bass.ds((g - 1) * FB, FB), :, :].rearrange("b s e -> s b e"), x3[:, :, :]).then_inc(s["out_done"], 16)
            steps1(sp, step)
            sp.wait_ge(s["out_done"], N * 16)

        @block.tensor
        def _(pe):
            pe.wait_ge(s["w_here"], NW)
            pe.wait_ge(s["zeroed"], 1)

            def step(g):
                if there(g, N):
                    pe.wait_ge(s["cm_done"], g + 1)
                    pe.wait_ge(s["even1_in"], (g + 1) * LR * 16)
                    for t in range(TILES):
                        after(pe, s["gelu_done"], g * TILES + t + 1 - len(h_bank))
                        out = h_bank[t % len(h_bank)][:, 0:FT]
                        for e in range(KE):
                            pe.matmul(out, w1[:, e, t * 128:(t + 1) * 128], m.x1T[:, e, bass.ds(g * FT, FT)], start=(e == 0), stop=False)
                        pe.matmul(out, even1[:, t // 2, (t % 2) * 128:(t % 2 + 1) * 128], cm[:, :], start=False, stop=True).then_inc(s["h_ps"], 1)
                if there(g + 1, N):
                    pe.wait_ge(s["odd1_done"], g + 2)
                    for e in range(KE):
                        mm = pe.matmul(c_bank[0:R, 0:FT], odd1[:, e, :, :].rearrange("p b i -> p (b i)"), m.x1T[:, e, bass.ds((g + 1) * FT, FT)],
                                       start=(e == 0), stop=(e == KE - 1))
                    mm.then_inc(s["c_ps"], 1)
                if there(g, N):
                    pe.wait_ge(s["gelu_done"], (g + 1) * TILES)
                    pe.wait_ge(s["odd2_done"], g + 1)
                    after(pe, s["tm_done"], g)
                    for e in range(KE):
                        for r in range(LR):
                            mm = pe.matmul(t_bank[32 * r:32 * r + R, 0:FT], odd2[:, e, :, :].rearrange("p b i -> p (b i)"), hT[:, 2 * r + e, :],
                                           start=(e == 0), stop=(e == KE - 1), skip_group_check=True)
                    mm.then_inc(s["t_ps"], 1)
                    after(pe, s["r3_done"], 2 * g)
                    for y in range(2):
                        for b in range(2):
                            out = y_bank[y][0:S, b * E:(b + 1) * E]
                            tok = slice((y * 2 + b) * S, (y * 2 + b + 1) * S)
                            for t in range(TILES):
                                pe.matmul(out, hT[:, t, tok], w2[:, t, :], start=(t == 0), stop=False)
                            if y == 0 and b == 0:
                                pe.wait_ge(s["tm_done"], g + 1)
                                pe.wait_ge(s["spread_done"], g + 1)
                            mm = pe.matmul(out, tm[:, tok], spread2[:, :, :].rearrange("p i n -> p (i n)"), start=False, stop=True)
                        mm.then_inc(s["y_ps"], 1)
            steps1(pe, step)

        @block.vector
        def _(dve):
            dve.memset(even1[:, :, :], 0.0)
            dve.memset(even2[:, :], 0.0)
            dve.memset(spread2[:, :, :], 0.0)
            dve.memset(t_bank[:, :], 0.0)
            dve.memset(cm[:, :], 0.0).then_inc(s["zeroed"], 1)
            dve.wait_ge(s["zeroed"], 1)
            dve.wait_ge(s["w_here"], NW)

            def step(g):
                if there(g - 1, N):
                    after(dve, s["x3_done"], g - 1)
                    for y in range(2):
                        dve.wait_ge(s["y_ps"], (g - 1) * 2 + y + 1)
                        dve.tensor_tensor(r3[:, 2 * y:2 * y + 2, :], y_bank[y][0:S, :].rearrange("p (b e) -> p b e", b=2),
                                          m.xres[:, bass.ds((g - 1) * FB + 2 * y, 2), :], ALU.add).then_inc(s["r3_done"], 1)
                    for b in range(FB):
                        dve.wait_ge(s["r3_done"], (g - 1) * 2 + b // 2 + 1)
                        bn = dve.bn_stats(st[:, b, :], r3[:, b, :])
                    bn.then_inc(s["st_done"], 1)
                    dve.wait_ge(s["st_done"], g)
                    apart(dve, m)
                    for b in range(FB):
                        bn = dve.bn_aggr(mv[:, b, :], st[:, b, :])
                    bn.then_inc(s["mv_done"], 1)
                if there(g, N):
                    dve.wait_ge(s["even2_in"], (g + 1) * LR * 16)
                    for r in range(LR):
                        rows = slice(32 * r, 32 * r + R)
                        a = even2[rows, r:E:LR]
                        src = bass.AP(tensor=a.tensor, offset=a.offset, ap=[list(a.ap[0]), [0, LR], list(a.ap[1])])
                        tt = dve.tensor_tensor(spread2[rows, :, :], src, own_rows[rows, :, :], ALU.mult)
                    tt.then_inc(s["spread_done"], 1)
                if there(g + 1, N):
                    dve.wait_ge(s["c_ps"], g + 2)
                    dve.scalar_tensor_tensor(cm[0:R, :], c_bank[0:R, 0:FT], scale[0:R, 0:1], own_batch[0:R, :], ALU.mult, ALU.mult).then_inc(s["cm_done"], 1)
                if there(g, N):
                    dve.wait_ge(s["t_ps"], g + 1)
                    dve.scalar_tensor_tensor(tm[:, :], t_bank[:, 0:FT], scale[:, 0:1], own_batch[:, :], ALU.mult, ALU.mult).then_inc(s["tm_done"], 1)
                if there(g - 1, N):
                    dve.wait_ge(s["rstd_done"], g)
                    after(dve, s["out_done"], (g - 1) * 16)
                    for b in range(FB):
                        ts = dve.tensor_scalar(x3[:, b, :], r3[:, b, :], mv[:, b, 0:1], rstd[:, b:b + 1], ALU.subtract, ALU.mult)
                    ts.then_inc(s["x3_done"], 1)
            steps1(dve, step)

        @block.scalar
        def _(act):
            act.wait_ge(s["w_here"], NW)

            def odd(n, first):
                a = m.x1T[:, :, bass.ds(n * FT, FT)].rearrange("p k (b s) -> p k b s", b=FB)
                return a[:, :, :, first:first + 2 * LR:2]

            def step(g):
                if there(g, N):
                    act.preload_act_table_set(GELU)
                    for t in range(TILES):
                        act.wait_ge(s["h_ps"], g * TILES + t + 1)
                        act.activation(hT[:, t, :], h_bank[t % len(h_bank)][:, 0:FT], ACT.Gelu, bias=b1[:, t:t + 1]).then_inc(s["gelu_done"], 1)
                        if t == 0:
                            after(act, s["t_ps"], g)
                            for e in range(KE):
                                cp = act.activation(odd2[:, e], odd(g, 10)[:, e], ACT.Copy)
                            cp.then_inc(s["odd2_done"], 1)
                            if there(g + 1, N):
                                after(act, s["c_ps"], g + 1)
                                for e in range(KE):
                                    cp = act.activation(odd1[:, e], odd(g + 1, 2)[:, e], ACT.Copy)
                                cp.then_inc(s["odd1_done"], 1)
                elif there(g + 1, N):
                    for e in range(KE):
                        cp = act.activation(odd1[:, e], odd(g + 1, 2)[:, e], ACT.Copy)
                    cp.then_inc(s["odd1_done"], 1)
                if there(g - 1, N):
                    act.preload_act_table_set(LOG_EXP)
                    act.wait_ge(s["mv_done"], g)
                    act.activation(lnv[:, :], mv[:, :, 1], ACT.Ln, bias=m.eps[0:S, :]).then_inc(s["lnv_done"], 1)
                    act.wait_ge(s["lnv_done"], g)
                    after(act, s["x3_done"], g - 1)
                    act.activation(rstd[:, :], lnv[:, :], ACT.Exp, scale=-0.5).then_inc(s["rstd_done"], 1)
            steps1(act, step)


def setup_phase(nc, m, ctx, io):
    def sb(name, shape, dt=F32):
        return ctx.enter_context(nc.sbuf_tensor(name, shape, dt))

    with ExitStack() as own:
        here = own.enter_context(nc.semaphore("s_here"))
        filled = own.enter_context(nc.semaphore("s_filled"))
        spread = own.enter_context(nc.semaphore("s_spread"))
        rows_ps = own.enter_context(nc.semaphore("s_rows_ps"))
        kept = own.enter_context(nc.semaphore("s_kept"))
        m.passed = ctx.enter_context(nc.semaphore("passed"))
        wo = own.enter_context(nc.sbuf_tensor("s_wo", [128, KE, E], F32))
        bv = own.enter_context(nc.sbuf_tensor("s_bv", [128, KE], F32))
        bvs = own.enter_context(nc.sbuf_tensor("s_bvs", [128, KE, S], F32))
        row = own.enter_context(nc.sbuf_tensor("s_row", [1, 2 * E], F32))
        ones = own.enter_context(nc.sbuf_tensor("s_ones", [128, S], F32))
        with nc.Block() as block:
            @block.sync
            def _(sp):
                sp.dma_start(m.ident[:, :], io["c_ident"]).then_inc(here, 16)
                sp.dma_start(wo[:, :, :], io["Wo"].rearrange("(k p) n -> p k n", p=128)).then_inc(here, 16)
                sp.dma_start(bv[:, :], io["bv"]).then_inc(here, 16)
                sp.dma_start(row[0:1, 0:E], io["bo"].rearrange("(a n) -> a n", a=1)).then_inc(here, 16)
                sp.dma_start(row[0:1, E:2 * E], io["b2"].rearrange("(a n) -> a n", a=1)).then_inc(here, 16)

            @block.vector
            def _(dve):
                dve.memset(m.eps[:, :], EPS)
                dve.memset(m.one[:, :], 1.0)
                dve.memset(ones[:, :], 1.0).then_inc(filled, 1)
                dve.wait_ge(filled, 1)
                dve.wait_ge(here, 5 * 16)
                for e in range(KE):
                    ts = dve.tensor_scalar(bvs[:, e, :], ones[:, :], bv[:, e:e + 1], None, ALU.mult)
                ts.then_inc(spread, 1)
                dve.wait_ge(rows_ps, 1)
                for b in range(2):
                    cp = dve.tensor_copy(m.bo_rows[:, b, :], m.bank[0][0:S, 0:E])
                cp.then_inc(kept, 1)
                dve.tensor_copy(m.b2_rows[:, :], m.bank[1][0:S, 0:E]).then_inc(kept, 1)
                dve.wait_ge(kept, 2)

            @block.tensor
            def _(pe):
                pe.wait_ge(spread, 1)
                for e in range(KE):
                    pe.matmul(m.bank[0][0:S, 0:E], bvs[:, e, :], wo[:, e, :], start=(e == 0), stop=False)
                pe.matmul(m.bank[0][0:S, 0:E], ones[0:1, :], row[0:1, 0:E], start=False, stop=True)
                pe.matmul(m.bank[1][0:S, 0:E], ones[0:1, :], row[0:1, E:2 * E], start=True, stop=True).then_inc(rows_ps, 1)


def program(nc, io):
    with ExitStack() as ctx:
        m = Memory()
        m.bank = [ctx.enter_context(nc.psum_tensor(f"bank{i}", [128, 512], F32)) for i in range(8)]
        m.ident = ctx.enter_context(nc.sbuf_tensor("ident", [128, 128], F32))
        m.eps = ctx.enter_context(nc.sbuf_tensor("eps", [128, 1], F32))
        m.one = ctx.enter_context(nc.sbuf_tensor("one", [128, 1], F32))
        m.bo_rows = ctx.enter_context(nc.sbuf_tensor("bo_rows", [S, 2, E], F32))
        m.b2_rows = ctx.enter_context(nc.sbuf_tensor("b2_rows", [S, E], F32))
        m.xres = ctx.enter_context(nc.sbuf_tensor("xres", [S, B, E], F32))
        m.lt = nc.dram_tensor("lora_tokens", (2, B, LR, E), F32, kind="Internal").ap()
        m.x1T = ctx.enter_context(nc.sbuf_tensor("x1T", [128, KE, B * S], F32))
        setup_phase(nc, m, ctx, io)
        with ExitStack() as own:
            gla_phase(nc, m, own, io)
        with ExitStack() as own:
            attention_phase(nc, m, own, io)
        with ExitStack() as own:
            ffn_phase(nc, m, own, io)


def laid_out(inputs):
    a = {k: np.asarray(v) for k, v in inputs.items()}
    out = {
        "x": a["x"],
        "xT": a["x"].reshape(B * S, KE, 128).transpose(1, 2, 0),
        "W_inT": a["L0_attn_W_in"].T, "W_outT": a["L0_attn_W_out"].T,
        "W_g1T": a["L0_attn_W_g1"].T, "W_g2T": a["L0_attn_W_g2"].T, "ln_w": a["L0_attn_ln_w"].reshape(KE, 128).T,
        "Wo": a["L0_xattn_Wo"], "bv": a["L0_xattn_bv"].reshape(KE, 128).T, "bo": a["L0_xattn_bo"], "b2": a["L0_ffn_b2"],
    }
    wo = np.zeros((4, 32, UNITS, E), np.float32)
    wo[:, 0:DK] = a["L0_xattn_Wo"].reshape(UNITS, 4, DK, E).transpose(1, 2, 0, 3)
    out.update({
        "W1T": a["L0_ffn_W1"].T, "W2T": a["L0_ffn_W2"].T, "b1": a["L0_ffn_b1"].reshape(TILES, 128).T,
        "scale": np.broadcast_to(a["L0_ffn_scale"], (128, 1)),
        "ctxT": a["ctx_512"].reshape(B * SC, C).T, "Wk": a["L0_xattn_Wk"], "Wv": a["L0_xattn_Wv"], "Wq": a["L0_xattn_Wq"],
        "Wo_units": wo.reshape(128, UNITS, E), "bk": a["L0_xattn_bk"].reshape(KE, 128).T, "bq": a["L0_xattn_bq"].reshape(KE, 128).T,
    })
    out.update(constants())
    return {k: np.ascontiguousarray(v) for k, v in out.items()}


def kernel(**inputs):
    import concourse.bacc as bacc
    from concourse.bass_utils import run_bass_kernel_spmd

    nc = bacc.Bacc("TRN2", target_bir_lowering=False, num_devices=1)
    arrays = laid_out(inputs)
    io = {k: nc.dram_tensor("in_" + k, v.shape, mybir.dt.from_np(v.dtype), kind="ExternalInput").ap() for k, v in arrays.items()}
    io["out"] = nc.dram_tensor("out", (B, S, E), F32, kind="ExternalOutput").ap()
    program(nc, io)
    r = run_bass_kernel_spmd(nc, [{"in_" + k: v for k, v in arrays.items()}], core_ids=[0])
    return r.results[0]["out"]
```

```python
import numpy as np
import concourse.bass as bass
from concourse import mybir
from contextlib import ExitStack

F32 = mybir.dt.float32
BF16 = mybir.dt.bfloat16
F32R = mybir.dt.float32r
I32 = mybir.dt.int32
ALU = mybir.AluOpType
ACT = mybir.ActivationFunctionType
AX = mybir.AxisListType

B, S, E = 32, 112, 256
D = 128
H = E // D
KE = E // 128
SC, C = 375, 128
NH, DK = 16, 16
HID = 1024
EPS = 1e-5
GELU = "gelu_and_others"
LOG_EXP = "natural_log_exp_and_others"

LEFT = [[(0, 1, 112, 64, 63)], [(0, 2, 64, 32, 31)], [(0, 3, 32, 16, 15)], [(0, 7, 16, 8, 7)]]
RIGHT = [[(64, 1, 112, 48, 63)], [(32, 2, 64, 16, 31), (48, 1, 112, 16, 31)], [(16, 3, 32, 16, 15)], [(8, 7, 16, 8, 7)]]
BASE = 8
BASE_CUT = 3
LEVELS = len(LEFT) + 1
LOG_MAX = 20.0
GATE_MAX = 40.0
SEG = 4
GT = 2 * S
GROUPS = B // 2


def tokens_of(run):
    first, blocks, stride, length, _ = run
    return [first + n * stride + i for n in range(blocks) for i in range(length)]


def constants():
    f = np.float32
    ident = np.eye(128, dtype=f)
    mask = np.zeros((S, LEVELS, S), np.int32)
    for n in range(LEVELS - 1):
        for l in LEFT[n]:
            for r in RIGHT[n]:
                for lb in range(l[1]):
                    for rb in range(r[1]):
                        if lb == rb:
                            s0, t0 = l[0] + lb * l[2], r[0] + rb * r[2]
                            mask[s0:s0 + l[3], n, t0:t0 + r[3]] = 1
    s, t = np.arange(S)[:, None], np.arange(S)[None, :]
    mask[:, LEVELS - 1, :] = (s // BASE == t // BASE) & (s <= t)
    assert (mask.sum(1) == (s <= t)).all()
    masks = np.repeat(mask[:, :, None, :], SEG, axis=2).reshape(S, LEVELS * SEG * S)
    keep = np.ones((128, SEG, S), f)
    keep[:, :, 0] = 0
    sel = np.zeros((128, 128), f)
    for i in range(4):
        sel[32 * i + DK, 32 * i:32 * i + 32] = 1
    vmask = np.ones((128, CHUNKS), f)
    vmask[0:CHUNK[1] + 128 - CHUNK[2], 2] = 0
    row = np.arange(128)
    batch_of = np.where(row % 32 < FB * LR, row % 32 // LR, -1)
    own_batch = (batch_of[:, None] == np.arange(FT)[None, :] // S).astype(f)
    own_rows = np.repeat((row[:, None] % LR == np.arange(LR)[None, :]).astype(f)[:, :, None], E // LR, axis=2)
    return {"c_own_batch": own_batch, "c_own_rows": own_rows, "c_sel": sel, "c_vmask": vmask, "c_ident": ident, "c_masks": np.ascontiguousarray(masks), "c_keep": keep.reshape(128, SEG * S)}


def after(eng, sem, value):
    if not isinstance(value, int) or value > 0:
        eng.wait_ge(sem, value)


def apart(eng, m):
    eng.sem_inc(m.passed, 1)


def there(g, n):
    return not isinstance(g, int) or 0 <= g < n


def steps(eng, first, lo, hi, last, step):
    for g in range(first, lo):
        step(g, g // 2, g % 2)
    with eng.Fori(0, (hi - lo) // 2) as i:
        for k in range(2):
            step(i * 2 + (lo + k), i + lo // 2, k)
    for g in range(hi, last):
        step(g, g // 2, g % 2)


def blocks(seg, run):
    first, n, stride, length, _ = run
    a = seg[:, :, first:first + length]
    return bass.AP(tensor=a.tensor, offset=a.offset, ap=[list(a.ap[0]), list(a.ap[1]), [stride, n], list(a.ap[2])])


def cuts(seg, run):
    _, n, stride, length, cut = run
    a = seg[:, :, cut:cut + 1]
    return bass.AP(tensor=a.tensor, offset=a.offset, ap=[list(a.ap[0]), list(a.ap[1]), [stride, n], [0, length]])




class Memory:
    pass


def high(eng, out, a):
    return eng.tensor_copy(out, a)


def product(pe, out, a, b, start, stop):
    for i, (x, y) in enumerate(((0, 0), (1, 0), (0, 1))):
        mm = pe.matmul(out, a[x], b[y], start=start and i == 0, stop=stop and i == 2)
    return mm


def gla_phase(nc, m, ctx, io):
    def sb(name, shape, dt=F32):
        return ctx.enter_context(nc.sbuf_tensor(name, shape, dt))

    def sem(name):
        return ctx.enter_context(nc.semaphore(name))

    W = SEG * S
    w_in = m.w_in
    w_out = sb("w_out", [128, KE, E])
    w_g1 = sb("w_g1", [128, KE, D])
    w_g2 = sb("w_g2", [128, E])
    ln_w = sb("ln_w", [128, KE])
    masks = sb("masks", [S, LEVELS, W], I32)
    keep = sb("keep", [128, W])
    w_inp = [sb(f"w_inp{i}", [128, KE, 3 * E], F32R) for i in range(2)]
    w_g1p = [sb(f"w_g1p{i}", [128, KE, D], F32R) for i in range(2)]
    xT = [sb(f"xT{k}", [128, KE, GT]) for k in range(2)]
    xp = [[sb(f"xp{k}{i}", [128, KE, GT], F32R) for i in range(2)] for k in range(2)]
    xr = [sb(f"xr{k}", [S, 2, E]) for k in range(2)]
    pre = sb("pre", [128, 2, W])
    lp = sb("lp", [128, 2, W])
    sg = sb("sg", [128, 2, W])
    kk = sb("kk", [128, SEG, S])
    qq = sb("qq", [128, SEG, S])
    cum = sb("cum", [128, SEG, S])
    dist = sb("dist", [128, LEVELS, SEG, S])
    dec = sb("dec", [128, LEVELS + 1, SEG, S])
    kh = [sb("kh0", [128, LEVELS, SEG, S]), m.kh1[:, :].rearrange("p (l g s) -> p l g s", l=LEVELS, g=SEG)]
    qh = [sb(f"qh{k}", [128, LEVELS, SEG, S]) for k in range(2)]
    aT = [sb(f"aT{k}", [S, W]) for k in range(2)]
    vv = [sb(f"vv{k}", [S, 2 * E]) for k in range(2)]
    g1 = sb("g1", [128, GT])
    gpre = sb("gpre", [S, 2 * E])
    gex = sb("gex", [S, 2 * E])
    gate = [sb(f"gate{k}", [S, 2 * E]) for k in range(2)]
    og = sb("og", [S, 2, E])
    on = sb("on", [S, 2, E])
    onT = sb("onT", [128, KE, GT])
    r1 = sb("r1", [S, 2, E])
    x1 = [sb(f"x1{k}", [S, 2, E]) for k in range(2)]
    st = sb("st", [S, 2, 2, 6])
    mv = sb("mv", [S, 2, 2, 2])
    lnv = sb("lnv", [S, 2, 2])
    rstd = sb("rstd", [S, 2, 2])

    names = ("keep_here w_here w_in_high w_in_low w_g1_high w_g1_low x_high x_low zeroed hats_zeroed lnw_folded q_ps lg_ps v_ps g1_ps gate_ps a_ps o_ps onT_ps att_ps x1T_ps "
             "pre_lg pre_q e_done l_done f_done k_done q_done cum_done dist_done dec_done hats_done a_masked "
             "gpre_done gex_done glog_done gate_done v_sb g1_sb og_done st_done mv_done lnv_done rstd_done on_done "
             "onT_sb r1_done x1_done x1T_sb x1_kept").split()
    s = {n: sem("g_" + n) for n in names}
    xT_in = [sem(f"g_xT_in{k}") for k in range(2)]
    xr_in = [sem(f"g_xr_in{k}") for k in range(2)]
    q_bank, lg_bank, v_bank, g1_bank, gate_bank, a0, a1, o_bank = m.bank
    a_bank = [a0, a1]
    N = GROUPS

    def kinds(g):
        return [i for i in range(2) if there(g - 1 - i, N)]

    with nc.Block() as block:
        @block.sync
        def _(sp):
            for q in range(2):
                sp.dma_start(xT[q][:, :, :], io["xT"][:, :, q * GT:(q + 1) * GT].rearrange("k p n -> p k n")).then_inc(xT_in[q], 16)

            def step(g, half, k):
                if isinstance(g, int) and g == -2:
                    sp.dma_start(keep[:, :], io["c_keep"]).then_inc(s["keep_here"], 16)
                    sp.dma_start(w_g1[:, :, :], io["W_g1T"].rearrange("(k p) n -> p k n", p=128)).then_inc(s["w_here"], 16)
                    sp.dma_start(w_g2[:, :], io["W_g2T"]).then_inc(s["w_here"], 16)
                    sp.dma_start(w_out[:, :, :], io["W_outT"].rearrange("(k p) n -> p k n", p=128)).then_inc(s["w_here"], 16)
                    sp.dma_start(ln_w[:, :], io["ln_w"]).then_inc(s["w_here"], 16)
                    sp.dma_start(masks[:, :, :], io["c_masks"].rearrange("p (l n) -> p l n", l=LEVELS)).then_inc(s["w_here"], 16)
                if there(g, N):
                    after(sp, s["r1_done"], g - 1)
                    apart(sp, m)
                    sp.dma_start(xr[k][:, :, :], io["x"][bass.ds(g * 2, 2), :, :].rearrange("b s e -> s b e")).then_inc(xr_in[k], 16)
                if there(g + 4, N):
                    sp.wait_ge(s["x_low"], g + 3)
                    apart(sp, m)
                    sp.dma_start(xT[k][:, :, :], io["xT"][:, :, bass.ds((g + 4) * GT, GT)].rearrange("k p n -> p k n")).then_inc(xT_in[k], 16)
            steps(sp, -2, 2, N - 4, N, step)

        WTS = 5 * 16

        @block.tensor
        def _(pe):
            pe.wait_ge(s["w_in_low"], 1)

            def step(g, half, k):
                n, nk = g + 1, 1 - k
                if there(g + 2, N):
                    pe.wait_ge(s["x_low"], g + 3)
                    after(pe, s["pre_lg"], g + 2)
                    for h in range(H):
                        for e in range(KE):
                            mm = product(pe, lg_bank[:, h * GT:(h + 1) * GT], [w[:, e, 2 * E + h * D:2 * E + (h + 1) * D] for w in w_inp],
                                         [x[:, e, :] for x in xp[k]], e == 0, e == KE - 1)
                    mm.then_inc(s["lg_ps"], 1)
                    after(pe, s["q_done"], g + 2)
                    for h in range(H):
                        for e in range(KE):
                            mm = product(pe, q_bank[:, h * GT:(h + 1) * GT], [w[:, e, E + h * D:E + (h + 1) * D] for w in w_inp],
                                         [x[:, e, :] for x in xp[k]], e == 0, e == KE - 1)
                    mm.then_inc(s["q_ps"], 1)
                def transpose_x1():
                    pe.wait_ge(s["x1_done"], g - 1)
                    after(pe, s["v_sb"], g + 1 if there(g, N) else N)
                    for e in range(KE):
                        for b in range(2):
                            mm = pe.transpose(v_bank[:, (e * 2 + b) * S:(e * 2 + b + 1) * S], x1[k][:, b, e * 128:(e + 1) * 128],
                                              m.ident[0:S, 0:S])
                    mm.then_inc(s["x1T_ps"], 1)
                if there(g, N):
                    pe.wait_ge(s["hats_done"], g + 1)
                    for l in range(LEVELS):
                        if l == LEVELS - 1 and there(g - 2, N):
                            transpose_x1()
                        turn = g * LEVELS + l
                        after(pe, s["a_masked"], turn - 1)
                        for j in range(SEG):
                            mm = pe.matmul(a_bank[(k * LEVELS + l) % 2][0:S, j * S:(j + 1) * S], kh[k][:, l, j, :], qh[k][:, l, j, :],
                                           start=True, stop=True)
                        mm.then_inc(s["a_ps"], 1)
                elif there(g - 2, N):
                    transpose_x1()
                if isinstance(g, int) and g == -1:
                    pe.wait_ge(s["w_g1_low"], 1)
                    pe.wait_ge(s["w_here"], WTS)
                if there(n, N):
                    after(pe, s["onT_sb"], n - 2)
                    for e in range(KE):
                        mm = product(pe, g1_bank[:, 0:GT], [w[:, e, :] for w in w_g1p], [x[:, e, :] for x in xp[nk]], e == 0, e == KE - 1)
                    mm.then_inc(s["g1_ps"], 1)
                    after(pe, s["x1T_sb"], n - 2)
                    after(pe, s["v_sb"], n)
                    for b in range(2):
                        for e in range(KE):
                            mm = product(pe, v_bank[0:S, b * E:(b + 1) * E], [x[:, e, b * S:(b + 1) * S] for x in xp[nk]],
                                         [w[:, e, 0:E] for w in w_inp], e == 0, e == KE - 1)
                    mm.then_inc(s["v_ps"], 1)
                    pe.wait_ge(s["g1_sb"], n + 1)
                    after(pe, s["r1_done"], n - 2)
                    for b in range(2):
                        mm = pe.matmul(gate_bank[0:S, b * E:(b + 1) * E], g1[:, b * S:(b + 1) * S], w_g2[:, :], start=True, stop=True)
                    mm.then_inc(s["gate_ps"], 1)
                if there(g - 1, N):
                    pe.wait_ge(s["on_done"], g)
                    for e in range(KE):
                        for b in range(2):
                            mm = pe.transpose(g1_bank[:, (e * 2 + b) * S:(e * 2 + b + 1) * S], on[:, b, e * 128:(e + 1) * 128],
                                              m.ident[0:S, 0:S])
                    mm.then_inc(s["onT_ps"], 1)
                if there(g, N):
                    pe.wait_ge(s["a_masked"], g * LEVELS + LEVELS)
                    pe.wait_ge(s["v_sb"], g + 1)
                    after(pe, s["og_done"], g)
                    for b in range(2):
                        for h in range(H):
                            j = h * 2 + b
                            c = b * E + h * D
                            mm = pe.matmul(o_bank[0:S, c:c + D], aT[k][:, j * S:(j + 1) * S], vv[k][:, c:c + D], start=True, stop=True)
                    mm.then_inc(s["o_ps"], 1)
                if isinstance(g, int) and g == 1:
                    pe.wait_ge(s["lnw_folded"], 1)
                if there(g - 1, N):
                    pe.wait_ge(s["onT_sb"], g)
                    pe.wait_ge(s["gpre_done"], g + 2 if there(g + 1, N) else N)
                    for b in range(2):
                        for e in range(KE):
                            mm = pe.matmul(gate_bank[0:S, b * E:(b + 1) * E], onT[:, e, b * S:(b + 1) * S], w_out[:, e, :],
                                           start=(e == 0), stop=(e == KE - 1))
                    mm.then_inc(s["att_ps"], 1)
            steps(pe, -2, 2, N - 2, N + 2, step)

        @block.vector
        def _(dve):
            for k in range(2):
                dve.memset(aT[k][:, :], 0.0)
            dve.memset(dist[:, :, :, :], 0.0).then_inc(s["zeroed"], 1)
            dve.wait_ge(m.w_in_here, 16)
            high(dve, w_inp[0][:, :, :], w_in[:, :, :]).then_inc(s["w_in_high"], 1)
            dve.wait_ge(s["w_in_high"], 1)
            dve.tensor_tensor(w_inp[1][:, :, :], w_in[:, :, :], w_inp[0][:, :, :], ALU.subtract).then_inc(s["w_in_low"], 1)
            dve.wait_ge(s["zeroed"], 1)

            def step(g, half, k):
                n, nk = g + 1, 1 - k
                f = g + 2
                if isinstance(g, int) and g == -1:
                    dve.wait_ge(s["w_here"], WTS)
                    high(dve, w_g1p[0][:, :, :], w_g1[:, :, :]).then_inc(s["w_g1_high"], 1)
                    dve.wait_ge(s["w_g1_high"], 1)
                    dve.tensor_tensor(w_g1p[1][:, :, :], w_g1[:, :, :], w_g1p[0][:, :, :], ALU.subtract).then_inc(s["w_g1_low"], 1)
                    for e in range(KE):
                        mul = dve.tensor_scalar(w_out[:, e, :], w_out[:, e, :], ln_w[:, e:e + 1], None, ALU.mult)
                    mul.then_inc(s["lnw_folded"], 1)

                def normalise():
                    if there(g - 1, N):
                        dve.wait_ge(s["rstd_done"], g)
                        after(dve, s["onT_ps"], g - 1)
                        for b in range(2):
                            ts = dve.tensor_scalar(on[:, b, :], og[:, b, :], mv[:, 0, b, 0:1], rstd[:, 0, b:b + 1], ALU.subtract, ALU.mult)
                        ts.then_inc(s["on_done"], 1)
                    if there(g - 2, N):
                        dve.wait_ge(s["rstd_done"], g)
                        after(dve, s["x1T_ps"], g - 3)
                        after(dve, s["x1_kept"], g - 3)
                        for b in range(2):
                            ts = dve.tensor_scalar(x1[k][:, b, :], r1[:, b, :], mv[:, 1, b, 0:1], rstd[:, 1, b:b + 1], ALU.subtract, ALU.mult)
                        ts.then_inc(s["x1_done"], 1)

                if there(g - 1, N):
                    dve.wait_ge(s["o_ps"], g)
                    dve.wait_ge(s["gate_done"], g)
                    dve.tensor_tensor(og[:, :, :].rearrange("p b e -> p (b e)"), o_bank[0:S, :], gate[nk][:, :], ALU.mult).then_inc(s["og_done"], 1)
                if there(g - 2, N):
                    dve.wait_ge(s["att_ps"], g - 1)
                    dve.wait_ge(xr_in[k], half * 16)
                    dve.tensor_tensor(r1[:, :, :].rearrange("p b e -> p (b e)"), gate_bank[0:S, :], xr[k][:, :, :].rearrange("p b e -> p (b e)"), ALU.add).then_inc(s["r1_done"], 1)
                if there(g - 1, N):
                    dve.wait_ge(s["og_done"], g)
                    for b in range(2):
                        bn = dve.bn_stats(st[:, 0, b, :], og[:, b, :])
                    if not there(g - 2, N):
                        bn.then_inc(s["st_done"], 1)
                if there(g - 2, N):
                    dve.wait_ge(s["r1_done"], g - 1)
                    for b in range(2):
                        bn = dve.bn_stats(st[:, 1, b, :], r1[:, b, :])
                    bn.then_inc(s["st_done"], 1)
                if there(g - 1, N) or there(g - 2, N):
                    dve.wait_ge(s["st_done"], g)
                    apart(dve, m)
                    for i in kinds(g):
                        for b in range(2):
                            bn = dve.bn_aggr(mv[:, i, b, :], st[:, i, b, :])
                    bn.then_inc(s["mv_done"], 1)
                if there(f, N):
                    dve.wait_ge(s["lg_ps"], f + 1)
                    after(dve, s["e_done"], f)
                    dve.tensor_scalar(pre[:, 0, :], lg_bank[:, 0:W], -LOG_MAX, None, ALU.max).then_inc(s["pre_lg"], 1)
                    dve.wait_ge(s["q_ps"], f + 1)
                    dve.tensor_scalar(pre[:, 1, :], q_bank[:, 0:W], -GATE_MAX, None, ALU.max).then_inc(s["pre_q"], 1)
                if there(g, N):
                    for l in range(LEVELS):
                        if l == 2:
                            normalise()
                        dve.wait_ge(s["a_ps"], g * LEVELS + l + 1)
                        after(dve, s["a_masked"], g * LEVELS + l)
                        if l == 0:
                            after(dve, s["o_ps"], g - 1)
                        apart(dve, m)
                        dve.copy_predicated(aT[k][:, :], masks[:, l, :], a_bank[(k * LEVELS + l) % 2][0:S, 0:W]).then_inc(s["a_masked"], 1)
                else:
                    normalise()
                if there(f, N):
                    if isinstance(g, int) and g == -2:
                        dve.wait_ge(s["keep_here"], 16)
                    dve.wait_ge(s["l_done"], f + 1)
                    after(dve, s["dist_done"], f)
                    dve.tensor_tensor_scan(cum[:, :, :].rearrange("p g s -> p (g s)"), keep[:, :], lp[:, 0, :], 0.0, ALU.mult, ALU.add).then_inc(s["cum_done"], 1)
                    dve.wait_ge(s["f_done"], f + 1)
                    after(dve, s["hats_done"], f)
                    dve.tensor_tensor(qq[:, :, :].rearrange("p g s -> p (g s)"), q_bank[:, 0:W], sg[:, 1, :], ALU.mult).then_inc(s["q_done"], 1)
                    dve.wait_ge(s["cum_done"], f + 1)
                    after(dve, s["dec_done"], f)
                for l in range(LEVELS - 1):
                    if l == 1 and there(n, N):
                        dve.wait_ge(s["gate_ps"], n + 1)
                        after(dve, s["gex_done"], n)
                        dve.tensor_scalar(gpre[:, :], gate_bank[0:S, :], -GATE_MAX, None, ALU.max).then_inc(s["gpre_done"], 1)
                    if there(f, N):
                        for run in LEFT[l]:
                            dve.tensor_tensor(blocks(dist[:, l], run), cuts(cum, run), blocks(cum, run), ALU.subtract)
                        for run in RIGHT[l]:
                            dve.tensor_tensor(blocks(dist[:, l], run), blocks(cum, run), cuts(cum, run), ALU.subtract)
                if there(f, N):
                    run = (0, S // BASE, BASE, BASE, BASE_CUT)
                    dve.tensor_tensor(blocks(dist[:, LEVELS - 1], run), blocks(cum, run), cuts(cum, run), ALU.subtract).then_inc(s["dist_done"], 1)
            steps(dve, -2, 4, N - 2, N + 2, step)

        @block.scalar
        def _(act):
            act.preload_act_table_set(LOG_EXP)
            act.wait_ge(s["zeroed"], 1)

            def step(g, half, k):
                n, nk = g + 1, 1 - k
                if there(g - 1, N) or there(g - 2, N):
                    of = slice(kinds(g)[0], kinds(g)[-1] + 1)
                    act.wait_ge(s["mv_done"], g)
                    act.activation(lnv[:, of, :], mv[:, of, :, 1], ACT.Ln, bias=m.eps[0:S, :]).then_inc(s["lnv_done"], 1)
                    act.wait_ge(s["lnv_done"], g)
                    after(act, s["on_done"], g - 1)
                    after(act, s["x1_done"], g - 2)
                    act.activation(rstd[:, of, :], lnv[:, of, :], ACT.Exp, scale=-0.5).then_inc(s["rstd_done"], 1)
                f = g + 2
                if there(f, N):
                    act.wait_ge(s["pre_lg"], f + 1)
                    act.wait_ge(s["pre_q"], f + 1)
                    after(act, s["cum_done"], f)
                    act.activation(lp[:, :, :], pre[:, :, :], ACT.Exp, scale=-1.0).then_inc(s["e_done"], 1)
                    act.wait_ge(s["e_done"], f + 1)
                    act.activation(lp[:, :, :], lp[:, :, :], ACT.Ln, bias=m.one[:, :]).then_inc(s["l_done"], 1)
                    act.wait_ge(s["l_done"], f + 1)
                    after(act, s["k_done"], f)
                    after(act, s["q_done"], f)
                    act.activation(sg[:, :, :], lp[:, :, :], ACT.Exp, scale=-1.0).then_inc(s["f_done"], 1)
                if there(g - 2, N):
                    act.wait_ge(s["x1T_ps"], g - 1)
                    act.activation(m.x1T[:, :, bass.ds((g - 2) * GT, GT)], v_bank[:, 0:W].rearrange("p (k n) -> p k n", k=KE), ACT.Copy).then_inc(s["x1T_sb"], 1)
                if there(n, N):
                    act.wait_ge(s["g1_ps"], n + 1)
                    after(act, s["gate_ps"], n)
                    act.activation(g1[:, :], g1_bank[:, 0:GT], ACT.Copy).then_inc(s["g1_sb"], 1)
                    act.wait_ge(s["v_ps"], n + 1)
                    after(act, s["o_ps"], n - 1)
                    act.activation(vv[nk][:, :], v_bank[0:S, :], ACT.Copy).then_inc(s["v_sb"], 1)
                if there(g - 1, N):
                    act.wait_ge(s["onT_ps"], g)
                    after(act, s["att_ps"], g - 1)
                    act.activation(onT[:, :, :], g1_bank[:, 0:W].rearrange("p (k n) -> p k n", k=KE), ACT.Copy).then_inc(s["onT_sb"], 1)
                if there(n, N):
                    act.wait_ge(s["gpre_done"], n + 1)
                    act.activation(gex[:, :], gpre[:, :], ACT.Exp, scale=-1.0).then_inc(s["gex_done"], 1)
                    act.wait_ge(s["gex_done"], n + 1)
                    act.activation(gex[:, :], gex[:, :], ACT.Ln, bias=m.one[0:S, :]).then_inc(s["glog_done"], 1)
                    act.wait_ge(s["glog_done"], n + 1)
                    after(act, s["og_done"], n - 1)
                    act.activation(gate[nk][:, :], gex[:, :], ACT.Exp, scale=-1.0).then_inc(s["gate_done"], 1)
                if there(f, N):
                    act.wait_ge(s["dist_done"], f + 1)
                    after(act, s["hats_done"], f)
                    act.activation(dec[:, 0:LEVELS, :, :], dist[:, :, :, :], ACT.Exp, scale=-1.0)
                    act.activation(dec[:, LEVELS, :, :], dist[:, LEVELS - 1, :, :], ACT.Exp).then_inc(s["dec_done"], 1)
            steps(act, -2, 4, N - 2, N + 2, step)

        @block.gpsimd
        def _(pool):
            def cut_x(q, k, value):
                pool.wait_ge(xT_in[k], value)
                after(pool, s["v_ps"], q - 1)
                apart(pool, m)
                high(pool, xp[k][0][:, :, :], xT[k][:, :, :]).then_inc(s["x_high"], 1)
                pool.wait_ge(s["x_high"], q + 1)
                pool.tensor_tensor(xp[k][1][:, :, :], xT[k][:, :, :], xp[k][0][:, :, :], ALU.subtract).then_inc(s["x_low"], 1)

            cut_x(0, 0, 16)
            for k in range(2):
                if k == 1:
                    pool.wait_ge(s["w_in_low"], 1)
                pool.memset(kh[k][:, :, :, :], 0.0)
                ms = pool.memset(qh[k][:, :, :, :], 0.0)
            ms.then_inc(s["hats_zeroed"], 1)
            pool.wait_ge(s["hats_zeroed"], 1)

            def step(g, half, k):
                n, nk = g + 1, 1 - k
                f = g + 2
                if there(f, N):
                    after(pool, s["hats_done"], f)
                    pool.wait_ge(s["f_done"], f + 1)
                    apart(pool, m)
                    pool.tensor_scalar(kk[:, :, :].rearrange("p g s -> p (g s)"), sg[:, 0, :], -1.0, 1.0, ALU.mult, ALU.add).then_inc(s["k_done"], 1)
                if there(g - 2, N):
                    pool.wait_ge(s["x1_done"], g - 1)
                    pool.tensor_tensor(m.xres[:, bass.ds((g - 2) * 2, 2), :], x1[k][:, :, :], m.bo_rows[:, :, :], ALU.add).then_inc(s["x1_kept"], 1)
                if there(g + 3, N):
                    cut_x(g + 3, nk, (half + k + 2) * 16)
                if there(f, N):
                    pool.wait_ge(s["dec_done"], f + 1)
                    pool.wait_ge(s["k_done"], f + 1)
                    pool.wait_ge(s["q_done"], f + 1)
                    after(pool, s["a_ps"], (f - 1) * LEVELS)
                    for l in range(LEVELS - 1):
                        for run in LEFT[l]:
                            pool.tensor_tensor(blocks(kh[k][:, l], run), blocks(kk, run), blocks(dec[:, l], run), ALU.mult)
                        for run in RIGHT[l]:
                            pool.tensor_tensor(blocks(qh[k][:, l], run), blocks(qq, run), blocks(dec[:, l], run), ALU.mult)
                    pool.tensor_tensor(qh[k][:, LEVELS - 1], qq[:, :, :], dec[:, LEVELS - 1], ALU.mult)
                    pool.tensor_tensor(kh[k][:, LEVELS - 1], kk[:, :, :], dec[:, LEVELS], ALU.mult).then_inc(s["hats_done"], 1)
            steps(pool, -2, 2, N - 4, N + 2, step)


K_PART = [0, 0, 1, 1, 0, 2]
Q_PART = [0, 1, 0, 1, 2, 0]
TERMS = len(K_PART)
SHIFT_ROW = TERMS * DK
CHUNK = [0, 128, SC - 128]
CHUNKS = len(CHUNK)
UNITS = NH // 4
SLOTS = UNITS * CHUNKS
VW = DK + 1
PAIRS = B // 2


def attention_phase(nc, m, ctx, io):
    def sb(name, shape, dt=F32):
        return ctx.enter_context(nc.sbuf_tensor(name, shape, dt))

    def sem(name):
        return ctx.enter_context(nc.semaphore("a_" + name))

    W = 4 * S
    wk = sb("wk", [C, E])
    wv = sb("wv", [C, E])
    wq = sb("wq", [128, KE, E])
    wo = sb("wo", [128, UNITS, E])
    sel = sb("sel", [128, 128])
    vmask = sb("vmask", [128, CHUNKS])
    bk = sb("bk", [128, KE])
    bq = sb("bq", [128, KE])
    bqs = sb("bqs", [128, KE])
    idb = sb("idb", [128, 128], BF16)
    ctxK = sb("ctxK", [C, 2 * SC])
    ctxV = sb("ctxV", [C, 2 * SC])
    kf = sb("kf", [128, KE, 2 * SC])
    kr = sb("kr", [128, KE, 2 * SC])
    kp = sb("kp", [128, 3, KE, 2 * SC], BF16)
    qf = sb("qf", [128, KE, GT])
    qr = sb("qr", [128, KE, GT])
    qp = sb("qp", [128, 3, KE, GT], BF16)
    KS = [sb(f"KS{k}", [SHIFT_ROW + 1, NH, 2 * SC], BF16) for k in range(2)]
    QS = [sb(f"QS{k}", [SHIFT_ROW + 1, NH, GT], BF16) for k in range(2)]
    V = [sb(f"V{k}", [128, 2, CHUNKS, NH, VW]) for k in range(2)]
    RING = 4
    EARLY = 2
    LAG = 2
    PT = [sb(f"PT{k}", [128, W]) for k in range(RING)]
    nm = sb("nm", [S, NH], BF16)
    ones = sb("ones", [NH, 2 * SC], BF16)
    mT = sb("mT", [NH, S], BF16)
    aT = sb("aT", [128, W])
    lz = sb("lz", [128, W])
    rz = sb("rz", [128, W])
    aN = sb("aN", [128, W])
    r2 = sb("r2", [S, E])
    x2 = [sb(f"x2{k}", [S, E]) for k in range(2)]
    st = sb("st_a", [S, 6])
    mv = sb("mv_a", [S, 2])
    lnv = sb("lnv_a", [S, 1])
    rstd = sb("rstd_a", [S, 1])
    kscr = nc.dram_tensor("k_parts", (PAIRS, 3, KE, 128, 2 * SC), BF16, kind="Internal").ap()
    qscr = nc.dram_tensor("q_parts", (PAIRS, 3, KE, 128, GT), BF16, kind="Internal").ap()

    names = ("w_here ready ones_done ones_in ctxK_in ctxV_in k_ps q_ps v_ps k_sb q_sb v_sb k_rest k2 k3 q_rest q2 q3 "
             "kscr_in qscr_in stack_in max_ps max_done mT_ps mT_sb st_ps pt_done pv_ps aT_done zb_ps lz_done rz_done "
             "aN_done wo_ps r2_done st_done mv_done lnv_done rstd_done x2_done x2T_ps x2T_sb x2_kept").split()
    s = {n: sem(n) for n in names}
    mrow_in = [sem(f"mrow_in{j}") for j in range(2)]
    lt_out = [sem(f"lt_out{j}") for j in range(2)]
    st_bank, mx_bank, pv_bank, pj_bank, misc = m.bank[0:2], m.bank[2:4], m.bank[4], m.bank[5:7], m.bank[7]
    N = PAIRS
    NW = 8 * 16

    def pieces(p, j):
        if j == 0:
            todo = [("k", p + 2, (t, b), t * 2 + b) for t in range(KE) for b in range(2)] + [("q", p + 2, t, t) for t in range(KE)]
        else:
            todo = [("v", p + 1, (b, c), b * CHUNKS + c) for b in range(2) for c in range(CHUNKS)]
        return {2 * i: x + ((i % 2),) for i, x in enumerate(todo)}

    COUNT = {"k": 4, "q": 2, "v": 6}

    def maxima(b, j, slot, k):
        if slot < NH // 2 - EARLY:
            return (b + 1, 1 - j, k if j == 0 else 1 - k, 2 * (slot + EARLY))
        if slot >= SLOTS - EARLY:
            return (b + 2, j, 1 - k, 2 * (slot - SLOTS + EARLY))
        return (B, None, None, None)

    with nc.Block() as block:
        @block.sync
        def _(sp):
            sp.dma_start(ctxK[:, :], io["ctxT"][:, 0:2 * SC]).then_inc(s["ctxK_in"], 16)
            for dst, src in ((wk[:, :], io["Wk"]), (wv[:, :], io["Wv"]), (wq[:, :, :], io["Wq"].rearrange("(k p) n -> p k n", p=128)),
                             (wo[:, :, :], io["Wo_units"]), (sel[:, :], io["c_sel"]), (vmask[:, :], io["c_vmask"]),
                             (bk[:, :], io["bk"]), (bq[:, :], io["bq"])):
                sp.dma_start(dst, src).then_inc(s["w_here"], 16)
            sp.wait_ge(s["ones_done"], 1)
            for k in range(2):
                sp.dma_start(KS[k][SHIFT_ROW:SHIFT_ROW + 1, :, :], ones[:, :]).then_inc(s["ones_in"], 16)

            def step(p, half, k):
                nk = 1 - k
                def shift_row(b, j, k):
                    if there(b, B):
                        sp.wait_ge(s["mT_sb"], b + 1)
                        apart(sp, m)
                        sp.dma_start(QS[k][SHIFT_ROW:SHIFT_ROW + 1, :, j * S:(j + 1) * S], mT[:, :]).then_inc(mrow_in[j], 16)

                def keep_tokens(b, j):
                    if there(b, B):
                        sp.wait_ge(s["x2_done"], b + 1)
                        for part in range(2):
                            first = 1 + 2 * LR * part
                            apart(sp, m)
                            sp.dma_start(m.lt[part, bass.ds(b, 1)].rearrange("a t e -> t (a e)"), x2[j][first:first + 2 * LR:2, :]).then_inc(lt_out[j], 16)

                if there(p + 1, N):
                    after(sp, s["v_ps"], (p + 1) * 6)
                    apart(sp, m)
                    sp.dma_start(ctxV[:, :], io["ctxT"][:, bass.ds((p + 1) * 2 * SC, 2 * SC)]).then_inc(s["ctxV_in"], 16)
                    after(sp, s["st_ps"], p * 2 * SLOTS)
                    apart(sp, m)
                    sp.wait_ge(s["kscr_in"], (p + 2) * 32)
                    for t in range(TERMS):
                        rows = slice(t * DK, (t + 1) * DK)
                        apart(sp, m)
                        sp.dma_start(KS[nk][rows, :, :], kscr[bass.ds(p + 1, 1), K_PART[t]].rearrange("a t (h d) n -> d (a t h) n", d=DK)).then_inc(s["stack_in"], 16)
                    sp.wait_ge(s["qscr_in"], (p + 2) * 16)
                    for t in range(TERMS):
                        rows = slice(t * DK, (t + 1) * DK)
                        apart(sp, m)
                        sp.dma_start(QS[nk][rows, :, :], qscr[bass.ds(p + 1, 1), Q_PART[t]].rearrange("a t (h d) n -> d (a t h) n", d=DK)).then_inc(s["stack_in"], 16)
                shift_row(p * 2 + 1, 1, k)
                if there(p + 3, N):
                    sp.wait_ge(s["k_ps"], (p + 3) * 4)
                    apart(sp, m)
                    sp.dma_start(ctxK[:, :], io["ctxT"][:, bass.ds((p + 3) * 2 * SC, 2 * SC)]).then_inc(s["ctxK_in"], 16)
                keep_tokens(p * 2 - 1, 1)
                if there(p + 2, N):
                    for t in range(KE):
                        sp.wait_ge(s["k3"], (p + 2) * 2 + t + 1)
                        apart(sp, m)
                        sp.dma_start(kscr[bass.ds(p + 2, 1), :, t].rearrange("a c p n -> p (a c) n"), kp[:, :, t, :]).then_inc(s["kscr_in"], 16)
                    sp.wait_ge(s["q3"], p + 3)
                    apart(sp, m)
                    sp.dma_start(qscr[bass.ds(p + 2, 1)].rearrange("a c t p n -> p (a c t) n"), qp[:, :, :, :].rearrange("p c t n -> p (c t) n")).then_inc(s["qscr_in"], 16)
                shift_row(p * 2 + 2, 0, nk)
                keep_tokens(p * 2, 0)
            steps(sp, -2, 2, N - 4, N + 1, step)
            for k in range(2):
                sp.wait_ge(lt_out[k], (B // 2) * 32)

        @block.tensor
        def _(pe):
            pe.wait_ge(s["w_here"], NW)
            pe.wait_ge(s["ready"], 1)

            def project(kind, q, args, i, turn, prior_sem, prior_value):
                pj = pj_bank[turn]
                after(pe, prior_sem, prior_value)
                if kind == "k":
                    t, b = args
                    pe.wait_ge(s["ctxK_in"], (q + 1) * 16)
                    pe.matmul(pj[:, 0:SC], wk[:, t * 128:(t + 1) * 128], ctxK[:, b * SC:(b + 1) * SC], start=True, stop=True).then_inc(s["k_ps"], 1)
                elif kind == "q":
                    for e in range(KE):
                        mm = pe.matmul(pj[:, 0:GT], wq[:, e, args * 128:(args + 1) * 128], m.x1T[:, e, bass.ds(q * GT, GT)], start=(e == 0), stop=(e == KE - 1))
                    mm.then_inc(s["q_ps"], 1)
                else:
                    b, c = args
                    pe.wait_ge(s["ctxV_in"], (q + 1) * 16)
                    pe.matmul(pj[:, 0:E], ctxV[:, b * SC + CHUNK[c]:b * SC + CHUNK[c] + 128], wv[:, :], start=True, stop=True).then_inc(s["v_ps"], 1)

            def weigh(b, k, j, slot):
                u, c = slot // CHUNKS, slot % CHUNKS
                n = b * SLOTS + slot
                pe.wait_ge(s["pt_done"], n + 1)
                if slot == 0:
                    pe.wait_ge(s["v_sb"], (b + 1) * 3)
                    after(pe, s["aT_done"], b)
                for i in range(4):
                    mm = pe.matmul(pv_bank[32 * i:32 * i + VW, u * S:(u + 1) * S], V[k][:, j, c, u * 4 + i, :], PT[(j * SLOTS + slot) % RING][:, i * S:(i + 1) * S],
                                   start=(c == 0), stop=(c == CHUNKS - 1), skip_group_check=True)
                mm.then_inc(s["pv_ps"], 1)

            def step(p, half, k):
                nk = 1 - k
                for j in range(2):
                    b = p * 2 + j
                    work = pieces(p, j)
                    for slot in range(SLOTS):
                        a, jj, kk, first = maxima(b, j, slot, k)

                        def row_scores(i):
                            if there(a, B):
                                h = first + i
                                if jj == 0 and h == 0:
                                    pe.wait_ge(s["stack_in"], (p + 2) * TERMS * 2 * 16)
                                after(pe, s["max_done"], a * NH + h - 1)
                                if h == 0:
                                    after(pe, s["mT_sb"], a)
                                pe.matmul(mx_bank[h % 2][0:S, 0:SC], QS[kk][0:SHIFT_ROW, h, jj * S:(jj + 1) * S],
                                          KS[kk][0:SHIFT_ROW, h, jj * SC:(jj + 1) * SC], start=True, stop=True).then_inc(s["max_ps"], 1)

                        if there(b, B):
                            n = b * SLOTS + slot
                            if slot == 0:
                                pe.wait_ge(mrow_in[j], (p + 1) * 16)
                            if isinstance(b, int) and b == 0 and slot == 0:
                                pe.wait_ge(s["ones_in"], 32)
                            after(pe, s["pt_done"], n - 1)
                            u, c = slot // CHUNKS, slot % CHUNKS
                            for i in range(4):
                                at = j * SC + CHUNK[c]
                                mm = pe.matmul(st_bank[slot % 2][:, i * S:(i + 1) * S], KS[k][:, u * 4 + i, at:at + 128],
                                               QS[k][:, u * 4 + i, j * S:(j + 1) * S], start=True, stop=True)
                            mm.then_inc(s["st_ps"], 1)
                        row_scores(0)
                        if there(b - 1, B) and slot < LAG:
                            weigh(b - 1, k if j else nk, 1 - j, SLOTS - LAG + slot)
                        elif there(b, B) and slot > LAG:
                            for t in ((0, 1) if slot == LAG + 1 else (slot - LAG,)):
                                weigh(b, k, j, t)
                        row_scores(1)
                        if slot in work and there(work[slot][1], N):
                            kind, q, args, i, turn = work[slot]
                            project(kind, q, args, i, turn, *last_piece(p, j, slot))
                        if there(b - 2, B) and slot == 0:
                            pe.wait_ge(s["x2_done"], b - 1)
                            for e in range(KE):
                                mm = pe.transpose(misc[:, e * S:(e + 1) * S], x2[j][:, e * 128:(e + 1) * 128], m.ident[0:S, 0:S])
                            mm.then_inc(s["x2T_ps"], 1)
                        if there(b - 1, B):
                            if slot == 2:
                                pe.wait_ge(s["aT_done"], b)
                                after(pe, s["x2T_sb"], b - 1)
                                pe.matmul(misc[:, 0:W], sel[:, :], aT[:, :], start=True, stop=True).then_inc(s["zb_ps"], 1)
                            if slot == 6:
                                pe.wait_ge(s["aN_done"], b)
                                pe.wait_ge(s["lz_done"], b)
                                for u in range(UNITS):
                                    mm = pe.matmul(misc[0:S, 0:E], aN[:, u * S:(u + 1) * S], wo[:, u, :], start=(u == 0), stop=(u == UNITS - 1))
                                mm.then_inc(s["wo_ps"], 1)
                        if there(b + 1, B) and slot == 6:
                            pe.wait_ge(s["max_done"], (b + 1) * NH + NH)
                            pe.transpose(mx_bank[0][0:NH, 0:S // 2].bitcast(BF16), nm[:, :], idb[0:S, 0:S]).then_inc(s["mT_ps"], 1)

            def last_piece(p, j, slot):
                i = slot // 2
                if j == 0:
                    if isinstance(p, int) and p == -1 and i < 2:
                        return s["q_sb"], i + 1
                    if i < 2:
                        return s["v_sb"], (p + 1) * 6 - 1 + i
                    return s["k_sb"], (p + 2) * 4 + i - 1
                if i < 2:
                    return s["q_sb"], (min(p + 2, N - 1) if isinstance(p, int) else p + 2) * 2 + i + 1
                return s["v_sb"], (p + 1) * 6 + i - 1
            steps(pe, -2, 2, N - 2, N + 1, step)

        @block.vector
        def _(dve):
            dve.memset(ones[:, :], 1.0).then_inc(s["ones_done"], 1)
            dve.wait_ge(s["w_here"], NW)
            dve.tensor_scalar(bqs[:, :], bq[:, :], DK ** -0.5, None, ALU.mult).then_inc(s["ready"], 1)
            dve.memset(pv_bank[:, :], 0.0)
            dve.tensor_copy(idb[:, :], m.ident[:, :])

            for k in range(2):
                for j in range(2):
                    for c in range(CHUNKS):
                        dve.tensor_copy(V[k][:, j, c, :, DK:DK + 1], vmask[:, c:c + 1].to_broadcast([128, NH, 1]))

            def step(p, half, k):
                for j in range(2):
                    b = p * 2 + j
                    for slot in range(SLOTS):
                        if there(b - 1, B) and slot == 5:
                            dve.wait_ge(s["rz_done"], b)
                            after(dve, s["wo_ps"], b - 1)
                            dve.tensor_tensor(aN[:, :], aT[:, :], rz[:, :], ALU.mult).then_inc(s["aN_done"], 1)
                        a, _, _, first = maxima(b, j, slot, k)
                        if there(a, B):
                            for h in (first, first + 1):
                                dve.wait_ge(s["max_ps"], a * NH + h + 1)
                                if h == 0:
                                    after(dve, s["mT_ps"], a)
                                dve.tensor_reduce(nm[:, h:h + 1], mx_bank[h % 2][0:S, 0:SC], AX.X, ALU.max, negate=True).then_inc(s["max_done"], 1)
                        if there(p + 2, N):
                            q = p + 2
                            for t in range(KE):
                                if j == 0 and slot == (7, 11)[t]:
                                    dve.wait_ge(s["k_rest"], q * 2 + t + 1)
                                    dve.tensor_copy(kp[:, 1, t, :], kr[:, t, :]).then_inc(s["k2"], 1)
                            if j == 1 and slot == 4:
                                dve.wait_ge(s["q_rest"], q + 1)
                                dve.tensor_copy(qp[:, 1], qr[:, :, :]).then_inc(s["q2"], 1)
                        if there(b - 1, B):
                            if slot == 7:
                                dve.wait_ge(s["wo_ps"], b)
                                dve.tensor_tensor(r2[:, :], misc[0:S, 0:E], m.xres[:, bass.ds(b - 1, 1), :].rearrange("p a e -> p (a e)"), ALU.add).then_inc(s["r2_done"], 1)
                                dve.wait_ge(s["r2_done"], b)
                                dve.bn_stats(st[:, :], r2[:, :]).then_inc(s["st_done"], 1)
                                dve.wait_ge(s["st_done"], b)
                                apart(dve, m)
                                dve.bn_aggr(mv[:, :], st[:, :]).then_inc(s["mv_done"], 1)
                            if slot == 10:
                                dve.wait_ge(s["rstd_done"], b)
                                after(dve, s["x2T_ps"], b - 2)
                                after(dve, s["x2_kept"], b - 2)
                                if there(b - 3, B):
                                    dve.wait_ge(lt_out[1 - j], ((b - 1) // 2 if isinstance(b, int) else p + j - 1) * 32)
                                dve.tensor_scalar(x2[1 - j][:, :], r2[:, :], mv[:, 0:1], rstd[:, 0:1], ALU.subtract, ALU.mult).then_inc(s["x2_done"], 1)
            steps(dve, -2, 2, N - 2, N + 1, step)

        @block.scalar
        def _(act):
            act.preload_act_table_set(LOG_EXP)
            act.wait_ge(s["w_here"], NW)
            act.wait_ge(s["ready"], 1)

            def step(p, half, k):
                nk = 1 - k
                for j in range(2):
                    b = p * 2 + j
                    work = pieces(p, j)
                    for slot in range(SLOTS):
                        if there(b, B):
                            n = b * SLOTS + slot
                            act.wait_ge(s["st_ps"], n + 1)
                            after(act, s["pv_ps"], n + 1 - RING)
                            act.activation(PT[(j * SLOTS + slot) % RING][:, :], st_bank[slot % 2][:, 0:W], ACT.Exp).then_inc(s["pt_done"], 1)
                        if there(b - 1, B):
                            if slot == LAG - 1:
                                act.wait_ge(s["pv_ps"], b * SLOTS)
                                after(act, s["aN_done"], b - 1)
                                act.activation(aT[:, :], pv_bank[:, 0:W], ACT.Copy).then_inc(s["aT_done"], 1)
                            if slot == 3:
                                act.wait_ge(s["zb_ps"], b)
                                act.activation(lz[:, :], misc[:, 0:W], ACT.Ln).then_inc(s["lz_done"], 1)
                                act.wait_ge(s["lz_done"], b)
                                after(act, s["aN_done"], b - 1)
                                act.activation(rz[:, :], lz[:, :], ACT.Exp, scale=-1.0).then_inc(s["rz_done"], 1)
                            if slot == 9:
                                act.wait_ge(s["mv_done"], b)
                                act.activation(lnv[:, :], mv[:, 1:2], ACT.Ln, bias=m.eps[0:S, :]).then_inc(s["lnv_done"], 1)
                                act.wait_ge(s["lnv_done"], b)
                                after(act, s["x2_done"], b - 1)
                                act.activation(rstd[:, :], lnv[:, :], ACT.Exp, scale=-0.5).then_inc(s["rstd_done"], 1)
                        if there(b + 1, B) and slot == 7:
                            jj = 1 - j
                            act.wait_ge(s["mT_ps"], b + 2)
                            if there(b, B):
                                act.wait_ge(mrow_in[1 - jj], (p + 1) * 16)
                            act.activation(mT[:, :], mx_bank[0][0:NH, 0:S // 2].bitcast(BF16), ACT.Copy).then_inc(s["mT_sb"], 1)
                        if there(b - 2, B) and slot == 1:
                            act.wait_ge(s["x2T_ps"], b - 1)
                            act.activation(m.x1T[:, :, bass.ds((b - 2) * S, S)], misc[:, 0:2 * S].rearrange("p (k n) -> p k n", k=KE), ACT.Copy).then_inc(s["x2T_sb"], 1)
                        if slot - 1 in work and there(work[slot - 1][1], N):
                            kind, q, args, i, turn = work[slot - 1]
                            act.wait_ge(s[kind + "_ps"], q * COUNT[kind] + i + 1)
                            pj = pj_bank[turn]
                            if kind == "k":
                                t, bb = args
                                after(act, s["k3"], q * 2 - 1 + t)
                                after(act, s["kscr_in"], q * 32)
                                act.activation(kf[:, t, bb * SC:(bb + 1) * SC], pj[:, 0:SC], ACT.Identity, bias=bk[:, t:t + 1])
                                act.activation(kp[:, 0, t, bb * SC:(bb + 1) * SC], pj[:, 0:SC], ACT.Identity, bias=bk[:, t:t + 1]).then_inc(s["k_sb"], 1)
                            elif kind == "q":
                                after(act, s["q3"], q)
                                after(act, s["qscr_in"], q * 16)
                                act.activation(qf[:, args, :], pj[:, 0:GT], ACT.Identity, bias=bqs[:, args:args + 1], scale=DK ** -0.5)
                                act.activation(qp[:, 0, args, :], pj[:, 0:GT], ACT.Identity, bias=bqs[:, args:args + 1], scale=DK ** -0.5).then_inc(s["q_sb"], 1)
                            else:
                                bb, c = args
                                after(act, s["pv_ps"], (q - 1) * 2 * SLOTS)
                                act.activation(V[nk][:, bb, c, :, 0:DK], pj[:, 0:E].rearrange("p (h d) -> p h d", h=NH), ACT.Identity, scale=vmask[:, c:c + 1]).then_inc(s["v_sb"], 1)
            steps(act, -2, 2, N - 4, N + 1, step)

        @block.gpsimd
        def _(pool):
            def step(p, half, k):
                if there(p + 2, N):
                    q = p + 2
                    for t in range(KE):
                        pool.wait_ge(s["k_sb"], q * 4 + 2 * t + 2)
                        pool.tensor_tensor(kr[:, t, :], kf[:, t, :], kp[:, 0, t, :], ALU.subtract).then_inc(s["k_rest"], 1)
                        pool.wait_ge(s["k2"], q * 2 + t + 1)
                        pool.tensor_tensor(kp[:, 2, t, :], kr[:, t, :], kp[:, 1, t, :], ALU.subtract).then_inc(s["k3"], 1)
                    pool.wait_ge(s["q_sb"], q * 2 + 2)
                    pool.tensor_tensor(qr[:, :, :], qf[:, :, :], qp[:, 0], ALU.subtract).then_inc(s["q_rest"], 1)
                    pool.wait_ge(s["q2"], q + 1)
                    pool.tensor_tensor(qp[:, 2], qr[:, :, :], qp[:, 1], ALU.subtract).then_inc(s["q3"], 1)
                for j in range(2):
                    b = p * 2 + j - 1
                    if there(b, B):
                        pool.wait_ge(s["x2_done"], b + 1)
                        pool.tensor_tensor(m.xres[:, bass.ds(b, 1), :].rearrange("p a e -> p (a e)"), x2[1 - j][:, :], m.b2_rows[:, :], ALU.add).then_inc(s["x2_kept"], 1)
            steps(pool, -2, 2, N - 2, N + 1, step)


FB = 4
FT = FB * S
FGROUPS = B // FB
LR = 4
TILES = HID // 128


def ffn_phase(nc, m, ctx, io):
    def sb(name, shape, dt=F32):
        return ctx.enter_context(nc.sbuf_tensor(name, shape, dt))

    def sem(name):
        return ctx.enter_context(nc.semaphore("f_" + name))

    R = FB * LR
    WCOLS = KE * HID
    assert WCOLS == TILES * E
    w_raw = sb("w_raw", [128, WCOLS])
    w1 = [sb(f"w1{i}", [128, KE, HID], F32R) for i in range(2)]
    w2 = [sb(f"w2{i}", [128, TILES, E], F32R) for i in range(2)]
    x = [sb(f"xp{i}", [128, KE, FT], F32R) for i in range(2)]
    odd1 = [sb(f"odd1{i}", [128, KE, 3, 32], F32R) for i in range(2)]
    odd2 = sb("odd2", [128, KE, FB, LR])
    b1 = sb("b1", [128, TILES])
    scale = sb("scale", [128, 1])
    own_batch = sb("own_batch", [128, FT])
    own_rows = sb("own_rows", [128, LR, E // LR])
    even1 = sb("even1", [96, LR, E])
    evens = sb("evens", [96, LR, E], F32R)
    cm = sb("cm", [96, FT])
    cs = sb("cs", [96, FT], F32R)
    even2 = sb("even2", [128, E])
    spread = sb("spread", [128, LR, E // LR])
    spread2 = [sb(f"spread2{i}", [128, LR, E // LR], F32R) for i in range(2)]
    tm = sb("tm", [128, FT])
    tmp = [sb(f"tmp{i}", [128, FT], F32R) for i in range(2)]
    h = sb("h", [128, TILES, FT])
    hT = [sb(f"hT{i}", [128, TILES, FT], F32R) for i in range(2)]
    r3 = sb("r3", [S, FB, E])
    x3 = sb("x3", [S, FB, E])
    st = sb("st_f", [S, FB, 6])
    mv = sb("mv_f", [S, FB, 2])
    lnv = sb("lnv_f", [S, FB])
    rstd = sb("rstd_f", [S, FB])
    names = ("here w1_here w2_here cleared zeroed w1h_done w2h_done w1_low w2_low even1_in even2_in xh_done x_low evens_high evens_done "
             "odd1_done odd2_done c_ps cm_done cs_high cs_done h_ps gelu_done hh_done h_low t_ps tm_done tmh_done tm_low "
             "spread_done spread_high spread_low y_ps r3_done st_done mv_done lnv_done rstd_done x3_done out_done").split()
    s = {n: sem(n) for n in names}
    h_bank = [m.bank[0], m.bank[1], m.bank[6], m.bank[7]]
    c_bank, t_bank, y_bank = m.bank[2], m.bank[3], m.bank[4:6]
    N = FGROUPS
    NW = 4 * 16

    def steps1(eng, step):
        for g in range(-1, 2):
            step(g)
        with eng.Fori(2, N - 1) as g:
            step(g)
        for g in range(N - 1, N + 1):
            step(g)

    with nc.Block() as block:
        @block.sync
        def _(sp):
            sp.dma_start(w_raw[:, :].rearrange("p (k n) -> p k n", k=KE), io["W1T"].rearrange("(k p) n -> p k n", p=128)).then_inc(s["w1_here"], 16)
            for dst, src in ((b1[:, :], io["b1"]), (scale[:, :], io["scale"]), (own_batch[:, :], io["c_own_batch"]),
                             (own_rows[:, :, :], io["c_own_rows"])):
                sp.dma_start(dst, src).then_inc(s["here"], 16)
            sp.wait_ge(s["zeroed"], 1)

            def step(g):
                if there(g + 1, N):
                    n = g + 1
                    after(sp, s["evens_done"], n)
                    for q in range(3):
                        for i in range(LR):
                            apart(sp, m)
                            sp.dma_start(even1[32 * q + i:32 * q + R:LR, i, :], m.lt[0, bass.ds(n * FB, FB), i, :]).then_inc(s["even1_in"], 16)
                    after(sp, s["spread_done"], n)
                    for r in range(LR):
                        apart(sp, m)
                        sp.dma_start(even2[32 * r:32 * r + R, :], m.lt[1, bass.ds(n * FB, FB), :, :].rearrange("b i e -> (b i) e")).then_inc(s["even2_in"], 16)
                if isinstance(g, int) and g == -1:
                    sp.wait_ge(s["w1_low"], 1)
                    sp.dma_start(w_raw[:, :].rearrange("p (k n) -> p k n", k=TILES), io["W2T"].rearrange("(k p) n -> p k n", p=128)).then_inc(s["w2_here"], 16)
                if there(g - 1, N):
                    sp.wait_ge(s["x3_done"], g)
                    apart(sp, m)
                    sp.dma_start(io["out"][bass.ds((g - 1) * FB, FB), :, :].rearrange("b s e -> s b e"), x3[:, :, :]).then_inc(s["out_done"], 16)
            steps1(sp, step)
            sp.wait_ge(s["out_done"], N * 16)

        @block.tensor
        def _(pe):

            def outputs(g, y):
                for b in range(2):
                    out = y_bank[y][0:S, b * E:(b + 1) * E]
                    tok = slice((y * 2 + b) * S, (y * 2 + b + 1) * S)
                    for t in range(TILES):
                        if y == 0 and b == 0:
                            pe.wait_ge(s["h_low"], g * TILES + t + 1)
                        product(pe, out, [a[:, t, tok] for a in hT], [a[:, t, :] for a in w2], t == 0, False)
                    if y == 0 and b == 0:
                        pe.wait_ge(s["tm_low"], g + 1)
                        pe.wait_ge(s["spread_low"], g + 1)
                    mm = product(pe, out, [a[:, tok] for a in tmp], [a[:, :, :].rearrange("p i n -> p (i n)") for a in spread2], False, True)
                mm.then_inc(s["y_ps"], 1)

            def step(g):
                if there(g, N):
                    if isinstance(g, int) and g == 0:
                        pe.wait_ge(s["w1_low"], 1)
                    for t in range(TILES):
                        after(pe, s["gelu_done"], g * TILES + t + 1 - len(h_bank))
                        out = h_bank[t % len(h_bank)][:, 0:FT]
                        for e in range(KE):
                            cols = slice(t * 128, (t + 1) * 128)
                            product(pe, out, [a[:, e, cols] for a in w1], [a[:, e, :] for a in x], e == 0, False)
                        if t == 0:
                            pe.wait_ge(s["cs_done"], g + 1)
                            pe.wait_ge(s["evens_done"], g + 1)
                        pe.matmul(out, evens[:, t // 2, (t % 2) * 128:(t % 2 + 1) * 128], cs[:, :], start=False, stop=True).then_inc(s["h_ps"], 1)
                    pe.wait_ge(s["odd2_done"], g + 1)
                    after(pe, s["tm_done"], g)
                    pe.wait_ge(s["gelu_done"], (g + 1) * TILES)
                    for e in range(KE):
                        for r in range(LR):
                            mm = pe.matmul(t_bank[32 * r:32 * r + R, 0:FT], odd2[:, e, :, :].rearrange("p b i -> p (b i)"), h[:, 2 * r + e, :],
                                           start=(e == 0), stop=(e == KE - 1), skip_group_check=True)
                    mm.then_inc(s["t_ps"], 1)
                    if isinstance(g, int) and g == 0:
                        pe.wait_ge(s["w2_low"], 1)
                    after(pe, s["r3_done"], 2 * g)
                    outputs(g, 0)
                if there(g + 1, N):
                    pe.wait_ge(s["odd1_done"], g + 2)
                    for e in range(KE):
                        mm = product(pe, c_bank[0:96, 0:FT], [a[:, e, :, :].rearrange("p q n -> p (q n)") for a in odd1], [a[:, e, :] for a in x], e == 0, e == KE - 1)
                    mm.then_inc(s["c_ps"], 1)
                if there(g, N):
                    outputs(g, 1)
            steps1(pe, step)

        @block.vector
        def _(dve):
            dve.memset(t_bank[:, :], 0.0)
            dve.wait_ge(s["cleared"], 1)
            for i in range(2):
                cp = dve.tensor_copy(odd1[i][:, :, :, :].rearrange("p e q n -> p (e q n)"), even2[:, 0:KE * 96])
            cp.then_inc(s["zeroed"], 1)

            def step(g):
                if there(g - 1, N):
                    after(dve, s["x3_done"], g - 1)
                    for y in range(2):
                        dve.wait_ge(s["y_ps"], (g - 1) * 2 + y + 1)
                        dve.tensor_tensor(r3[:, 2 * y:2 * y + 2, :], y_bank[y][0:S, :].rearrange("p (b e) -> p b e", b=2),
                                          m.xres[:, bass.ds((g - 1) * FB + 2 * y, 2), :], ALU.add).then_inc(s["r3_done"], 1)
                    for b in range(FB):
                        dve.wait_ge(s["r3_done"], (g - 1) * 2 + b // 2 + 1)
                        bn = dve.bn_stats(st[:, b, :], r3[:, b, :])
                    bn.then_inc(s["st_done"], 1)
                    dve.wait_ge(s["st_done"], g)
                    apart(dve, m)
                    for b in range(FB):
                        bn = dve.bn_aggr(mv[:, b, :], st[:, b, :])
                    bn.then_inc(s["mv_done"], 1)
                if there(g, N):
                    dve.wait_ge(s["even2_in"], (g + 1) * LR * 16)
                    for r in range(LR):
                        rows = slice(32 * r, 32 * r + 32)
                        a = even2[rows, r:E:LR]
                        src = bass.AP(tensor=a.tensor, offset=a.offset, ap=[list(a.ap[0]), [0, LR], list(a.ap[1])])
                        tt = dve.tensor_tensor(spread[rows, :, :], src, own_rows[rows, :, :], ALU.mult)
                    tt.then_inc(s["spread_done"], 1)
                    dve.wait_ge(s["spread_done"], g + 1)
                    high(dve, spread2[0][:, :, :], spread[:, :, :]).then_inc(s["spread_high"], 1)
                    dve.wait_ge(s["spread_high"], g + 1)
                    dve.tensor_tensor(spread2[1][:, :, :], spread[:, :, :], spread2[0][:, :, :], ALU.subtract).then_inc(s["spread_low"], 1)
                    if isinstance(g, int) and g == 0:
                        dve.wait_ge(s["w2_here"], 16)
                        high(dve, w2[0][:, :, :], w_raw[:, :].rearrange("p (k n) -> p k n", k=TILES)).then_inc(s["w2h_done"], 1)
                    for t in range(TILES):
                        dve.wait_ge(s["gelu_done"], g * TILES + t + 1)
                        high(dve, hT[0][:, t, :], h[:, t, :]).then_inc(s["hh_done"], 1)
                if there(g + 1, N):
                    after(dve, s["h_ps"], (g + 1) * TILES)
                    after(dve, s["odd2_done"], g + 1)
                    high(dve, x[0][:, :, :], m.x1T[:, :, bass.ds((g + 1) * FT, FT)]).then_inc(s["xh_done"], 1)
                if there(g, N):
                    dve.wait_ge(s["t_ps"], g + 1)
                    dve.scalar_tensor_tensor(tm[:, :], t_bank[:, 0:FT], scale[:, 0:1], own_batch[:, :], ALU.mult, ALU.mult).then_inc(s["tm_done"], 1)
                    dve.wait_ge(s["tm_done"], g + 1)
                    high(dve, tmp[0][:, :], tm[:, :]).then_inc(s["tmh_done"], 1)
                    dve.wait_ge(s["tmh_done"], g + 1)
                    dve.tensor_tensor(tmp[1][:, :], tm[:, :], tmp[0][:, :], ALU.subtract).then_inc(s["tm_low"], 1)
                if isinstance(g, int) and g == -1:
                    dve.wait_ge(s["w1_here"], 16)
                    raw = w_raw[:, :].rearrange("p (k n) -> p k n", k=KE)
                    high(dve, w1[0][:, :, :], raw).then_inc(s["w1h_done"], 1)
                    dve.wait_ge(s["w1h_done"], 1)
                    dve.tensor_tensor(w1[1][:, :, :], raw, w1[0][:, :, :], ALU.subtract).then_inc(s["w1_low"], 1)
                    dve.wait_ge(s["here"], NW)
                if there(g + 1, N):
                    dve.wait_ge(s["even1_in"], (g + 2) * LR * 3 * 16)
                    high(dve, evens[:, :, :], even1[:, :, :]).then_inc(s["evens_high"], 1)
                    dve.wait_ge(s["evens_high"], g + 2)
                    dve.tensor_tensor(evens[32:64, :, :], even1[32:64, :, :], evens[32:64, :, :], ALU.subtract).then_inc(s["evens_done"], 1)
                    dve.wait_ge(s["c_ps"], g + 2)
                    dve.scalar_tensor_tensor(cm[:, :], c_bank[0:96, 0:FT], scale[0:96, 0:1], own_batch[0:96, :], ALU.mult, ALU.mult).then_inc(s["cm_done"], 1)
                    dve.wait_ge(s["cm_done"], g + 2)
                    high(dve, cs[:, :], cm[:, :]).then_inc(s["cs_high"], 1)
                    dve.wait_ge(s["cs_high"], g + 2)
                    dve.tensor_tensor(cs[64:96, :], cm[64:96, :], cs[64:96, :], ALU.subtract).then_inc(s["cs_done"], 1)
                if there(g - 1, N):
                    dve.wait_ge(s["rstd_done"], g)
                    after(dve, s["out_done"], (g - 1) * 16)
                    for b in range(FB):
                        ts = dve.tensor_scalar(x3[:, b, :], r3[:, b, :], mv[:, b, 0:1], rstd[:, b:b + 1], ALU.subtract, ALU.mult)
                    ts.then_inc(s["x3_done"], 1)
            steps1(dve, step)

        @block.scalar
        def _(act):
            act.wait_ge(s["zeroed"], 1)

            def odd(part, e):
                return x[part][:, e, :].rearrange("p (b s) -> p b s", b=FB)[:, :, 2:2 + 2 * LR:2]

            def step(g):
                if there(g, N):
                    if isinstance(g, int) and g == 0:
                        act.wait_ge(s["here"], NW)
                    act.preload_act_table_set(GELU)
                    for t in range(TILES):
                        act.wait_ge(s["h_ps"], g * TILES + t + 1)
                        after(act, s["h_low"], (g - 1) * TILES + t + 1)
                        act.activation(h[:, t, :], h_bank[t % len(h_bank)][:, 0:FT], ACT.Gelu, bias=b1[:, t:t + 1]).then_inc(s["gelu_done"], 1)
                        if t == 0:
                            after(act, s["t_ps"], g)
                            for e in range(KE):
                                tok = m.x1T[:, e, bass.ds(g * FT, FT)].rearrange("p (b s) -> p b s", b=FB)
                                cp = act.activation(odd2[:, e], tok[:, :, 10:10 + 2 * LR:2], ACT.Copy)
                            cp.then_inc(s["odd2_done"], 1)
                if there(g + 1, N):
                    act.wait_ge(s["x_low"], g + 2)
                    after(act, s["c_ps"], g + 1)
                    for part in range(2):
                        for e in range(KE):
                            a = odd(part, e)
                            src = bass.AP(tensor=a.tensor, offset=a.offset, ap=[list(a.ap[0]), [0, 3], list(a.ap[1]), list(a.ap[2])])
                            cp = act.activation(odd1[part][:, e, :, 0:R].rearrange("p q (b i) -> p q b i", b=FB), src, ACT.Copy)
                    cp.then_inc(s["odd1_done"], 1)
                if there(g - 1, N):
                    act.preload_act_table_set(LOG_EXP)
                    act.wait_ge(s["mv_done"], g)
                    act.activation(lnv[:, :], mv[:, :, 1], ACT.Ln, bias=m.eps[0:S, :]).then_inc(s["lnv_done"], 1)
                    act.wait_ge(s["lnv_done"], g)
                    after(act, s["x3_done"], g - 1)
                    act.activation(rstd[:, :], lnv[:, :], ACT.Exp, scale=-0.5).then_inc(s["rstd_done"], 1)
            steps1(act, step)

        @block.gpsimd
        def _(pool):
            pool.memset(even1[:, :, :], 0.0)
            pool.memset(even2[:, :], 0.0).then_inc(s["cleared"], 1)

            def step(g):
                if there(g, N):
                    for t in range(TILES):
                        pool.wait_ge(s["hh_done"], g * TILES + t + 1)
                        pool.tensor_tensor(hT[1][:, t, :], h[:, t, :], hT[0][:, t, :], ALU.subtract).then_inc(s["h_low"], 1)
                if there(g + 1, N):
                    pool.wait_ge(s["xh_done"], g + 2)
                    pool.tensor_tensor(x[1][:, :, :], m.x1T[:, :, bass.ds((g + 1) * FT, FT)], x[0][:, :, :], ALU.subtract).then_inc(s["x_low"], 1)
                if isinstance(g, int) and g == -1:
                    pool.wait_ge(s["w2h_done"], 1)
                    pool.tensor_tensor(w2[1][:, :, :], w_raw[:, :].rearrange("p (k n) -> p k n", k=TILES), w2[0][:, :, :], ALU.subtract).then_inc(s["w2_low"], 1)
            steps1(pool, step)


def setup_phase(nc, m, ctx, io):
    def sb(name, shape, dt=F32):
        return ctx.enter_context(nc.sbuf_tensor(name, shape, dt))

    with ExitStack() as own:
        here = own.enter_context(nc.semaphore("s_here"))
        filled = own.enter_context(nc.semaphore("s_filled"))
        spread = own.enter_context(nc.semaphore("s_spread"))
        rows_ps = own.enter_context(nc.semaphore("s_rows_ps"))
        kept = own.enter_context(nc.semaphore("s_kept"))
        m.passed = ctx.enter_context(nc.semaphore("passed"))
        wo = own.enter_context(nc.sbuf_tensor("s_wo", [128, KE, E], F32))
        bv = own.enter_context(nc.sbuf_tensor("s_bv", [128, KE], F32))
        bvs = own.enter_context(nc.sbuf_tensor("s_bvs", [128, KE, S], F32))
        row = own.enter_context(nc.sbuf_tensor("s_row", [1, 2 * E], F32))
        ones = own.enter_context(nc.sbuf_tensor("s_ones", [128, S], F32))
        with nc.Block() as block:
            @block.sync
            def _(sp):
                sp.dma_start(m.w_in[:, :, :], io["W_inT"].rearrange("(k p) n -> p k n", p=128)).then_inc(m.w_in_here, 16)
                sp.dma_start(m.ident[:, :], io["c_ident"]).then_inc(here, 16)
                sp.dma_start(wo[:, :, :], io["Wo"].rearrange("(k p) n -> p k n", p=128)).then_inc(here, 16)
                sp.dma_start(bv[:, :], io["bv"]).then_inc(here, 16)
                sp.dma_start(row[0:1, 0:E], io["bo"].rearrange("(a n) -> a n", a=1)).then_inc(here, 16)
                sp.dma_start(row[0:1, E:2 * E], io["b2"].rearrange("(a n) -> a n", a=1)).then_inc(here, 16)

            @block.vector
            def _(dve):
                dve.memset(m.eps[:, :], EPS)
                dve.memset(m.one[:, :], 1.0)
                dve.memset(ones[:, :], 1.0).then_inc(filled, 1)
                dve.wait_ge(filled, 1)
                dve.wait_ge(here, 5 * 16)
                for e in range(KE):
                    ts = dve.tensor_scalar(bvs[:, e, :], ones[:, :], bv[:, e:e + 1], None, ALU.mult)
                ts.then_inc(spread, 1)
                dve.wait_ge(rows_ps, 1)
                for b in range(2):
                    cp = dve.tensor_copy(m.bo_rows[:, b, :], m.bank[0][0:S, 0:E])
                cp.then_inc(kept, 1)
                dve.tensor_copy(m.b2_rows[:, :], m.bank[1][0:S, 0:E]).then_inc(kept, 1)
                dve.wait_ge(kept, 2)

            @block.tensor
            def _(pe):
                pe.wait_ge(spread, 1)
                for e in range(KE):
                    pe.matmul(m.bank[0][0:S, 0:E], bvs[:, e, :], wo[:, e, :], start=(e == 0), stop=False)
                pe.matmul(m.bank[0][0:S, 0:E], ones[0:1, :], row[0:1, 0:E], start=False, stop=True)
                pe.matmul(m.bank[1][0:S, 0:E], ones[0:1, :], row[0:1, E:2 * E], start=True, stop=True).then_inc(rows_ps, 1)


def program(nc, io):
    with ExitStack() as ctx:
        m = Memory()
        m.bank = [ctx.enter_context(nc.psum_tensor(f"bank{i}", [128, 512], F32)) for i in range(8)]
        m.ident = ctx.enter_context(nc.sbuf_tensor("ident", [128, 128], F32))
        m.eps = ctx.enter_context(nc.sbuf_tensor("eps", [128, 1], F32))
        m.one = ctx.enter_context(nc.sbuf_tensor("one", [128, 1], F32))
        m.bo_rows = ctx.enter_context(nc.sbuf_tensor("bo_rows", [S, 2, E], F32))
        m.b2_rows = ctx.enter_context(nc.sbuf_tensor("b2_rows", [S, E], F32))
        m.xres = ctx.enter_context(nc.sbuf_tensor("xres", [S, B, E], F32))
        m.lt = nc.dram_tensor("lora_tokens", (2, B, LR, E), F32, kind="Internal").ap()
        m.x1T = ctx.enter_context(nc.sbuf_tensor("x1T", [128, KE, B * S], F32))
        with ExitStack() as own:
            m.kh1 = own.enter_context(nc.sbuf_tensor("kh1", [128, LEVELS * SEG * S], F32))
            m.w_in = m.kh1[:, 0:KE * 3 * E].rearrange("p (k n) -> p k n", k=KE)
            m.w_in_here = own.enter_context(nc.semaphore("w_in_here"))
            setup_phase(nc, m, ctx, io)
            gla_phase(nc, m, own, io)
        with ExitStack() as own:
            attention_phase(nc, m, own, io)
        with ExitStack() as own:
            ffn_phase(nc, m, own, io)


def laid_out(inputs):
    a = {k: np.asarray(v) for k, v in inputs.items()}
    out = {
        "x": a["x"],
        "xT": a["x"].reshape(B * S, KE, 128).transpose(1, 2, 0),
        "W_inT": a["L0_attn_W_in"].T, "W_outT": a["L0_attn_W_out"].T,
        "W_g1T": a["L0_attn_W_g1"].T, "W_g2T": a["L0_attn_W_g2"].T, "ln_w": a["L0_attn_ln_w"].reshape(KE, 128).T,
        "Wo": a["L0_xattn_Wo"], "bv": a["L0_xattn_bv"].reshape(KE, 128).T, "bo": a["L0_xattn_bo"], "b2": a["L0_ffn_b2"],
    }
    wo = np.zeros((4, 32, UNITS, E), np.float32)
    wo[:, 0:DK] = a["L0_xattn_Wo"].reshape(UNITS, 4, DK, E).transpose(1, 2, 0, 3)
    out.update({
        "W1T": a["L0_ffn_W1"].T, "W2T": a["L0_ffn_W2"].T, "b1": a["L0_ffn_b1"].reshape(TILES, 128).T,
        "scale": np.broadcast_to(a["L0_ffn_scale"], (128, 1)),
        "ctxT": a["ctx_512"].reshape(B * SC, C).T, "Wk": a["L0_xattn_Wk"], "Wv": a["L0_xattn_Wv"], "Wq": a["L0_xattn_Wq"],
        "Wo_units": wo.reshape(128, UNITS, E), "bk": a["L0_xattn_bk"].reshape(KE, 128).T, "bq": a["L0_xattn_bq"].reshape(KE, 128).T,
    })
    out.update(constants())
    return {k: np.ascontiguousarray(v) for k, v in out.items()}


def kernel(**inputs):
    import concourse.bacc as bacc
    from concourse.bass_utils import run_bass_kernel_spmd

    nc = bacc.Bacc("TRN2", target_bir_lowering=False, num_devices=1)
    arrays = laid_out(inputs)
    io = {k: nc.dram_tensor("in_" + k, v.shape, mybir.dt.from_np(v.dtype), kind="ExternalInput").ap() for k, v in arrays.items()}
    io["out"] = nc.dram_tensor("out", (B, S, E), F32, kind="ExternalOutput").ap()
    program(nc, io)
    r = run_bass_kernel_spmd(nc, [{"in_" + k: v for k, v in arrays.items()}], core_ids=[0])
    return r.results[0]["out"]
```
